# Optimizing a Trainium2 kernel written in Bass

```python
import numpy as np
import jax
import jax.numpy as jnp

def _softmax(x, axis=-1):
    return jax.nn.softmax(x, axis=axis)

def _gelu(x):
    return jax.nn.gelu(x, approximate=True)

def _silu(x):
    return jax.nn.silu(x)

def _sigmoid(x):
    return jax.nn.sigmoid(x)

def _layernorm(x, axis=-1, eps=1e-05):
    m = jnp.mean(x, axis=axis, keepdims=True)
    v = jnp.var(x, axis=axis, keepdims=True)
    return (x - m) / jnp.sqrt(v + eps)

def _scatter_add(tgt, idx, src, axis=0):
    return tgt.at[idx].add(src)

def _segment_sum(src, seg, n):
    return jax.ops.segment_sum(src, seg, n)
kernel_name = 'mk_macaron_d1_jaxref_r8_2d7dd0'

def setup_inputs(seed: int=0):
    np.random.seed(seed)
    _w = jnp.asarray

    def _L0_attn_setup():
        import jax, jax.numpy as jnp
        import numpy as np
        import math
        HIDDEN = 128
        HEADS = 16
        HEAD_DIM = HIDDEN // HEADS
        NUM_FEATURES = 64
        B, N = (4, 512)

        def _feature_map(x, rf):
            proj = jnp.einsum('bhnd,fd->bhnf', x, rf) / jnp.sqrt(jnp.float32(NUM_FEATURES))
            norm = jnp.linalg.norm(x, axis=-1, keepdims=True)
            return jnp.exp(proj - norm)
        key = jax.random.key(seed)
        ks = jax.random.split(key, 5)
        x = jax.random.normal(ks[0], (B, N, HIDDEN), dtype=jnp.float32)
        w_qkv = jax.random.normal(ks[1], (3 * HIDDEN, HIDDEN), dtype=jnp.float32) / math.sqrt(HIDDEN)
        w_out = jax.random.normal(ks[2], (HIDDEN, HIDDEN), dtype=jnp.float32) / math.sqrt(HIDDEN)
        b_out = jnp.zeros((HIDDEN,), dtype=jnp.float32)
        random_features = jax.random.normal(ks[3], (NUM_FEATURES, HEAD_DIM), dtype=jnp.float32)
        return {'x': x, 'w_qkv': w_qkv, 'w_out': w_out, 'b_out': b_out, 'random_features': random_features}
    _L0_attn_in = _L0_attn_setup()

    def _L0_ffn_setup():
        import jax, jax.numpy as jnp
        import numpy as np
        H = 128
        M = 64
        E = 16
        TOP_K = 4
        N_GROUP = 4
        TOPK_GROUP = 2
        SCALE = 2.5
        B, S = (2, 128)

        def _gate(x2d, gate_kernel, gate_bias):
            n = x2d.shape[0]
            logits = jnp.dot(x2d.astype(jnp.float32), gate_kernel.astype(jnp.float32))
            scores = jax.nn.sigmoid(logits)
            scores_for_choice = scores + gate_bias
            group_scores = scores_for_choice.reshape(n, N_GROUP, E // N_GROUP)
            top2 = jax.lax.top_k(group_scores, k=2)[0]
            group_sum = jnp.sum(top2, axis=-1)
            group_idx = jax.lax.top_k(group_sum, k=TOPK_GROUP)[1]
            group_mask = jnp.zeros_like(group_sum).at[jnp.arange(n)[:, None], group_idx].set(1.0)
            score_mask = jnp.repeat(group_mask[:, :, None], E // N_GROUP, axis=2).reshape(n, E)
            masked_scores = jnp.where(score_mask > 0, scores_for_choice, 0.0)
            topk_weight, topk_idx = jax.lax.top_k(masked_scores, k=TOP_K)
            topk_weight = topk_weight / (jnp.sum(topk_weight, axis=-1, keepdims=True) + 1e-20)
            topk_weight = topk_weight * SCALE
            return (topk_idx, topk_weight)
        key = jax.random.key(seed)
        ks = jax.random.split(key, 9)
        sc_h = 1.0 / np.sqrt(H)
        sc_m = 1.0 / np.sqrt(M)
        return {'hidden_states': jax.random.normal(ks[0], (B, S, H), jnp.float32), 'gate_kernel': jax.random.normal(ks[1], (H, E), jnp.float32) * sc_h, 'gate_bias': jax.random.normal(ks[2], (E,), jnp.float32) * 0.01, 'w_gate': jax.random.normal(ks[3], (E, H, M), jnp.float32) * sc_h, 'w_up': jax.random.normal(ks[4], (E, H, M), jnp.float32) * sc_h, 'w_down': jax.random.normal(ks[5], (E, M, H), jnp.float32) * sc_m, 'sw_gate': jax.random.normal(ks[6], (H, 2 * M), jnp.float32) * sc_h, 'sw_up': jax.random.normal(ks[7], (H, 2 * M), jnp.float32) * sc_h, 'sw_down': jax.random.normal(ks[8], (2 * M, H), jnp.float32) * (1.0 / np.sqrt(2 * M))}
    _L0_ffn_in = _L0_ffn_setup()
    _d = {'L0_attn_x': _L0_attn_in['x'], 'L0_attn_w_qkv': _L0_attn_in['w_qkv'], 'L0_attn_w_out': _L0_attn_in['w_out'], 'L0_attn_b_out': _L0_attn_in['b_out'], 'L0_attn_random_features': _L0_attn_in['random_features'], 'L0_ffn_gate_kernel': _L0_ffn_in['gate_kernel'], 'L0_ffn_gate_bias': _L0_ffn_in['gate_bias'], 'L0_ffn_w_gate': _L0_ffn_in['w_gate'], 'L0_ffn_w_up': _L0_ffn_in['w_up'], 'L0_ffn_w_down': _L0_ffn_in['w_down'], 'L0_ffn_sw_gate': _L0_ffn_in['sw_gate'], 'L0_ffn_sw_up': _L0_ffn_in['sw_up'], 'L0_ffn_sw_down': _L0_ffn_in['sw_down']}
    _x0 = _d['L0_attn_x']
    _d['L0_attn_x'] = jax.random.normal(jax.random.fold_in(jax.random.key(seed), 1), (16, 256, 128), dtype=_x0.dtype)
    del _x0
    return _d

def reference(L0_attn_x, L0_attn_w_qkv, L0_attn_w_out, L0_attn_b_out, L0_attn_random_features, L0_ffn_gate_kernel, L0_ffn_gate_bias, L0_ffn_w_gate, L0_ffn_w_up, L0_ffn_w_down, L0_ffn_sw_gate, L0_ffn_sw_up, L0_ffn_sw_down):

    def _L0_attn_ref(x, w_qkv, w_out, b_out, random_features):
        import jax, jax.numpy as jnp
        import numpy as np
        import math
        HIDDEN = 128
        HEADS = 16
        HEAD_DIM = HIDDEN // HEADS
        NUM_FEATURES = 64
        B, N = (4, 512)

        def _feature_map(x, rf):
            proj = jnp.einsum('bhnd,fd->bhnf', x, rf) / jnp.sqrt(jnp.float32(NUM_FEATURES))
            norm = jnp.linalg.norm(x, axis=-1, keepdims=True)
            return jnp.exp(proj - norm)
        b, n, _ = x.shape
        qkv = jnp.einsum('bnh,oh->bno', x, w_qkv)
        qkv = qkv.reshape(b, n, 3, HEADS, HEAD_DIM)
        qkv = jnp.transpose(qkv, (2, 0, 3, 1, 4))
        q, k, v = (qkv[0], qkv[1], qkv[2])
        q_prime = _feature_map(q, random_features)
        k_prime = _feature_map(k, random_features)
        kv = jnp.einsum('bhnf,bhnd->bhfd', k_prime, v)
        normalizer = jnp.einsum('bhnf,bhf->bhn', q_prime, k_prime.sum(axis=2))
        out = jnp.einsum('bhnf,bhfd->bhnd', q_prime, kv)
        out = out / (normalizer[..., None] + 1e-06)
        out = jnp.transpose(out, (0, 2, 1, 3)).reshape(b, n, HIDDEN)
        return jnp.einsum('bnh,oh->bno', out, w_out) + b_out

    def _L0_ffn_ref(hidden_states, gate_kernel, gate_bias, w_gate, w_up, w_down, sw_gate, sw_up, sw_down):
        import jax, jax.numpy as jnp
        import numpy as np
        H = 128
        M = 64
        E = 16
        TOP_K = 4
        N_GROUP = 4
        TOPK_GROUP = 2
        SCALE = 2.5
        B, S = (2, 128)

        def _gate(x2d, gate_kernel, gate_bias):
            n = x2d.shape[0]
            logits = jnp.dot(x2d.astype(jnp.float32), gate_kernel.astype(jnp.float32))
            scores = jax.nn.sigmoid(logits)
            scores_for_choice = scores + gate_bias
            group_scores = scores_for_choice.reshape(n, N_GROUP, E // N_GROUP)
            top2 = jax.lax.top_k(group_scores, k=2)[0]
            group_sum = jnp.sum(top2, axis=-1)
            group_idx = jax.lax.top_k(group_sum, k=TOPK_GROUP)[1]
            group_mask = jnp.zeros_like(group_sum).at[jnp.arange(n)[:, None], group_idx].set(1.0)
            score_mask = jnp.repeat(group_mask[:, :, None], E // N_GROUP, axis=2).reshape(n, E)
            masked_scores = jnp.where(score_mask > 0, scores_for_choice, 0.0)
            topk_weight, topk_idx = jax.lax.top_k(masked_scores, k=TOP_K)
            topk_weight = topk_weight / (jnp.sum(topk_weight, axis=-1, keepdims=True) + 1e-20)
            topk_weight = topk_weight * SCALE
            return (topk_idx, topk_weight)
        orig_shape = hidden_states.shape
        x = hidden_states.reshape(-1, orig_shape[-1])
        topk_idx, topk_weight = _gate(x, gate_kernel, gate_bias)
        onehot = (topk_idx[:, :, None] == jnp.arange(E)[None, None, :]).astype(topk_weight.dtype)
        combine = jnp.einsum('nke,nk->ne', onehot, topk_weight)
        g = jnp.einsum('nh,ehm->enm', x, w_gate)
        u = jnp.einsum('nh,ehm->enm', x, w_up)
        inter = jax.nn.silu(g) * u
        y_e = jnp.einsum('enm,emh->enh', inter, w_down)
        y = jnp.einsum('ne,enh->nh', combine, y_e)
        shared = jnp.dot(jax.nn.silu(jnp.dot(x, sw_gate)) * jnp.dot(x, sw_up), sw_down)
        return (y + shared).reshape(orig_shape)
    x = L0_attn_x
    x = x + 0.5 * _L0_ffn_ref(_layernorm(x, axis=-1), L0_ffn_gate_kernel, L0_ffn_gate_bias, L0_ffn_w_gate, L0_ffn_w_up, L0_ffn_w_down, L0_ffn_sw_gate, L0_ffn_sw_up, L0_ffn_sw_down)
    x = x + _L0_attn_ref(_layernorm(x, axis=-1), L0_attn_w_qkv, L0_attn_w_out, L0_attn_b_out, L0_attn_random_features)
    x = x + 0.5 * _L0_ffn_ref(_layernorm(x, axis=-1), L0_ffn_gate_kernel, L0_ffn_gate_bias, L0_ffn_w_gate, L0_ffn_w_up, L0_ffn_w_down, L0_ffn_sw_gate, L0_ffn_sw_up, L0_ffn_sw_down)
    return x

_drawn_inputs = setup_inputs


def setup_inputs(seed=0):
    import zlib

    import numpy as np

    out = dict(_drawn_inputs(seed))
    spreads = {'L0_attn_b_out': (0.0, 0.1)}
    factors = {'L0_attn_random_features': 4.016}
    for name, (base, spread) in spreads.items():
        noise = np.random.default_rng([zlib.crc32(name.encode()), seed]).standard_normal(out[name].shape)
        drawn = base * np.exp(spread * noise) if base else spread * noise
        out[name] = jnp.asarray(drawn.astype(out[name].dtype))
    for name, factor in factors.items():
        out[name] = (out[name] * factor).astype(out[name].dtype)
    return out
```

```python
from contextlib import ExitStack

import concourse.bass as bass
from concourse import mybir

F32 = mybir.dt.float32
F32R = mybir.dt.float32r
ALU = mybir.AluOpType
ACT = mybir.ActivationFunctionType
AX_X = mybir.AxisListType.X
ds = bass.ds

P = 128
H = 128
TOKENS = 4096
TILES = 4
CT = TILES * P
CHUNKS = TOKENS // CT
EXPERTS = 16
GROUPS = 4
EG = EXPERTS // GROUPS
M = 64
PAIRS = EXPERTS * M // P
BLOCKS = PAIRS + 1
SCALE = 2.5
LN_EPS = 1e-5
HEADS = 16
HD = H // HEADS
NF = 64
HG = 4
QG = HEADS // HG
STACK = 3 * HG * HD + 2 * HG
SLOT = 16
BT = 2 * P
ROWS = TOKENS // BT
DIAG = P + 2 * SLOT
LN_ATT = CHUNKS
LN_FFN2 = CHUNKS + ROWS

SILU_CREDIT = 2
S_CREDIT = 4
Q_CREDIT = 9
QL_CREDIT = 3
D_CREDIT = 3
Y_CREDIT = 1
YT_CREDIT = 1
XT_CREDIT = 1
EXP_CREDIT = 2
K_CREDIT = 4
QF_CREDIT = 4
KV_CREDIT = 1
KV_COPY_CREDIT = 1
KV_TR_CREDIT = 2
O_CREDIT = 1
O_COPY_CREDIT = 1
PROJ_CREDIT = 1
STACK_CREDIT = 4
N2_CREDIT = 1

ROUTE_STEPS = 28
DIVIDE_STEPS = 2
FRONT_STEPS = 3
KV_STEPS = 4
ROW_STEPS = DIVIDE_STEPS + FRONT_STEPS + KV_STEPS
GK_CONSTS = 5
ROUTE_CONSTS = GK_CONSTS + 1 + (GROUPS - 1) + 3
ALL_CONSTS = ROUTE_CONSTS + 7
NORM2_LEAST = 2.0 ** -60


def macaron_kernel(nc, x, wall, gate_k, gate_b, wqkv, wout, b_out, rft, pair_sel, norm_sel, out):
    x_v = x.rearrange("(c b p i) h -> c p b (i h)", c=CHUNKS, b=2, i=2)
    out_v = out.rearrange("(c b p i) h -> c p b (i h)", c=CHUNKS, b=2, i=2)

    with ExitStack() as ctx:
        def sb(name, shape, dt=F32):
            return ctx.enter_context(nc.sbuf_tensor(name, shape, dt))

        def psum(name, shape):
            return ctx.enter_context(nc.psum_tensor(name, shape, F32))

        def sem(name):
            return ctx.enter_context(nc.semaphore(name))

        X = sb("X", [P, CHUNKS * TILES * H])
        ident = sb("ident", [P, P])
        xn = sb("xn", [P, TILES * H])
        stats = sb("stats", [P, TILES, 6])
        meanvar = sb("meanvar", [P, TILES, 2])
        vareps = sb("vareps", [P, TILES])
        rstd = sb("rstd", [P, TILES])
        minus_half = sb("minus_half", [P, TILES])

        w_hi = sb("w_hi", [P, 3 * BLOCKS * P], F32R)
        w_lo = sb("w_lo", [P, 3 * BLOCKS * P], F32R)
        gk_hi = sb("gk_hi", [P, P], F32R)
        gk_lo = sb("gk_lo", [P, P], F32R)
        gk_raw = sb("gk_raw", [P, EXPERTS])
        gb_rows = sb("gb_rows", [P, EXPERTS])
        sel_r = sb("sel_r", [P, PAIRS * P], F32R)
        x_hi = sb("x_hi", [P, CHUNKS * CT], F32R)
        x_lo = sb("x_lo", [P, CHUNKS * CT], F32R)
        combine_t = sb("combine_t", [P, CHUNKS * CT], F32R)
        y_sb = sb("y_sb", [P, CT])
        scores_t = sb("scores_t", [P, CT])
        silu_g = sb("silu_g", [P, 4, CT])
        silu_s = sb("silu_s", [P, CT])
        weighted = sb("weighted", [P, 2, CT])
        gated = sb("gated", [P, 3, CT])
        gated_hi = sb("gated_hi", [P, 3, CT], F32R)
        gated_lo = sb("gated_lo", [P, 3, CT], F32R)

        sfc = sb("sfc", [P, TILES * EXPERTS])
        pair_hi = sb("pair_hi", [P, 16, 2])
        pair_lo = sb("pair_lo", [P, 16, 2])
        g_top = sb("g_top", [P, 16])
        g_mid = sb("g_mid", [P, 16])
        g_low = sb("g_low", [P, 16])
        g_sum = sb("g_sum", [P, TILES, GROUPS])
        g_gt = sb("g_gt", [P, TILES, GROUPS, GROUPS])
        g_eq = sb("g_eq", [P, TILES, GROUPS, GROUPS])
        g_before = sb("g_before", [P, GROUPS, GROUPS])
        g_rank = sb("g_rank", [P, 16])
        masked = sb("masked", [P, TILES, EXPERTS])
        top8 = sb("top8", [P, TILES, 8])
        above = sb("above", [P, TILES, EXPERTS])
        tied = sb("tied", [P, TILES * EXPERTS])
        n_above = sb("n_above", [P, TILES])
        restart = sb("restart", [P, TILES * EXPERTS])
        order = sb("order", [P, TILES * EXPERTS])
        chosen = sb("chosen", [P, TILES, EXPERTS])
        w_sum = sb("w_sum", [P, TILES])
        combine = sb("combine", [P, TILES, EXPERTS])
        combine_s = sb("combine_s", [P, TILES, P], F32R)

        wqkv_sb = sb("wqkv_sb", [P, 3 * H])
        wout_sb = sb("wout_sb", [P, H])
        bout_rows = sb("bout_rows", [P, H])
        rf_raw = sb("rf_raw", [STACK, HG * NF])
        rf_r = sb("rf_r", [STACK, HG * NF], F32R)
        x_t = sb("x_t", [P, BT])
        qkv = sb("qkv", [P, 2, 3 * H])
        squares = sb("squares", [P, 2, 2 * H])
        n2 = sb("n2", [P, 2 * 2 * HEADS])
        ln_n2 = sb("ln_n2", [P, 2 * 2 * HEADS])
        norm = sb("norm", [P, 2 * 2 * HEADS])
        stack = sb("stack", [P, 2 * 2 * QG, STACK], F32R)
        qk_r = sb("qk_r", [STACK, 2 * QG, BT], F32R)
        v_r = sb("v_r", [P, 2, QG, P], F32R)
        exp_k = sb("exp_k", [P, 2 * 1024])
        exp_q = silu_g[:].rearrange("p b n -> p (b n)")
        k_lo = x_hi[:, 0:2048]
        q_lo = x_hi[:, 2048:4096]
        k_hi = x_lo[:, 0:2048]
        q_hi = x_lo[:, 2048:4096]
        kv_t = sb("kv_t", [P, 4 * BT])
        kv_tmp = sb("kv_tmp", [P, 2, 4, 2 * SLOT])
        kv_sum = sb("kv_sum", [P, 2, 4, 2 * SLOT])
        kv_own = sb("kv_own", [P, 2, 4, 2 * SLOT])
        head_mask = sb("head_mask", [P, 2 * SLOT])
        kv_hi = sb("kv_hi", [P, 2, 4 * DIAG], F32R)
        kv_lo = sb("kv_lo", [P, 2, 4 * DIAG], F32R)
        o_sb = sb("o_sb", [P, CT])
        den = sb("den", [P, 2 * HEADS])
        rden = sb("rden", [P, 2 * HEADS])
        on = sb("on", [P, BT])
        on_t = sb("on_t", [P, BT])

        pG = psum("pG", [P, 2, 512])
        pU = psum("pU", [P, 2, 512])
        pC = psum("pC", [P, 512])
        pY = psum("pY", [P, 512])
        T0 = psum("T0", [P, 512])
        T1 = psum("T1", [P, 512])

        x_loaded = sem("x_loaded")
        w_loaded = [sem(f"w_loaded_{kind}") for kind in ("gate", "up", "down")]
        small_loaded = sem("small_loaded")
        rf_zeroed = sem("rf_zeroed")
        rf_loaded = sem("rf_loaded")
        rf_ready = sem("rf_ready")
        out_stored = sem("out_stored")
        const_step = sem("const_step")
        w_hi_ready = sem("w_hi_ready")
        w_lo_ready = sem("w_lo_ready")
        small_hi_ready = sem("small_hi_ready")
        small_lo_ready = sem("small_lo_ready")
        route_step = sem("route_step")
        att_step = sem("att_step")
        bn_step = sem("bn_step")
        var_ready = sem("var_ready")
        bn_aggr_go = sem("bn_aggr_go")
        max_go = sem("max_go")
        pool_go = sem("pool_go")
        mv_ready = sem("mv_ready")
        rstd_ready = sem("rstd_ready")
        xn_ready = sem("xn_ready")
        xt_ready = sem("xt_ready")
        xhi_ready = sem("xhi_ready")
        xlo_ready = sem("xlo_ready")
        logits_ready = sem("logits_ready")
        scores_ready = sem("scores_ready")
        scores_tok_ready = sem("scores_tok_ready")
        sfc_ready = sem("sfc_ready")
        combine_ready = sem("combine_ready")
        combine_tok_t = sem("combine_tok_t")
        combine_t_ready = sem("combine_t_ready")
        g_ready = sem("g_ready")
        u_ready = sem("u_ready")
        c_ready = sem("c_ready")
        silu_done = sem("silu_done")
        s_used = sem("s_used")
        gated_done = sem("gated_done")
        gated_hi_done = sem("gated_hi_done")
        gated_lo_done = sem("gated_lo_done")
        down_done = sem("down_done")
        y_done = sem("y_done")
        yt_ready = sem("yt_ready")
        ffn_x_done = sem("ffn_x_done")

        xta_ready = sem("xta_ready")
        qkv_ready = sem("qkv_ready")
        qkv_copied = sem("qkv_copied")
        squares_ready = sem("squares_ready")
        n2_ready = sem("n2_ready")
        ln_ready = sem("ln_ready")
        norm_split = sem("norm_split")
        norm_ready = sem("norm_ready")
        stack_ready = sem("stack_ready")
        stack_dup_ready = sem("stack_dup_ready")
        v_ready = sem("v_ready")
        stack_t_ready = sem("stack_t_ready")
        qk_even_ready = sem("qk_even_ready")
        qk_odd_ready = sem("qk_odd_ready")
        feat_ready = sem("feat_ready")
        exp_done = sem("exp_done")
        k_hi_done = sem("k_hi_done")
        k_lo_done = sem("k_lo_done")
        q_hi_done = sem("q_hi_done")
        q_lo_done = sem("q_lo_done")
        kv_ready = sem("kv_ready")
        kv_copied = sem("kv_copied")
        kv_tr_ready = sem("kv_tr_ready")
        kv_tr_read = sem("kv_tr_read")
        kv_split = sem("kv_split")
        o_ready = sem("o_ready")
        o_copied = sem("o_copied")
        o_tr_ready = sem("o_tr_ready")
        on_ready = sem("on_ready")
        on_tr_ready = sem("on_tr_ready")
        on_copied = sem("on_copied")
        proj_ready = sem("proj_ready")
        att_x_added = sem("att_x_added")
        att_x_done = sem("att_x_done")

        def tiles_of(ap, n=TILES):
            return ap.rearrange("p (t h) -> p t h", t=n)

        def w_block(w, kind, j):
            k = (kind * BLOCKS + j) * P
            return w[:, k:k + P]

        wn = BLOCKS * P
        sel_raw = kv_t
        w_stage = [exp_k[:, 0:wn], exp_q[:, 0:wn], gated[:].rearrange("p b n -> p (b n)")[:, 0:wn]]

        class Steps:
            def __init__(self, eng, s, base=0):
                self.eng, self.s, self.base, self.n = eng, s, base, 0

            def link(self, ins):
                self.n += 1
                ins.then_inc(self.s, 1)
                self.eng.wait_ge(self.s, self.base + self.n)

        block = ctx.enter_context(nc.Block())

        @block.sync
        def _(sp):
            def x_chunk(c):
                return X[:, c * CT:(c + 1) * CT].rearrange("p (b w) -> p b w", b=2)

            sp.dma_start(x_chunk(0), x_v[0]).then_inc(x_loaded, 16)
            sp.dma_start(gk_raw[:], gate_k).then_inc(small_loaded, 16)
            sp.dma_start(gb_rows[:], gate_b.partition_broadcast(P)).then_inc(small_loaded, 16)
            sp.dma_start(sel_raw[:], pair_sel).then_inc(small_loaded, 16)
            for c in range(1, CHUNKS):
                sp.wait_ge(x_loaded, 16 * c)
                sp.dma_start(x_chunk(c), x_v[c]).then_inc(x_loaded, 16)
            sp.dma_start(wqkv_sb[:], wqkv).then_inc(small_loaded, 16)
            sp.dma_start(wout_sb[:], wout).then_inc(small_loaded, 16)
            sp.dma_start(bout_rows[:], b_out.partition_broadcast(P)).then_inc(small_loaded, 16)
            sp.wait_ge(rf_zeroed, 1)
            for part in range(3):
                for hh in range(HG):
                    r = (part * HG + hh) * HD
                    sp.dma_start(rf_raw[r:r + HD, hh * NF:(hh + 1) * NF], rft).then_inc(rf_loaded, 16)
            sp.dma_start(rf_raw[3 * HG * HD:STACK, :], norm_sel).then_inc(rf_loaded, 16)
            for c in range(CHUNKS):
                sp.wait_ge(ffn_x_done, CHUNKS + c + 1)
                sp.dma_start(out_v[c], x_chunk(c)).then_inc(out_stored, 16)
            sp.wait_ge(out_stored, 16 * CHUNKS)

        @block.gpsimd
        def _(pool):
            pool.sem_inc(gated_lo_done, QL_CREDIT)
            pool.sem_inc(q_lo_done, QF_CREDIT)

            def rstd_of(p, n):
                pool.wait_ge(mv_ready, p + 1)
                pool.sem_inc(pool_go, 1)
                nc.gpsimd.tensor_scalar(vareps[:, 0:n], meanvar[:, 0:n, 1], LN_EPS, 0.0, ALU.add,
                                        ALU.add).then_inc(var_ready, 1)
                pool.wait_ge(var_ready, p + 1)
                nc.gpsimd.tensor_tensor(rstd[:, 0:n], vareps[:, 0:n], minus_half[:, 0:n],
                                        ALU.pow).then_inc(rstd_ready, 1)

            def constants():
                steps = Steps(pool, const_step)
                steps.link(nc.gpsimd.memset(minus_half[:], -0.5))
                steps.link(nc.gpsimd.memset(ident[:], 0.0))
                steps.link(nc.gpsimd.affine_select(out=ident[:], in_=ident[:], compare_op=ALU.not_equal,
                                                   fill=1.0, base=0, pattern=[[-1, P]], channel_multiplier=1))
                steps.link(nc.gpsimd.memset(gk_hi[:].bitcast(F32), 0.0))
                steps.link(nc.gpsimd.memset(gk_lo[:].bitcast(F32), 0.0))
                assert steps.n == GK_CONSTS
                rstd_of(0, TILES)
                steps.link(nc.gpsimd.memset(g_before[:], 0.0))
                for g in range(1, GROUPS):
                    steps.link(nc.gpsimd.memset(g_before[:, g, 0:g], 1.0))
                steps.link(nc.gpsimd.memset(restart[:], 1.0))
                steps.link(nc.gpsimd.memset(restart[:, 0::EXPERTS], 0.0))
                steps.link(nc.gpsimd.memset(combine_s[:].bitcast(F32), 0.0))
                assert steps.n == ROUTE_CONSTS
                rstd_of(1, TILES)
                nc.gpsimd.memset(rf_raw[:], 0.0).then_inc(rf_zeroed, 1)
                steps.link(nc.gpsimd.memset(head_mask[:], 0.0))
                steps.link(nc.gpsimd.memset(head_mask[0:M, 0:SLOT], 1.0))
                steps.link(nc.gpsimd.memset(head_mask[M:P, SLOT:2 * SLOT], 1.0))
                steps.link(nc.gpsimd.memset(v_r[:].bitcast(F32), 0.0))
                ones_cols = v_r[:, :, :, 0:HG * SLOT].rearrange("p t g (k s) -> p (t g) k s", s=SLOT)[:, :, :, HD]
                steps.link(nc.gpsimd.memset(ones_cols.bitcast(F32), 1.0))
                steps.link(nc.gpsimd.memset(kv_hi[:].bitcast(F32), 0.0))
                steps.link(nc.gpsimd.memset(kv_lo[:].bitcast(F32), 0.0))
                assert steps.n == ALL_CONSTS

            def ffn(f0, ln0):
                def lo_part(n, j):
                    pool.wait_ge(gated_hi_done, n + 1)
                    nc.gpsimd.tensor_tensor(gated_lo[:, j % 3], gated[:, j % 3], gated_hi[:, j % 3].bitcast(F32),
                                            ALU.subtract).then_inc(gated_lo_done, 1)

                def chunk(c, prev, ln):
                    n0 = (c + f0) * BLOCKS
                    for j in range(BLOCKS):
                        if j >= 1:
                            lo_part(n0 + (j - 1), j - 1)
                        elif prev:
                            lo_part(n0 - 1, BLOCKS - 1)
                        if j == 8 and ln:
                            rstd_of(c + (2 + ln0), TILES)

                chunk(0, False, True)
                with pool.Fori(1, CHUNKS - 2) as c:
                    chunk(c, True, True)
                chunk(CHUNKS - 2, True, False)
                chunk(CHUNKS - 1, True, False)
                lo_part((f0 + CHUNKS) * BLOCKS - 1, BLOCKS - 1)

            def squares_and_dup(a):
                pool.wait_ge(qkv_copied, 2 * a + 2)
                pool.wait_ge(n2_ready, a + N2_CREDIT)
                nc.gpsimd.tensor_tensor(squares[:], qkv[:, :, 0:2 * H], qkv[:, :, 0:2 * H],
                                        ALU.mult).then_inc(squares_ready, 1)
                pool.wait_ge(stack_t_ready, 4 * a + STACK_CREDIT)
                pool.sem_inc(pool_go, 1)
                for t in range(2):
                    last = nc.gpsimd.tensor_scalar(
                        stack[:, 8 * t:8 * t + 8, 64:96],
                        qkv[:, t, 0:2 * H].rearrange("p (g d) -> p g d", g=2 * QG),
                        1.0, 0.0, ALU.mult, ALU.add)
                last.then_inc(stack_dup_ready, 1)

            def q_split(a, u):
                cols = slice(u * CT, (u + 1) * CT)
                pool.wait_ge(exp_done, 8 * a + (4 + u + 1 + EXP_CREDIT))
                pool.wait_ge(o_ready, a + O_CREDIT)
                pool.sem_inc(pool_go, 1)
                nc.gpsimd.tensor_scalar(q_hi[:, cols], exp_q[:, cols], 1.0, 0.0, ALU.mult,
                                        ALU.add).then_inc(q_hi_done, 1)
                pool.wait_ge(q_hi_done, 4 * a + (u + 1))
                nc.gpsimd.tensor_tensor(q_lo[:, cols], exp_q[:, cols], q_hi[:, cols].bitcast(F32),
                                        ALU.subtract).then_inc(q_lo_done, 1)

            def bias(a):
                pool.wait_ge(att_x_added, a + 1)
                xs = tiles_of(X[:, ds(a * BT, BT)], 2)
                nc.gpsimd.tensor_tensor(xs, xs, bout_rows[:].unsqueeze(1).broadcast_to((P, 2, H)),
                                        ALU.add).then_inc(att_x_done, 1)

            def row(a, late, front, ln):
                if ln:
                    rstd_of(a + (2 + LN_ATT), 2)
                if front:
                    squares_and_dup(a + 1)
                q_split(a, 0)
                q_split(a, 1)
                if late:
                    bias(a - 1)
                q_split(a, 2)
                q_split(a, 3)

            constants()
            ffn(0, 0)
            pool.wait_ge(small_loaded, 16 * 6)
            rstd_of(LN_ATT, 2)
            squares_and_dup(0)
            rstd_of(LN_ATT + 1, 2)
            row(0, False, True, True)
            with pool.Fori(1, ROWS - 2) as a:
                row(a, True, True, True)
            row(ROWS - 2, True, True, False)
            row(ROWS - 1, True, False, False)
            bias(ROWS - 1)
            rstd_of(LN_FFN2, TILES)
            rstd_of(LN_FFN2 + 1, TILES)
            ffn(CHUNKS, LN_FFN2)

        @block.scalar
        def _(act):
            for k, stage in enumerate(w_stage):
                act.dma_start(stage, wall[:, k * BLOCKS * P:(k + 1) * BLOCKS * P]).then_inc(w_loaded[k], 16)
            act.sem_inc(silu_done, SILU_CREDIT)
            act.sem_inc(y_done, Y_CREDIT)
            act.sem_inc(exp_done, EXP_CREDIT)
            act.sem_inc(kv_copied, KV_COPY_CREDIT)
            act.sem_inc(o_copied, O_COPY_CREDIT)

            def copy(o, i):
                return nc.scalar.activation(o, i, ACT.Copy)

            def x_hi_part(f, c, p):
                act.wait_ge(xt_ready, p + (1 + XT_CREDIT))
                copy(x_hi[:, ds(c * CT, CT)], T0[:]).then_inc(xhi_ready, 1)

            def scores(f):
                act.wait_ge(logits_ready, f + 1)
                nc.scalar.activation(scores_t[:], T1[:], ACT.Sigmoid).then_inc(scores_ready, 1)

            def combine_copy(f, c):
                act.wait_ge(combine_tok_t, f + 1)
                copy(combine_t[:, ds(c * CT, CT)], T0[:]).then_inc(combine_t_ready, 1)

            def weight_hi(k):
                act.wait_ge(w_loaded[k], 16)
                copy(w_hi[:, k * BLOCKS * P:(k + 1) * BLOCKS * P], w_stage[k]).then_inc(w_hi_ready, 1)

            def ffn(f0, ln0):
                def hi_part(n, j):
                    act.wait_ge(gated_done, n + (1 + Q_CREDIT))
                    act.wait_ge(down_done, n + (1 - 3 + D_CREDIT))
                    copy(gated_hi[:, j % 3], gated[:, j % 3]).then_inc(gated_hi_done, 1)

                def y_copy(f):
                    act.wait_ge(down_done, f * BLOCKS + (BLOCKS + D_CREDIT))
                    act.wait_ge(yt_ready, f + YT_CREDIT)
                    copy(y_sb[:], pY[:]).then_inc(y_done, 1)

                def chunk(c, prev, nxt):
                    f = c + f0
                    n0, m0 = f * BLOCKS, f * PAIRS
                    for j in range(BLOCKS):
                        if j == 1 and nxt:
                            x_hi_part(f + 1, c + 1, c + (ln0 + 1))
                        if j == 3 and prev:
                            y_copy(f - 1)
                        if j == 3 and nxt:
                            scores(f + 1)
                        act.wait_ge(g_ready, n0 + (j + 1))
                        if j < PAIRS:
                            act.wait_ge(s_used, m0 + (j + 1 - 4 + S_CREDIT))
                            nc.scalar.activation(silu_g[:, j % 4], pG[:, j % 2], ACT.Silu).then_inc(silu_done, 1)
                        else:
                            act.wait_ge(gated_done, n0 + (j + 1 - BLOCKS + Q_CREDIT))
                            nc.scalar.activation(silu_s[:], pG[:, j % 2], ACT.Silu).then_inc(silu_done, 1)
                        if j >= 1:
                            hi_part(n0 + (j - 1), j - 1)
                        elif prev:
                            hi_part(n0 - 1, BLOCKS - 1)
                        if j == 8 and nxt:
                            combine_copy(f + 1, c + 1)

                chunk(0, False, True)
                with act.Fori(1, CHUNKS - 1) as c:
                    chunk(c, True, True)
                chunk(CHUNKS - 1, True, False)
                hi_part((f0 + CHUNKS) * BLOCKS - 1, BLOCKS - 1)
                y_copy(f0 + CHUNKS - 1)

            def x_t_copy(a):
                act.wait_ge(xt_ready, a + (LN_ATT + 1 + XT_CREDIT))
                if not isinstance(a, int) or a > 0:
                    act.wait_ge(qkv_ready, 2 * a)
                copy(x_t[:], T1[:, 0:BT]).then_inc(xta_ready, 1)

            def qkv_copy(a):
                if not isinstance(a, int) or a > 0:
                    act.wait_ge(v_ready, a)
                    act.wait_ge(stack_dup_ready, a)
                for t, bank in enumerate((T0, T1)):
                    act.wait_ge(qkv_ready, 2 * a + (t + 1))
                    copy(qkv[:, t], bank[:, 0:3 * H]).then_inc(qkv_copied, 1)

            def norms(a):
                act.wait_ge(n2_ready, a + (1 + N2_CREDIT))
                nc.scalar.activation(ln_n2[:], n2[:], ACT.Ln).then_inc(ln_ready, 1)
                act.wait_ge(ln_ready, a + 1)
                nc.scalar.activation(norm[:], ln_n2[:], ACT.Exp, scale=0.5).then_inc(norm_ready, 1)

            def stack_copies(a):
                for s in (0, 2):
                    act.wait_ge(stack_t_ready, 4 * a + (s + 1 + STACK_CREDIT))
                    copy(qk_r[:, 2 * s:2 * s + 2].rearrange("p g n -> p (g n)"),
                         T0[0:STACK, :]).then_inc(qk_even_ready, 1)

            def k_features(a, u):
                cols = slice(u * CT, (u + 1) * CT)
                act.wait_ge(feat_ready, 8 * a + (u + 1))
                act.wait_ge(k_lo_done, 4 * a + (u + 1 - 4 + K_CREDIT))
                nc.scalar.activation(exp_k[:, cols], pG[:, u % 2], ACT.Exp, scale=NF ** -0.5).then_inc(exp_done, 1)
                act.wait_ge(exp_done, 8 * a + (u + 1 + EXP_CREDIT))
                act.wait_ge(kv_ready, a + KV_CREDIT)
                copy(k_hi[:, cols], exp_k[:, cols]).then_inc(k_hi_done, 1)

            def q_features(a, u):
                act.wait_ge(feat_ready, 8 * a + (4 + u + 1))
                act.wait_ge(q_lo_done, 4 * a + (u + 1 - 4 + QF_CREDIT))
                nc.scalar.activation(exp_q[:, u * CT:(u + 1) * CT], pG[:, u % 2], ACT.Exp,
                                     scale=NF ** -0.5).then_inc(exp_done, 1)

            def o_copy(a):
                act.wait_ge(o_ready, a + (1 + O_CREDIT))
                if not isinstance(a, int) or a > 0:
                    act.wait_ge(o_tr_ready, a)
                copy(o_sb[:], pC[:]).then_inc(o_copied, 1)

            def on_copy(a):
                act.wait_ge(on_tr_ready, a + 1)
                act.wait_ge(proj_ready, a + PROJ_CREDIT)
                copy(on_t[:], T1[:, 0:BT]).then_inc(on_copied, 1)

            def kv_copy(a):
                act.wait_ge(kv_ready, a + (1 + KV_CREDIT))
                act.wait_ge(kv_tr_ready, 2 * a + KV_TR_CREDIT)
                copy(kv_t[:], pU[:].rearrange("p b n -> p (b n)")).then_inc(kv_copied, 1)

            def row(a, late, front, xt):
                for u in range(4):
                    k_features(a, u)
                if late:
                    o_copy(a - 1)
                if front:
                    qkv_copy(a + 1)
                for u in range(4):
                    q_features(a, u)
                kv_copy(a)
                if late:
                    on_copy(a - 1)
                if front:
                    norms(a + 1)
                if xt:
                    x_t_copy(a + 2)
                if front:
                    stack_copies(a + 1)

            act.wait_ge(small_loaded, 16 * 3)
            act.wait_ge(const_step, GK_CONSTS)
            copy(gk_hi[:, 0:EXPERTS], gk_raw[:]).then_inc(small_hi_ready, 1)
            copy(sel_r[:], sel_raw[:]).then_inc(small_hi_ready, 1)
            x_hi_part(0, 0, 0)
            weight_hi(0)
            weight_hi(1)
            scores(0)
            weight_hi(2)
            combine_copy(0, 0)
            ffn(0, 0)

            act.wait_ge(rf_loaded, 16 * 13)
            copy(rf_r[:], rf_raw[:]).then_inc(rf_ready, 1)
            x_t_copy(0)
            qkv_copy(0)
            norms(0)
            x_t_copy(1)
            stack_copies(0)
            row(0, False, True, True)
            with act.Fori(1, ROWS - 2) as a:
                row(a, True, True, True)
            row(ROWS - 2, True, True, False)
            row(ROWS - 1, True, False, False)
            o_copy(ROWS - 1)
            on_copy(ROWS - 1)

            x_hi_part(CHUNKS, 0, LN_FFN2)
            scores(CHUNKS)
            combine_copy(CHUNKS, 0)
            ffn(CHUNKS, LN_FFN2)

        @block.vector
        def _(dve):
            dve.sem_inc(s_used, S_CREDIT)
            dve.sem_inc(gated_done, Q_CREDIT)
            dve.sem_inc(k_lo_done, K_CREDIT)
            dve.sem_inc(n2_ready, N2_CREDIT)
            tt = nc.vector.tensor_tensor

            def ln_stats(p, x0, n):
                if not isinstance(p, int) or p > 0:
                    dve.wait_ge(xn_ready, p)
                for t in range(n):
                    last = nc.vector.bn_stats(stats[:, t, :], X[:, ds(x0 + t * H, H)])
                last.then_inc(bn_step, 1)
                dve.wait_ge(bn_step, p + 1)
                dve.sem_inc(bn_aggr_go, 1)
                for t in range(n):
                    last = nc.vector.bn_aggr(meanvar[:, t, :], stats[:, t, :])
                last.then_inc(mv_ready, 1)

            def ln_apply(p, x0, n):
                dve.wait_ge(rstd_ready, p + 1)
                dve.wait_ge(xt_ready, p + XT_CREDIT)
                for t in range(n):
                    last = nc.vector.tensor_scalar(xn[:, t * H:(t + 1) * H], X[:, ds(x0 + t * H, H)],
                                                   meanvar[:, t, 0:1], rstd[:, t:t + 1], ALU.subtract, ALU.mult)
                last.then_inc(xn_ready, 1)

            def x_lo_part(f, c):
                dve.wait_ge(xhi_ready, f + 1)
                cols = ds(c * CT, CT)
                tt(x_lo[:, cols], T0[:], x_hi[:, cols].bitcast(F32), ALU.subtract).then_inc(xlo_ready, 1)

            def weight_lo(k):
                dve.wait_ge(w_hi_ready, k + 1)
                cols = slice(k * BLOCKS * P, (k + 1) * BLOCKS * P)
                tt(w_lo[:, cols], w_stage[k], w_hi[:, cols].bitcast(F32), ALU.subtract).then_inc(w_lo_ready, 1)

            def per_tile(ap):
                return ap.unsqueeze(2).broadcast_to((P, TILES, EXPERTS))

            def route_groups(f, steps):
                dve.wait_ge(scores_tok_ready, f + 1)
                if not isinstance(f, int) or f > 0:
                    dve.wait_ge(combine_ready, f)
                tt(sfc[:].rearrange("p (t e) -> p t e", t=TILES),
                   T1[:].rearrange("p (t e) -> p t e", t=TILES)[:, :, 0:EXPERTS],
                   gb_rows[:].unsqueeze(1).broadcast_to((P, TILES, EXPERTS)), ALU.add).then_inc(sfc_ready, 1)
                dve.wait_ge(sfc_ready, f + 1)
                s4 = sfc[:].rearrange("p (g e) -> p g e", e=EG)
                steps.link(tt(pair_hi[:], s4[:, :, 0:2], s4[:, :, 2:4], ALU.max))
                steps.link(tt(pair_lo[:], s4[:, :, 0:2], s4[:, :, 2:4], ALU.min))
                steps.link(tt(g_top[:], pair_hi[:, :, 0], pair_hi[:, :, 1], ALU.max))
                steps.link(tt(g_mid[:], pair_hi[:, :, 0], pair_hi[:, :, 1], ALU.min))
                steps.link(tt(g_low[:], pair_lo[:, :, 0], pair_lo[:, :, 1], ALU.max))
                steps.link(tt(g_mid[:], g_mid[:], g_low[:], ALU.max))
                steps.link(tt(g_sum[:].rearrange("p t g -> p (t g)"), g_top[:], g_mid[:], ALU.add))
                other = g_sum[:].unsqueeze(2).broadcast_to((P, TILES, GROUPS, GROUPS))
                own = g_sum[:].unsqueeze(3).broadcast_to((P, TILES, GROUPS, GROUPS))
                steps.link(tt(g_gt[:], other, own, ALU.is_gt))
                steps.link(tt(g_eq[:], other, own, ALU.is_equal))
                steps.link(tt(g_eq[:], g_eq[:], g_before[:].unsqueeze(1).broadcast_to((P, TILES, GROUPS, GROUPS)),
                              ALU.mult))

            def route_experts(f, steps):
                steps.link(tt(g_gt[:], g_gt[:], g_eq[:], ALU.add))
                steps.link(nc.vector.tensor_reduce(g_rank[:], g_gt[:].rearrange("p t g o -> p (t g) o"), AX_X, ALU.add))
                steps.link(nc.vector.tensor_scalar(g_rank[:], g_rank[:], 2.0, None, ALU.is_lt))
                steps.link(tt(masked[:].rearrange("p t (g e) -> p (t g) e", e=EG),
                              sfc[:].rearrange("p (g e) -> p g e", e=EG),
                              g_rank[:].unsqueeze(2).broadcast_to((P, 16, EG)), ALU.mult))
                dve.sem_inc(max_go, 1)
                for t in range(TILES):
                    last = nc.vector.max(top8[:, t, :], masked[:, t, :])
                steps.link(last)
                fourth = per_tile(top8[:, :, 3])
                steps.link(tt(above[:], masked[:], fourth, ALU.is_gt))
                steps.link(tt(tied[:].rearrange("p (t e) -> p t e", t=TILES), masked[:], fourth, ALU.is_equal))
                steps.link(nc.vector.tensor_reduce(n_above[:], above[:], AX_X, ALU.add))
                steps.link(nc.vector.tensor_tensor_scan(order[:], restart[:], tied[:], 0.0, ALU.mult, ALU.add))
                order3 = order[:].rearrange("p (t e) -> p t e", t=TILES)
                steps.link(tt(order3, order3, per_tile(n_above[:]), ALU.add))

            def route_weights(f, steps):
                order3 = order[:].rearrange("p (t e) -> p t e", t=TILES)
                tied3 = tied[:].rearrange("p (t e) -> p t e", t=TILES)
                steps.link(nc.vector.scalar_tensor_tensor(chosen[:], order3, 4.0, tied3, ALU.is_le, ALU.mult))
                steps.link(tt(chosen[:], chosen[:], above[:], ALU.add))
                steps.link(tt(masked[:], masked[:], chosen[:], ALU.mult))
                steps.link(nc.vector.tensor_reduce(w_sum[:], masked[:], AX_X, ALU.add))
                steps.link(nc.vector.tensor_scalar(w_sum[:], w_sum[:], 1e-20, None, ALU.add))
                steps.link(nc.vector.reciprocal(w_sum[:], w_sum[:]))
                steps.link(nc.vector.scalar_tensor_tensor(combine[:], masked[:], SCALE, per_tile(w_sum[:]),
                                                          ALU.mult, ALU.mult))
                if not isinstance(f, int) or f > 0:
                    dve.wait_ge(combine_tok_t, f)
                steps.link(nc.vector.tensor_copy(combine_s[:, :, 0:EXPERTS], combine[:]))
                tt(combine_s[:, :, EXPERTS:2 * EXPERTS], combine[:], combine_s[:, :, 0:EXPERTS].bitcast(F32),
                   ALU.subtract).then_inc(combine_ready, 1)
                assert steps.n == ROUTE_STEPS, steps.n

            def ffn(f0, ln0):
                def add_y(f, c):
                    dve.wait_ge(yt_ready, f + (1 + YT_CREDIT))
                    xs = X[:, ds(c * CT, CT)]
                    nc.vector.scalar_tensor_tensor(xs, T0[:], 0.5, xs, ALU.mult, ALU.add).then_inc(ffn_x_done, 1)

                def chunk(c, prev, nxt, ln):
                    f = c + f0
                    n0, m0 = f * BLOCKS, f * PAIRS
                    if nxt:
                        steps = Steps(dve, route_step, (f + 1) * ROUTE_STEPS)
                    for j in range(BLOCKS):
                        if j < PAIRS:
                            dve.wait_ge(silu_done, n0 + (j + 1 + SILU_CREDIT))
                            dve.wait_ge(c_ready, m0 + (j + 1))
                            dve.wait_ge(gated_done, n0 + (j + 1 - 2 + Q_CREDIT))
                            tt(weighted[:, j % 2], pC[:], silu_g[:, j % 4], ALU.mult).then_inc(s_used, 1)
                            dve.wait_ge(s_used, m0 + (j + 1 + S_CREDIT))
                            factor = weighted[:, j % 2]
                        else:
                            dve.wait_ge(silu_done, n0 + (j + 1 + SILU_CREDIT))
                            factor = silu_s[:]
                        dve.wait_ge(u_ready, n0 + (j + 1))
                        dve.wait_ge(gated_lo_done, n0 + (j + 1 - 3 + QL_CREDIT))
                        tt(gated[:, j % 3], pU[:, j % 2], factor, ALU.mult).then_inc(gated_done, 1)
                        if j == 1 and nxt:
                            x_lo_part(f + 1, c + 1)
                        if j == 4 and nxt:
                            route_groups(f + 1, steps)
                        if j == 5 and prev:
                            add_y(f - 1, c - 1)
                        if j == 5 and nxt:
                            route_experts(f + 1, steps)
                        if j == 6 and nxt:
                            route_weights(f + 1, steps)
                        if j == 7 and ln:
                            if f0 == 0:
                                dve.wait_ge(x_loaded, c * 16 + 48)
                            ln_stats(c + (2 + ln0), (c + 2) * CT, TILES)
                        if j == 8 and ln:
                            ln_apply(c + (2 + ln0), (c + 2) * CT, TILES)

                chunk(0, False, True, True)
                with dve.Fori(1, CHUNKS - 2) as c:
                    chunk(c, True, True, True)
                chunk(CHUNKS - 2, True, True, False)
                chunk(CHUNKS - 1, True, False, False)
                add_y(f0 + CHUNKS - 1, CHUNKS - 1)

            def route(f):
                steps = Steps(dve, route_step, f * ROUTE_STEPS)
                route_groups(f, steps)
                route_experts(f, steps)
                route_weights(f, steps)

            def att_stats(a):
                ln_stats(a + LN_ATT, a * BT, 2)

            def stack_parts(a):
                dve.wait_ge(qkv_copied, 2 * a + 2)
                dve.wait_ge(stack_t_ready, 4 * a + STACK_CREDIT)
                s4 = stack[:].rearrange("p (t g) s -> p t g s", t=2)
                qk = qkv[:, :, 0:2 * H].rearrange("p t (g d) -> p t g d", g=2 * QG)
                nc.vector.tensor_copy(s4[:, :, :, 0:32], qk).then_inc(stack_ready, 1)
                dve.wait_ge(stack_ready, 2 * a + 1)
                tt(s4[:, :, :, 32:64], qk, s4[:, :, :, 0:32].bitcast(F32), ALU.subtract).then_inc(stack_ready, 1)

            def v_parts(a, steps):
                dve.wait_ge(kv_ready, a + KV_CREDIT)
                for t in range(2):
                    v = qkv[:, t, 2 * H:3 * H].rearrange("p (g k d) -> p g k d", g=QG, k=HG)
                    part = v_r[:, t].rearrange("p g (l k s) -> p l g k s", l=2, s=SLOT)
                    steps.link(nc.vector.tensor_copy(part[:, 0, :, :, 0:HD], v))
                    last = tt(part[:, 1, :, :, 0:HD], v, part[:, 0, :, :, 0:HD].bitcast(F32), ALU.subtract)
                last.then_inc(v_ready, 1)

            def squared_norms(a, steps):
                dve.wait_ge(squares_ready, a + 1)
                if not isinstance(a, int) or a > 0:
                    dve.wait_ge(ln_ready, a)
                steps.link(nc.vector.tensor_reduce(
                    n2[:].rearrange("p (t h) -> p t h", t=2),
                    squares[:].rearrange("p t (h d) -> p t h d", d=HD), AX_X, ALU.add))
                nc.vector.tensor_scalar(n2[:], n2[:], NORM2_LEAST, None, ALU.max).then_inc(n2_ready, 1)

            def norm_parts(a):
                dve.wait_ge(norm_ready, a + 1)
                nrm = norm[:].rearrange("p (t k) -> p t k", k=HG)
                nc.vector.tensor_copy(stack[:, :, 96:100], nrm).then_inc(norm_split, 1)
                dve.wait_ge(norm_split, 2 * a + 1)
                tt(stack[:, :, 100:104], nrm, stack[:, :, 96:100].bitcast(F32), ALU.subtract).then_inc(norm_split, 1)

            def stack_copies(a):
                for s in (1, 3):
                    dve.wait_ge(stack_t_ready, 4 * a + (s + 1 + STACK_CREDIT))
                    nc.vector.tensor_copy(qk_r[:, 2 * s:2 * s + 2].rearrange("p g n -> p (g n)"),
                                          T1[0:STACK, :]).then_inc(qk_odd_ready, 1)

            def k_lo_part(a, u):
                cols = slice(u * CT, (u + 1) * CT)
                dve.wait_ge(k_hi_done, 4 * a + (u + 1))
                tt(k_lo[:, cols], exp_k[:, cols], k_hi[:, cols].bitcast(F32), ALU.subtract).then_inc(k_lo_done, 1)

            def divide(a, steps):
                dve.wait_ge(o_tr_ready, a + 1)
                slots = T0[:].rearrange("p (h s) -> p h s", s=SLOT)
                steps.link(nc.vector.tensor_scalar(den[:], slots[:, :, HD], 1e-6, None, ALU.add))
                steps.link(nc.vector.reciprocal(rden[:], den[:]))
                if not isinstance(a, int) or a > 0:
                    dve.wait_ge(on_tr_ready, a)
                tt(on[:].rearrange("p (h d) -> p h d", d=HD), slots[:, :, 0:HD],
                   rden[:].unsqueeze(2).broadcast_to((P, 2 * HEADS, HD)), ALU.mult).then_inc(on_ready, 1)

            def add_projection(a):
                dve.wait_ge(proj_ready, a + (1 + PROJ_CREDIT))
                xs = X[:, ds(a * BT, BT)]
                tt(xs, T0[:, 0:BT], xs, ALU.add).then_inc(att_x_added, 1)

            def kv_parts(a, steps):
                for jh, bank in enumerate((T0, T1)):
                    dve.wait_ge(kv_tr_ready, 2 * a + (jh + 1 + KV_TR_CREDIT))
                    rows = bank[:].rearrange("p (g r w) -> p g r w", g=2, r=2)
                    for r in range(2):
                        w = 2 * SLOT * r
                        own = slice(r, 4, 2)
                        last = nc.vector.tensor_copy(kv_tmp[:, jh, own, :], rows[:, :, r, M + w:M + w + 2 * SLOT])
                    steps.link(last)
                    for r in range(2):
                        w = 2 * SLOT * r
                        own = slice(r, 4, 2)
                        last = tt(kv_sum[:, jh, own, :], rows[:, :, r, w:w + 2 * SLOT], kv_tmp[:, jh, own, :], ALU.add)
                    last.then_inc(kv_tr_read, 1)
                dve.wait_ge(kv_tr_read, 2 * a + 2)
                flat = "p j k s -> p (j k) s"
                mask = head_mask[:].unsqueeze(1).broadcast_to((P, 8, 2 * SLOT))
                steps.link(tt(kv_own[:].rearrange(flat), kv_sum[:].rearrange(flat), mask, ALU.mult))
                dve.wait_ge(o_ready, a + O_CREDIT)
                hi = kv_hi[:].rearrange("p j (k s) -> p j k s", s=DIAG)[:, :, :, 0:2 * SLOT]
                lo = kv_lo[:].rearrange("p j (k s) -> p j k s", s=DIAG)[:, :, :, 0:2 * SLOT]
                steps.link(nc.vector.tensor_copy(hi, kv_own[:]))
                tt(lo, kv_own[:], hi.bitcast(F32), ALU.subtract).then_inc(kv_split, 1)

            def front_steps(a, steps):
                stack_parts(a)
                v_parts(a, steps)

            def row(a, late, front, ln):
                steps = Steps(dve, att_step, a * ROW_STEPS + (FRONT_STEPS - DIVIDE_STEPS) if late else FRONT_STEPS)
                k_lo_part(a, 0)
                k_lo_part(a, 1)
                if ln:
                    att_stats(a + 2)
                k_lo_part(a, 2)
                k_lo_part(a, 3)
                if ln:
                    ln_apply(a + (2 + LN_ATT), (a + 2) * BT, 2)
                if late:
                    divide(a - 1, steps)
                if front:
                    front_steps(a + 1, steps)
                    squared_norms(a + 1, steps)
                if late:
                    add_projection(a - 1)
                if front:
                    norm_parts(a + 1)
                    stack_copies(a + 1)
                kv_parts(a, steps)
                assert steps.n == (DIVIDE_STEPS if late else 0) + (FRONT_STEPS if front else 0) + KV_STEPS, steps.n

            dve.wait_ge(x_loaded, 16)
            ln_stats(0, 0, TILES)
            ln_apply(0, 0, TILES)
            dve.wait_ge(small_hi_ready, 2)
            tt(gk_lo[:, 0:EXPERTS], gk_raw[:], gk_hi[:, 0:EXPERTS].bitcast(F32), ALU.subtract).then_inc(small_lo_ready, 1)
            x_lo_part(0, 0)
            weight_lo(0)
            weight_lo(1)
            dve.wait_ge(const_step, ROUTE_CONSTS)
            route(0)
            weight_lo(2)
            dve.wait_ge(x_loaded, 32)
            ln_stats(1, CT, TILES)
            ln_apply(1, CT, TILES)
            ffn(0, 0)

            dve.wait_ge(const_step, ALL_CONSTS)
            dve.wait_ge(ffn_x_done, CHUNKS)
            att_stats(0)
            ln_apply(LN_ATT, 0, 2)
            dve.wait_ge(rf_ready, 1)
            tt(rf_r[64:96, :], rf_raw[64:96, :], rf_r[64:96, :].bitcast(F32), ALU.subtract).then_inc(rf_ready, 1)
            prologue = Steps(dve, att_step, 0)
            att_stats(1)
            front_steps(0, prologue)
            squared_norms(0, prologue)
            assert prologue.n == FRONT_STEPS, prologue.n
            ln_apply(LN_ATT + 1, BT, 2)
            norm_parts(0)
            stack_copies(0)
            row(0, False, True, True)
            with dve.Fori(1, ROWS - 2) as a:
                row(a, True, True, True)
            row(ROWS - 2, True, True, False)
            row(ROWS - 1, True, False, False)
            divide(ROWS - 1, Steps(dve, att_step, ROWS * ROW_STEPS - DIVIDE_STEPS))
            add_projection(ROWS - 1)

            dve.wait_ge(att_x_done, ROWS)
            ln_stats(LN_FFN2, 0, TILES)
            ln_apply(LN_FFN2, 0, TILES)
            x_lo_part(CHUNKS, 0)
            ln_stats(LN_FFN2 + 1, CT, TILES)
            route(CHUNKS)
            ln_apply(LN_FFN2 + 1, CT, TILES)
            ffn(CHUNKS, LN_FFN2)

        @block.tensor
        def _(pe):
            pe.sem_inc(down_done, D_CREDIT)
            pe.sem_inc(yt_ready, YT_CREDIT)
            pe.sem_inc(xt_ready, XT_CREDIT)
            pe.sem_inc(stack_t_ready, STACK_CREDIT)
            pe.sem_inc(kv_ready, KV_CREDIT)
            pe.sem_inc(kv_tr_ready, KV_TR_CREDIT)
            pe.sem_inc(o_ready, O_CREDIT)
            pe.sem_inc(proj_ready, PROJ_CREDIT)

            def three_passes(o, w_h, w_l, x_h, x_l, start=True, stop=True):
                nc.tensor.matmul(o, w_h, x_h, start=start, stop=False)
                nc.tensor.matmul(o, w_h, x_l, start=False, stop=False)
                return nc.tensor.matmul(o, w_l, x_h, start=False, stop=stop)

            def transpose_x(p, bank, n):
                pe.wait_ge(xn_ready, p + 1)
                for t in range(n):
                    last = nc.tensor.transpose(bank[:, t * P:(t + 1) * P], xn[:, t * H:(t + 1) * H], ident[:])
                last.then_inc(xt_ready, 1)

            def logits(f, c):
                pe.wait_ge(xlo_ready, f + 1)
                if not isinstance(f, int) or f > 0:
                    pe.wait_ge(sfc_ready, f)
                cols = ds(c * CT, CT)
                three_passes(T1[:], gk_hi[:], gk_lo[:], x_hi[:, cols], x_lo[:, cols]).then_inc(logits_ready, 1)

            def scores_to_tokens(f):
                pe.wait_ge(scores_ready, f + 1)
                for t in range(TILES):
                    last = nc.tensor.transpose(T1[:, t * P:(t + 1) * P], scores_t[:, t * P:(t + 1) * P], ident[:])
                last.then_inc(scores_tok_ready, 1)

            def transpose_combine(f):
                pe.wait_ge(combine_ready, f + 1)
                for t in range(TILES):
                    last = nc.tensor.transpose(T0[:, t * P:(t + 1) * P], combine_s[:, t, :].bitcast(F32), ident[:])
                last.then_inc(combine_tok_t, 1)

            def ffn(f0, ln0):
                def down(n, j):
                    pe.wait_ge(gated_lo_done, n + (1 + QL_CREDIT))
                    return three_passes(pY[:], w_block(w_hi, 2, j), w_block(w_lo, 2, j), gated_hi[:, j % 3],
                                        gated_lo[:, j % 3], start=(j == 0), stop=(j == BLOCKS - 1)
                                        ).then_inc(down_done, 1)

                def transpose_y(f):
                    pe.wait_ge(y_done, f + (1 + Y_CREDIT))
                    for t in range(TILES):
                        last = nc.tensor.transpose(T0[:, t * P:(t + 1) * P], y_sb[:, t * P:(t + 1) * P], ident[:])
                    last.then_inc(yt_ready, 1)

                def chunk(c, prev, nxt):
                    f = c + f0
                    n0, m0 = f * BLOCKS, f * PAIRS
                    cols = ds(c * CT, CT)
                    first = isinstance(f, int) and f == 0
                    pe.wait_ge(xlo_ready, f + 1)
                    for j in range(BLOCKS):
                        if first and j == 0:
                            pe.wait_ge(w_lo_ready, 2)
                        pe.wait_ge(silu_done, n0 + ((j if j == 0 else j - 1) + SILU_CREDIT))
                        three_passes(pG[:, j % 2], w_block(w_hi, 0, j), w_block(w_lo, 0, j), x_hi[:, cols],
                                     x_lo[:, cols]).then_inc(g_ready, 1)
                        pe.wait_ge(gated_done, n0 + ((j if j == 0 else j - 1) + Q_CREDIT))
                        three_passes(pU[:, j % 2], w_block(w_hi, 1, j), w_block(w_lo, 1, j), x_hi[:, cols],
                                     x_lo[:, cols]).then_inc(u_ready, 1)
                        if j < PAIRS:
                            if j == 0:
                                pe.wait_ge(combine_t_ready, f + 1)
                            pe.wait_ge(s_used, m0 + (j + S_CREDIT))
                            nc.tensor.matmul(pC[:], sel_r[:, j * P:(j + 1) * P], combine_t[:, cols], start=True,
                                             stop=True).then_inc(c_ready, 1)
                        if first and j == 3:
                            pe.wait_ge(w_lo_ready, 3)
                        if j == 3:
                            pe.wait_ge(y_done, f + Y_CREDIT)
                        if j >= 3:
                            down(n0 + (j - 3), j - 3)
                        elif prev:
                            down(n0 + (j - 3), j + BLOCKS - 3)
                        if j == 0 and nxt:
                            transpose_x(c + (1 + ln0), T0, TILES)
                        if j == 2 and nxt:
                            logits(f + 1, c + 1)
                        if j == 3 and nxt:
                            scores_to_tokens(f + 1)
                        if j == 4 and prev:
                            if nxt:
                                pe.wait_ge(xlo_ready, f + 2)
                            transpose_y(f - 1)
                        if j == 7 and nxt:
                            if prev:
                                pe.wait_ge(ffn_x_done, f)
                            transpose_combine(f + 1)

                chunk(0, False, True)
                with pe.Fori(1, CHUNKS - 1) as c:
                    chunk(c, True, True)
                chunk(CHUNKS - 1, True, False)
                for j in range(BLOCKS - 3, BLOCKS):
                    down((f0 + CHUNKS - 1) * BLOCKS + j, j)
                pe.wait_ge(ffn_x_done, f0 + CHUNKS - 1)
                transpose_y(f0 + CHUNKS - 1)

            def qkv_product(a, t):
                bank = (T0, T1)[t]
                if t == 0:
                    pe.wait_ge(xta_ready, a + 1)
                    if not isinstance(a, int) or a > 1:
                        pe.wait_ge(kv_tr_read, 2 * a - 3)
                elif not isinstance(a, int) or a > 1:
                    pe.wait_ge(kv_tr_read, 2 * a - 2)
                nc.tensor.matmul(bank[:, 0:3 * H], x_t[:, t * P:(t + 1) * P], wqkv_sb[:], start=True,
                                 stop=True).then_inc(qkv_ready, 1)

            def transpose_stack(a):
                pe.wait_ge(stack_ready, 2 * a + 2)
                pe.wait_ge(stack_dup_ready, a + 1)
                pe.wait_ge(norm_split, 2 * a + 2)
                for s in range(4):
                    bank = (T0, T1)[s % 2]
                    if s == 2:
                        pe.wait_ge(qk_even_ready, 2 * a + 1)
                    if s == 3:
                        pe.wait_ge(qk_odd_ready, 2 * a + 1)
                    for i in range(2):
                        for t in range(2):
                            last = nc.tensor.transpose(bank[0:STACK, i * BT + t * P:i * BT + (t + 1) * P],
                                                       stack[:, 2 * QG * t + 2 * s + i, :].bitcast(F32), ident[:])
                    last.then_inc(stack_t_ready, 1)

            def k_unit(a, u):
                t, half = u // 2, u % 2
                pe.wait_ge(exp_done, 8 * a + (u + 1 - 2 + EXP_CREDIT))
                for i in range(2):
                    last = nc.tensor.matmul(pG[:, u % 2, i * BT:(i + 1) * BT],
                                            qk_r[:, QG + 2 * half + i, t * P:(t + 1) * P], rf_r[:],
                                            start=True, stop=True)
                last.then_inc(feat_ready, 1)

            def q_unit(a, u):
                pe.wait_ge(exp_done, 8 * a + (4 + u + 1 - 2 + EXP_CREDIT))
                for i in range(2):
                    last = nc.tensor.matmul(pG[:, u % 2, i * BT:(i + 1) * BT], rf_r[:, i * P:(i + 1) * P],
                                            qk_r[:, u, :], start=True, stop=True)
                last.then_inc(feat_ready, 1)

            def kv_product(a):
                pe.wait_ge(v_ready, a + 1)
                pe.wait_ge(k_lo_done, 4 * a + (4 + K_CREDIT))
                pe.wait_ge(kv_copied, a + KV_COPY_CREDIT)
                for g in range(QG):
                    o = pU[:, g // 2, (g % 2) * BT:(g % 2 + 1) * BT]
                    for n, (t, k) in enumerate([(0, k_hi), (0, k_lo), (1, k_hi), (1, k_lo)]):
                        col = t * HEADS * NF + g * BT
                        last = nc.tensor.matmul(o, v_r[:, t, g, :], k[:, col:col + BT], start=(n == 0), stop=(n == 3))
                last.then_inc(kv_ready, 1)

            def transpose_kv(a):
                pe.wait_ge(kv_copied, a + (1 + KV_COPY_CREDIT))
                for jh, bank in enumerate((T0, T1)):
                    for k in range(4):
                        j = 4 * jh + k
                        last = nc.tensor.transpose(bank[:, k * P:(k + 1) * P], kv_t[:, j * P:(j + 1) * P], ident[:])
                    last.then_inc(kv_tr_ready, 1)

            def o_product(a, jh):
                if jh == 0:
                    pe.wait_ge(kv_split, a + 1)
                    pe.wait_ge(o_copied, a + O_COPY_CREDIT)
                    pe.wait_ge(q_lo_done, 4 * a + (2 + QF_CREDIT))
                else:
                    pe.wait_ge(q_lo_done, 4 * a + (4 + QF_CREDIT))
                for k in range(4):
                    q = slice((4 * jh + k) * BT, (4 * jh + k + 1) * BT)
                    w = slice(k * P, (k + 1) * P)
                    last = three_passes(pC[:, jh * BT:(jh + 1) * BT], kv_hi[:, jh, w], kv_lo[:, jh, w], q_hi[:, q],
                                        q_lo[:, q], start=(k == 0), stop=(k == 3))
                if jh == 1:
                    last.then_inc(o_ready, 1)

            def transpose_o(a):
                pe.wait_ge(o_copied, a + (1 + O_COPY_CREDIT))
                for t in range(2):
                    for jh in range(2):
                        c = (2 * t + jh) * P
                        last = nc.tensor.transpose(T0[:, c:c + P], o_sb[:, jh * BT + t * P:jh * BT + (t + 1) * P],
                                                   ident[:])
                last.then_inc(o_tr_ready, 1)

            def transpose_on(a):
                pe.wait_ge(on_ready, a + 1)
                for t in range(2):
                    last = nc.tensor.transpose(T1[:, t * P:(t + 1) * P], on[:, t * P:(t + 1) * P], ident[:])
                last.then_inc(on_tr_ready, 1)

            def projection(a):
                pe.wait_ge(on_copied, a + 1)
                for t in range(2):
                    last = nc.tensor.matmul(T0[:, t * P:(t + 1) * P], on_t[:, t * P:(t + 1) * P], wout_sb[:],
                                            start=True, stop=True)
                last.then_inc(proj_ready, 1)

            def row(a, late, front, xt):
                pe.wait_ge(qk_even_ready, 2 * a + 2)
                pe.wait_ge(qk_odd_ready, 2 * a + 2)
                k_unit(a, 0)
                k_unit(a, 1)
                if late:
                    o_product(a - 1, 0)
                k_unit(a, 2)
                k_unit(a, 3)
                if late:
                    o_product(a - 1, 1)
                if front:
                    qkv_product(a + 1, 0)
                    qkv_product(a + 1, 1)
                q_unit(a, 0)
                q_unit(a, 1)
                if late:
                    if front:
                        pe.wait_ge(qkv_copied, 2 * a + 3)
                    else:
                        pe.wait_ge(kv_tr_read, 2 * a - 1)
                    transpose_o(a - 1)
                q_unit(a, 2)
                kv_product(a)
                q_unit(a, 3)
                if late:
                    if front:
                        pe.wait_ge(qkv_copied, 2 * a + 4)
                    else:
                        pe.wait_ge(kv_tr_read, 2 * a)
                    transpose_on(a - 1)
                    projection(a - 1)
                if xt:
                    if not late:
                        pe.wait_ge(qkv_copied, 2 * a + 4)
                    transpose_x(a + (2 + LN_ATT), T1, 2)
                if front:
                    if late:
                        pe.wait_ge(att_x_added, a)
                        pe.wait_ge(on_copied, a)
                    if xt:
                        pe.wait_ge(xta_ready, a + 3)
                    transpose_stack(a + 1)
                    pe.wait_ge(qk_even_ready, 2 * a + 4)
                    pe.wait_ge(qk_odd_ready, 2 * a + 4)
                else:
                    pe.wait_ge(att_x_added, a)
                    pe.wait_ge(on_copied, a)
                transpose_kv(a)

            pe.wait_ge(const_step, GK_CONSTS)
            transpose_x(0, T0, TILES)
            pe.wait_ge(small_lo_ready, 1)
            logits(0, 0)
            scores_to_tokens(0)
            transpose_combine(0)
            ffn(0, 0)

            pe.wait_ge(small_loaded, 16 * 6)
            pe.wait_ge(silu_done, CHUNKS * BLOCKS + SILU_CREDIT)
            pe.wait_ge(gated_done, CHUNKS * BLOCKS + Q_CREDIT)
            pe.wait_ge(sfc_ready, CHUNKS)
            pe.wait_ge(ffn_x_done, CHUNKS)
            transpose_x(LN_ATT, T1, 2)
            qkv_product(0, 0)
            qkv_product(0, 1)
            pe.wait_ge(qkv_copied, 2)
            transpose_x(LN_ATT + 1, T1, 2)
            pe.wait_ge(xta_ready, 2)
            transpose_stack(0)
            pe.wait_ge(rf_ready, 2)
            row(0, False, True, True)
            with pe.Fori(1, ROWS - 2) as a:
                row(a, True, True, True)
            row(ROWS - 2, True, True, False)
            row(ROWS - 1, True, False, False)
            o_product(ROWS - 1, 0)
            o_product(ROWS - 1, 1)
            pe.wait_ge(kv_tr_read, 2 * ROWS)
            transpose_o(ROWS - 1)
            transpose_on(ROWS - 1)
            projection(ROWS - 1)

            pe.wait_ge(att_x_added, ROWS)
            pe.wait_ge(exp_done, 8 * ROWS + EXP_CREDIT)
            transpose_x(LN_FFN2, T0, TILES)
            logits(CHUNKS, 0)
            scores_to_tokens(CHUNKS)
            pe.wait_ge(xlo_ready, CHUNKS + 1)
            transpose_combine(CHUNKS)
            ffn(CHUNKS, LN_FFN2)


def kernel(**inputs):
    import numpy as np
    import concourse.bacc as bacc
    from concourse.bass_utils import run_bass_kernel_spmd

    i = {name: np.asarray(a) for name, a in inputs.items()}
    shape = i["L0_attn_x"].shape

    def up(name, shared):
        w = i[name].transpose(1, 0, 2).reshape(H, EXPERTS * M)
        return np.concatenate([w, i[shared]], axis=1)

    down = i["L0_ffn_w_down"].reshape(PAIRS, P, H).transpose(1, 0, 2).reshape(P, PAIRS * H)
    down = np.concatenate([down, i["L0_ffn_sw_down"]], axis=1)
    wall = np.concatenate([up("L0_ffn_w_gate", "L0_ffn_sw_gate"), up("L0_ffn_w_up", "L0_ffn_sw_up"), down], axis=1)

    pair_sel = np.zeros((P, PAIRS * P), np.float32)
    for e in range(EXPERTS):
        pair_sel[[e, EXPERTS + e], e * M:(e + 1) * M] = 1.0
    norm_sel = np.zeros((2 * HG, HG * NF), np.float32)
    for h in range(HG):
        norm_sel[[h, HG + h], h * NF:(h + 1) * NF] = -float(NF) ** 0.5

    arrays = {
        "x": i["L0_attn_x"].reshape(TOKENS, H),
        "wall": wall,
        "gate_k": i["L0_ffn_gate_kernel"],
        "gate_b": i["L0_ffn_gate_bias"],
        "wqkv": i["L0_attn_w_qkv"].T,
        "wout": i["L0_attn_w_out"].T,
        "b_out": i["L0_attn_b_out"],
        "rft": i["L0_attn_random_features"].T,
        "pair_sel": pair_sel,
        "norm_sel": norm_sel,
    }
    arrays = {name + "_dram": np.ascontiguousarray(a) for name, a in arrays.items()}
    nc = bacc.Bacc("TRN2", target_bir_lowering=False, num_devices=1)
    args = [nc.dram_tensor(name, a.shape, mybir.dt.from_np(a.dtype), kind="ExternalInput").ap()
            for name, a in arrays.items()]
    args.append(nc.dram_tensor("out_dram", (TOKENS, H), F32, kind="ExternalOutput").ap())
    macaron_kernel(nc, *args)
    r = run_bass_kernel_spmd(nc, [arrays], core_ids=[0])
    return r.results[0]["out_dram"].reshape(shape)
```

```python
from contextlib import ExitStack

import concourse.bass as bass
from concourse import mybir

F32 = mybir.dt.float32
F32R = mybir.dt.float32r
ALU = mybir.AluOpType
ACT = mybir.ActivationFunctionType
AX_X = mybir.AxisListType.X
ds = bass.ds

P = 128
H = 128
TOKENS = 4096
TILES = 4
CT = TILES * P
CHUNKS = TOKENS // CT
EXPERTS = 16
GROUPS = 4
EG = EXPERTS // GROUPS
M = 64
PAIRS = EXPERTS * M // P
BLOCKS = PAIRS + 1
SCALE = 2.5
LN_EPS = 1e-5
HEADS = 16
HD = H // HEADS
NF = 64
HG = 4
QG = HEADS // HG
STACK = 3 * HG * HD + 2 * HG
SLOT = 16
BT = 2 * P
ROWS = TOKENS // BT
DIAG = P + 2 * SLOT
LN_ATT = CHUNKS
LN_FFN2 = CHUNKS + ROWS

SILU_CREDIT = 2
S_CREDIT = 4
Q_CREDIT = 9
QL_CREDIT = 3
D_CREDIT = 3
Y_CREDIT = 1
YT_CREDIT = 1
XT_CREDIT = 1
EXP_CREDIT = 2
K_CREDIT = 4
QF_CREDIT = 4
KV_CREDIT = 1
KV_COPY_CREDIT = 1
KV_TR_CREDIT = 2
O_CREDIT = 1
O_COPY_CREDIT = 1
PROJ_CREDIT = 1
STACK_CREDIT = 4
N2_CREDIT = 1

ROUTE_STEPS = 20
DIVIDE_STEPS = 2
FRONT_STEPS = 3
KV_STEPS = 4
ROW_STEPS = DIVIDE_STEPS + FRONT_STEPS + KV_STEPS
GK_CONSTS = 5
ROUTE_CONSTS = GK_CONSTS + 1 + (GROUPS - 1) + 3
ALL_CONSTS = ROUTE_CONSTS + 7
NORM2_LEAST = 2.0 ** -60


def macaron_kernel(nc, x, wall, gate_k, gate_b, wqkv, wout, b_out, rft, pair_sel, norm_sel, out):
    x_v = x.rearrange("(c b p i) h -> c p b (i h)", c=CHUNKS, b=2, i=2)
    out_v = out.rearrange("(c b p i) h -> c p b (i h)", c=CHUNKS, b=2, i=2)

    with ExitStack() as ctx:
        def sb(name, shape, dt=F32):
            return ctx.enter_context(nc.sbuf_tensor(name, shape, dt))

        def psum(name, shape):
            return ctx.enter_context(nc.psum_tensor(name, shape, F32))

        def sem(name):
            return ctx.enter_context(nc.semaphore(name))

        X = sb("X", [P, CHUNKS * TILES * H])
        ident = sb("ident", [P, P])
        xn = sb("xn", [P, TILES * H])
        stats = sb("stats", [P, TILES, 6])
        meanvar = sb("meanvar", [P, TILES, 2])
        vareps = sb("vareps", [P, TILES])
        rstd = sb("rstd", [P, TILES])
        minus_half = sb("minus_half", [P, TILES])

        w_hi = sb("w_hi", [P, 3 * BLOCKS * P], F32R)
        w_lo = sb("w_lo", [P, 3 * BLOCKS * P], F32R)
        gk_hi = sb("gk_hi", [P, P], F32R)
        gk_lo = sb("gk_lo", [P, P], F32R)
        gk_raw = sb("gk_raw", [P, EXPERTS])
        gb_rows = sb("gb_rows", [P, EXPERTS])
        sel_r = sb("sel_r", [P, PAIRS * P], F32R)
        x_hi = sb("x_hi", [P, CHUNKS * CT], F32R)
        x_lo = sb("x_lo", [P, CHUNKS * CT], F32R)
        combine_t = sb("combine_t", [P, CHUNKS * CT], F32R)
        y_sb = sb("y_sb", [P, CT])
        scores_t = sb("scores_t", [P, CT])
        silu_g = sb("silu_g", [P, 4, CT])
        silu_s = sb("silu_s", [P, CT])
        weighted = sb("weighted", [P, 2, CT])
        gated = sb("gated", [P, 3, CT])
        gated_hi = sb("gated_hi", [P, 3, CT], F32R)
        gated_lo = sb("gated_lo", [P, 3, CT], F32R)

        sfc = sb("sfc", [P, TILES * EXPERTS])
        pair_hi = sb("pair_hi", [P, 16, 2])
        pair_lo = sb("pair_lo", [P, 16, 2])
        g_top = sb("g_top", [P, 16])
        g_mid = sb("g_mid", [P, 16])
        g_low = sb("g_low", [P, 16])
        g_sum = sb("g_sum", [P, TILES, GROUPS])
        g_gt = sb("g_gt", [P, TILES, GROUPS, GROUPS])
        g_eq = sb("g_eq", [P, TILES, GROUPS, GROUPS])
        g_before = sb("g_before", [P, GROUPS, GROUPS])
        g_rank = sb("g_rank", [P, 16])
        masked = sb("masked", [P, TILES, EXPERTS])
        top8 = sb("top8", [P, TILES, 8])
        above = sb("above", [P, TILES, EXPERTS])
        tied = sb("tied", [P, TILES * EXPERTS])
        n_above = sb("n_above", [P, TILES])
        restart = sb("restart", [P, TILES * EXPERTS])
        order = sb("order", [P, TILES * EXPERTS])
        chosen = sb("chosen", [P, TILES, EXPERTS])
        w_sum = sb("w_sum", [P, TILES])
        combine = sb("combine", [P, TILES, EXPERTS])
        combine_s = sb("combine_s", [P, TILES, P], F32R)

        wqkv_sb = sb("wqkv_sb", [P, 3 * H])
        wout_sb = sb("wout_sb", [P, H])
        bout_rows = sb("bout_rows", [P, H])
        rf_raw = sb("rf_raw", [STACK, HG * NF])
        rf_r = sb("rf_r", [STACK, HG * NF], F32R)
        x_t = sb("x_t", [P, BT])
        qkv = sb("qkv", [P, 2, 3 * H])
        squares = sb("squares", [P, 2, 2 * H])
        n2 = sb("n2", [P, 2 * 2 * HEADS])
        ln_n2 = sb("ln_n2", [P, 2 * 2 * HEADS])
        norm = sb("norm", [P, 2 * 2 * HEADS])
        stack = sb("stack", [P, 2 * 2 * QG, STACK], F32R)
        qk_r = sb("qk_r", [STACK, 2 * QG, BT], F32R)
        v_r = sb("v_r", [P, 2, QG, P], F32R)
        exp_k = sb("exp_k", [P, 2 * 1024])
        exp_q = silu_g[:].rearrange("p b n -> p (b n)")
        k_lo = x_hi[:, 0:2048]
        q_lo = x_hi[:, 2048:4096]
        k_hi = x_lo[:, 0:2048]
        q_hi = x_lo[:, 2048:4096]
        kv_t = sb("kv_t", [P, 4 * BT])
        kv_tmp = sb("kv_tmp", [P, 2, 4, 2 * SLOT])
        kv_sum = sb("kv_sum", [P, 2, 4, 2 * SLOT])
        kv_own = sb("kv_own", [P, 2, 4, 2 * SLOT])
        head_mask = sb("head_mask", [P, 2 * SLOT])
        kv_hi = sb("kv_hi", [P, 2, 4 * DIAG], F32R)
        kv_lo = sb("kv_lo", [P, 2, 4 * DIAG], F32R)
        o_sb = sb("o_sb", [P, CT])
        den = sb("den", [P, 2 * HEADS])
        rden = sb("rden", [P, 2 * HEADS])
        on = sb("on", [P, BT])
        on_t = sb("on_t", [P, BT])

        pG = psum("pG", [P, 2, 512])
        pU = psum("pU", [P, 2, 512])
        pC = psum("pC", [P, 512])
        pY = psum("pY", [P, 512])
        T0 = psum("T0", [P, 512])
        T1 = psum("T1", [P, 512])

        x_loaded = sem("x_loaded")
        w_loaded = [sem(f"w_loaded_{kind}") for kind in ("gate", "up", "down")]
        small_loaded = sem("small_loaded")
        rf_zeroed = sem("rf_zeroed")
        rf_loaded = sem("rf_loaded")
        rf_ready = sem("rf_ready")
        out_stored = sem("out_stored")
        const_step = sem("const_step")
        w_hi_ready = sem("w_hi_ready")
        w_lo_ready = sem("w_lo_ready")
        small_hi_ready = sem("small_hi_ready")
        small_lo_ready = sem("small_lo_ready")
        route_step = sem("route_step")
        att_step = sem("att_step")
        bn_step = sem("bn_step")
        var_ready = sem("var_ready")
        bn_aggr_go = sem("bn_aggr_go")
        max_go = sem("max_go")
        pool_go = sem("pool_go")
        mv_ready = sem("mv_ready")
        rstd_ready = sem("rstd_ready")
        xn_ready = sem("xn_ready")
        xt_ready = sem("xt_ready")
        xhi_ready = sem("xhi_ready")
        xlo_ready = sem("xlo_ready")
        logits_ready = sem("logits_ready")
        scores_ready = sem("scores_ready")
        scores_tok_ready = sem("scores_tok_ready")
        sfc_ready = sem("sfc_ready")
        combine_hi_ready = sem("combine_hi_ready")
        combine_ready = sem("combine_ready")
        combine_tok_t = sem("combine_tok_t")
        combine_t_ready = sem("combine_t_ready")
        g_ready = sem("g_ready")
        u_ready = sem("u_ready")
        c_ready = sem("c_ready")
        silu_done = sem("silu_done")
        s_used = sem("s_used")
        gated_done = sem("gated_done")
        gated_hi_done = sem("gated_hi_done")
        gated_lo_done = sem("gated_lo_done")
        down_done = sem("down_done")
        y_done = sem("y_done")
        yt_ready = sem("yt_ready")
        ffn_x_done = sem("ffn_x_done")

        xta_ready = sem("xta_ready")
        qkv_ready = sem("qkv_ready")
        qkv_copied = sem("qkv_copied")
        squares_ready = sem("squares_ready")
        n2_ready = sem("n2_ready")
        ln_ready = sem("ln_ready")
        norm_split = sem("norm_split")
        norm_ready = sem("norm_ready")
        stack_ready = sem("stack_ready")
        stack_dup_ready = sem("stack_dup_ready")
        v_ready = sem("v_ready")
        stack_t_ready = sem("stack_t_ready")
        qk_even_ready = sem("qk_even_ready")
        qk_odd_ready = sem("qk_odd_ready")
        feat_ready = sem("feat_ready")
        exp_done = sem("exp_done")
        k_hi_done = sem("k_hi_done")
        k_lo_done = sem("k_lo_done")
        q_hi_done = sem("q_hi_done")
        q_lo_done = sem("q_lo_done")
        kv_ready = sem("kv_ready")
        kv_copied = sem("kv_copied")
        kv_tr_ready = sem("kv_tr_ready")
        kv_tr_read = sem("kv_tr_read")
        kv_split = sem("kv_split")
        o_ready = sem("o_ready")
        o_copied = sem("o_copied")
        o_tr_ready = sem("o_tr_ready")
        on_ready = sem("on_ready")
        on_tr_ready = sem("on_tr_ready")
        on_copied = sem("on_copied")
        proj_ready = sem("proj_ready")
        att_x_added = sem("att_x_added")
        att_x_done = sem("att_x_done")

        def tiles_of(ap, n=TILES):
            return ap.rearrange("p (t h) -> p t h", t=n)

        def w_block(w, kind, j):
            k = (kind * BLOCKS + j) * P
            return w[:, k:k + P]

        wn = BLOCKS * P
        sel_raw = kv_t
        w_stage = [exp_k[:, 0:wn], exp_q[:, 0:wn], gated[:].rearrange("p b n -> p (b n)")[:, 0:wn]]

        class Steps:
            def __init__(self, eng, s, base=0):
                self.eng, self.s, self.base, self.n = eng, s, base, 0

            def mark(self, ins):
                self.n += 1
                ins.then_inc(self.s, 1)

            def wait(self):
                self.eng.wait_ge(self.s, self.base + self.n)

            def link(self, ins):
                self.mark(ins)
                self.wait()

        block = ctx.enter_context(nc.Block())

        @block.sync
        def _(sp):
            def x_chunk(c):
                return X[:, c * CT:(c + 1) * CT].rearrange("p (b w) -> p b w", b=2)

            sp.dma_start(x_chunk(0), x_v[0]).then_inc(x_loaded, 16)
            sp.dma_start(gk_raw[:], gate_k).then_inc(small_loaded, 16)
            sp.dma_start(gb_rows[:], gate_b.partition_broadcast(P)).then_inc(small_loaded, 16)
            sp.dma_start(sel_raw[:], pair_sel).then_inc(small_loaded, 16)
            for c in range(1, CHUNKS):
                sp.wait_ge(x_loaded, 16 * c)
                sp.dma_start(x_chunk(c), x_v[c]).then_inc(x_loaded, 16)
            sp.dma_start(wqkv_sb[:], wqkv).then_inc(small_loaded, 16)
            sp.dma_start(wout_sb[:], wout).then_inc(small_loaded, 16)
            sp.dma_start(bout_rows[:], b_out.partition_broadcast(P)).then_inc(small_loaded, 16)
            sp.wait_ge(rf_zeroed, 1)
            for part in range(3):
                for hh in range(HG):
                    r = (part * HG + hh) * HD
                    sp.dma_start(rf_raw[r:r + HD, hh * NF:(hh + 1) * NF], rft).then_inc(rf_loaded, 16)
            sp.dma_start(rf_raw[3 * HG * HD:STACK, :], norm_sel).then_inc(rf_loaded, 16)
            for c in range(CHUNKS):
                sp.wait_ge(ffn_x_done, CHUNKS + c + 1)
                sp.dma_start(out_v[c], x_chunk(c)).then_inc(out_stored, 16)
            sp.wait_ge(out_stored, 16 * CHUNKS)

        @block.gpsimd
        def _(pool):
            pool.sem_inc(gated_lo_done, QL_CREDIT)
            pool.sem_inc(q_lo_done, QF_CREDIT)

            def rstd_of(p, n):
                pool.wait_ge(mv_ready, p + 1)
                pool.sem_inc(pool_go, 1)
                nc.gpsimd.tensor_scalar(vareps[:, 0:n], meanvar[:, 0:n, 1], LN_EPS, 0.0, ALU.add,
                                        ALU.add).then_inc(var_ready, 1)
                pool.wait_ge(var_ready, p + 1)
                nc.gpsimd.tensor_tensor(rstd[:, 0:n], vareps[:, 0:n], minus_half[:, 0:n],
                                        ALU.pow).then_inc(rstd_ready, 1)

            def constants():
                steps = Steps(pool, const_step)
                steps.link(nc.gpsimd.memset(minus_half[:], -0.5))
                steps.link(nc.gpsimd.memset(ident[:], 0.0))
                steps.link(nc.gpsimd.affine_select(out=ident[:], in_=ident[:], compare_op=ALU.not_equal,
                                                   fill=1.0, base=0, pattern=[[-1, P]], channel_multiplier=1))
                steps.link(nc.gpsimd.memset(gk_hi[:].bitcast(F32), 0.0))
                steps.link(nc.gpsimd.memset(gk_lo[:].bitcast(F32), 0.0))
                assert steps.n == GK_CONSTS
                rstd_of(0, TILES)
                steps.link(nc.gpsimd.memset(g_before[:], 0.0))
                for g in range(1, GROUPS):
                    steps.link(nc.gpsimd.memset(g_before[:, g, 0:g], 1.0))
                steps.link(nc.gpsimd.memset(restart[:], 1.0))
                steps.link(nc.gpsimd.memset(restart[:, 0::EXPERTS], 0.0))
                steps.link(nc.gpsimd.memset(combine_s[:].bitcast(F32), 0.0))
                assert steps.n == ROUTE_CONSTS
                rstd_of(1, TILES)
                nc.gpsimd.memset(rf_raw[:], 0.0).then_inc(rf_zeroed, 1)
                steps.link(nc.gpsimd.memset(head_mask[:], 0.0))
                steps.link(nc.gpsimd.memset(head_mask[0:M, 0:SLOT], 1.0))
                steps.link(nc.gpsimd.memset(head_mask[M:P, SLOT:2 * SLOT], 1.0))
                steps.link(nc.gpsimd.memset(v_r[:].bitcast(F32), 0.0))
                ones_cols = v_r[:, :, :, 0:HG * SLOT].rearrange("p t g (k s) -> p (t g) k s", s=SLOT)[:, :, :, HD]
                steps.link(nc.gpsimd.memset(ones_cols.bitcast(F32), 1.0))
                steps.link(nc.gpsimd.memset(kv_hi[:].bitcast(F32), 0.0))
                steps.link(nc.gpsimd.memset(kv_lo[:].bitcast(F32), 0.0))
                assert steps.n == ALL_CONSTS

            def ffn(f0, ln0):
                def lo_part(n, j):
                    pool.wait_ge(gated_hi_done, n + 1)
                    nc.gpsimd.tensor_tensor(gated_lo[:, j % 3], gated[:, j % 3], gated_hi[:, j % 3].bitcast(F32),
                                            ALU.subtract).then_inc(gated_lo_done, 1)

                def chunk(c, prev, nxt2):
                    n0 = (c + f0) * BLOCKS
                    for j in range(BLOCKS):
                        if j >= 1:
                            lo_part(n0 + (j - 1), j - 1)
                        elif prev:
                            lo_part(n0 - 1, BLOCKS - 1)
                        if j == 2 and nxt2:
                            rstd_of(c + (2 + ln0), TILES)

                chunk(0, False, True)
                with pool.Fori(1, CHUNKS - 2) as c:
                    chunk(c, True, True)
                chunk(CHUNKS - 2, True, False)
                chunk(CHUNKS - 1, True, False)
                lo_part((f0 + CHUNKS) * BLOCKS - 1, BLOCKS - 1)

            def squares_and_dup(a):
                pool.wait_ge(qkv_copied, 2 * a + 2)
                pool.wait_ge(n2_ready, a + N2_CREDIT)
                nc.gpsimd.tensor_tensor(squares[:], qkv[:, :, 0:2 * H], qkv[:, :, 0:2 * H],
                                        ALU.mult).then_inc(squares_ready, 1)
                pool.wait_ge(stack_t_ready, 4 * a + STACK_CREDIT)
                pool.sem_inc(pool_go, 1)
                for t in range(2):
                    last = nc.gpsimd.tensor_scalar(
                        stack[:, 8 * t:8 * t + 8, 64:96],
                        qkv[:, t, 0:2 * H].rearrange("p (g d) -> p g d", g=2 * QG),
                        1.0, 0.0, ALU.mult, ALU.add)
                last.then_inc(stack_dup_ready, 1)

            def q_split(a, u):
                cols = slice(u * CT, (u + 1) * CT)
                pool.wait_ge(exp_done, 8 * a + (4 + u + 1 + EXP_CREDIT))
                pool.wait_ge(o_ready, a + O_CREDIT)
                pool.sem_inc(pool_go, 1)
                nc.gpsimd.tensor_scalar(q_hi[:, cols], exp_q[:, cols], 1.0, 0.0, ALU.mult,
                                        ALU.add).then_inc(q_hi_done, 1)
                pool.wait_ge(q_hi_done, 4 * a + (u + 1))
                nc.gpsimd.tensor_tensor(q_lo[:, cols], exp_q[:, cols], q_hi[:, cols].bitcast(F32),
                                        ALU.subtract).then_inc(q_lo_done, 1)

            def bias(a):
                pool.wait_ge(att_x_added, a + 1)
                xs = tiles_of(X[:, ds(a * BT, BT)], 2)
                nc.gpsimd.tensor_tensor(xs, xs, bout_rows[:].unsqueeze(1).broadcast_to((P, 2, H)),
                                        ALU.add).then_inc(att_x_done, 1)

            def row(a, late, front, ln):
                if ln:
                    rstd_of(a + (2 + LN_ATT), 2)
                if front:
                    squares_and_dup(a + 1)
                q_split(a, 0)
                q_split(a, 1)
                if late:
                    bias(a - 1)
                q_split(a, 2)
                q_split(a, 3)

            constants()
            ffn(0, 0)
            pool.wait_ge(small_loaded, 16 * 6)
            rstd_of(LN_ATT, 2)
            squares_and_dup(0)
            rstd_of(LN_ATT + 1, 2)
            row(0, False, True, True)
            with pool.Fori(1, ROWS - 2) as a:
                row(a, True, True, True)
            row(ROWS - 2, True, True, False)
            row(ROWS - 1, True, False, False)
            bias(ROWS - 1)
            rstd_of(LN_FFN2, TILES)
            rstd_of(LN_FFN2 + 1, TILES)
            ffn(CHUNKS, LN_FFN2)

        @block.scalar
        def _(act):
            for k, stage in enumerate(w_stage):
                act.dma_start(stage, wall[:, k * BLOCKS * P:(k + 1) * BLOCKS * P]).then_inc(w_loaded[k], 16)
            act.sem_inc(silu_done, SILU_CREDIT)
            act.sem_inc(y_done, Y_CREDIT)
            act.sem_inc(exp_done, EXP_CREDIT)
            act.sem_inc(kv_copied, KV_COPY_CREDIT)
            act.sem_inc(o_copied, O_COPY_CREDIT)

            def copy(o, i):
                return nc.scalar.activation(o, i, ACT.Copy)

            def x_hi_part(f, c, p):
                act.wait_ge(xt_ready, p + (1 + XT_CREDIT))
                copy(x_hi[:, ds(c * CT, CT)], T1[:]).then_inc(xhi_ready, 1)

            def scores(f):
                act.wait_ge(logits_ready, f + 1)
                if not isinstance(f, int) or f > 0:
                    act.wait_ge(scores_tok_ready, f)
                nc.scalar.activation(scores_t[:], T1[:], ACT.Sigmoid).then_inc(scores_ready, 1)

            def combine_copy(f, c):
                act.wait_ge(combine_tok_t, f + 1)
                copy(combine_t[:, ds(c * CT, CT)], T0[:]).then_inc(combine_t_ready, 1)

            def weight_hi(k):
                act.wait_ge(w_loaded[k], 16)
                copy(w_hi[:, k * BLOCKS * P:(k + 1) * BLOCKS * P], w_stage[k]).then_inc(w_hi_ready, 1)

            def ffn(f0, ln0):
                def hi_part(n, j):
                    act.wait_ge(gated_done, n + (1 + Q_CREDIT))
                    act.wait_ge(down_done, n + (1 - 3 + D_CREDIT))
                    copy(gated_hi[:, j % 3], gated[:, j % 3]).then_inc(gated_hi_done, 1)

                def y_copy(f):
                    act.wait_ge(down_done, f * BLOCKS + (BLOCKS + D_CREDIT))
                    act.wait_ge(yt_ready, f + YT_CREDIT)
                    copy(y_sb[:], pY[:]).then_inc(y_done, 1)

                def chunk(c, prev, nxt, nxt2):
                    f = c + f0
                    n0, m0 = f * BLOCKS, f * PAIRS
                    for j in range(BLOCKS):
                        if j == 3 and prev:
                            y_copy(f - 1)
                        if j == 6 and nxt2:
                            x_hi_part(f + 2, c + 2, c + (ln0 + 2))
                        if j == 8 and nxt2:
                            scores(f + 2)
                        act.wait_ge(g_ready, n0 + (j + 1))
                        if j < PAIRS:
                            act.wait_ge(s_used, m0 + (j + 1 - 4 + S_CREDIT))
                            nc.scalar.activation(silu_g[:, j % 4], pG[:, j % 2], ACT.Silu).then_inc(silu_done, 1)
                        else:
                            act.wait_ge(gated_done, n0 + (j + 1 - BLOCKS + Q_CREDIT))
                            nc.scalar.activation(silu_s[:], pG[:, j % 2], ACT.Silu).then_inc(silu_done, 1)
                        if j >= 1:
                            hi_part(n0 + (j - 1), j - 1)
                        elif prev:
                            hi_part(n0 - 1, BLOCKS - 1)
                        if j == 8 and nxt:
                            combine_copy(f + 1, c + 1)

                chunk(0, False, True, True)
                with act.Fori(1, CHUNKS - 2) as c:
                    chunk(c, True, True, True)
                chunk(CHUNKS - 2, True, True, False)
                chunk(CHUNKS - 1, True, False, False)
                hi_part((f0 + CHUNKS) * BLOCKS - 1, BLOCKS - 1)
                y_copy(f0 + CHUNKS - 1)

            def x_t_copy(a):
                act.wait_ge(xt_ready, a + (LN_ATT + 1 + XT_CREDIT))
                if not isinstance(a, int) or a > 0:
                    act.wait_ge(qkv_ready, 2 * a)
                copy(x_t[:], T1[:, 0:BT]).then_inc(xta_ready, 1)

            def qkv_copy(a):
                if not isinstance(a, int) or a > 0:
                    act.wait_ge(v_ready, a)
                    act.wait_ge(stack_dup_ready, a)
                for t, bank in enumerate((T0, T1)):
                    act.wait_ge(qkv_ready, 2 * a + (t + 1))
                    copy(qkv[:, t], bank[:, 0:3 * H]).then_inc(qkv_copied, 1)

            def norms(a):
                act.wait_ge(n2_ready, a + (1 + N2_CREDIT))
                nc.scalar.activation(ln_n2[:], n2[:], ACT.Ln).then_inc(ln_ready, 1)
                act.wait_ge(ln_ready, a + 1)
                nc.scalar.activation(norm[:], ln_n2[:], ACT.Exp, scale=0.5).then_inc(norm_ready, 1)

            def stack_copies(a):
                for s in (0, 2):
                    act.wait_ge(stack_t_ready, 4 * a + (s + 1 + STACK_CREDIT))
                    copy(qk_r[:, 2 * s:2 * s + 2].rearrange("p g n -> p (g n)"),
                         T0[0:STACK, :]).then_inc(qk_even_ready, 1)

            def k_features(a, u):
                cols = slice(u * CT, (u + 1) * CT)
                act.wait_ge(feat_ready, 8 * a + (u + 1))
                act.wait_ge(k_lo_done, 4 * a + (u + 1 - 4 + K_CREDIT))
                nc.scalar.activation(exp_k[:, cols], pG[:, u % 2], ACT.Exp, scale=NF ** -0.5).then_inc(exp_done, 1)
                act.wait_ge(exp_done, 8 * a + (u + 1 + EXP_CREDIT))
                act.wait_ge(kv_ready, a + KV_CREDIT)
                copy(k_hi[:, cols], exp_k[:, cols]).then_inc(k_hi_done, 1)

            def q_features(a, u):
                act.wait_ge(feat_ready, 8 * a + (4 + u + 1))
                act.wait_ge(q_lo_done, 4 * a + (u + 1 - 4 + QF_CREDIT))
                nc.scalar.activation(exp_q[:, u * CT:(u + 1) * CT], pG[:, u % 2], ACT.Exp,
                                     scale=NF ** -0.5).then_inc(exp_done, 1)

            def o_copy(a):
                act.wait_ge(o_ready, a + (1 + O_CREDIT))
                if not isinstance(a, int) or a > 0:
                    act.wait_ge(o_tr_ready, a)
                copy(o_sb[:], pC[:]).then_inc(o_copied, 1)

            def on_copy(a):
                act.wait_ge(on_tr_ready, a + 1)
                act.wait_ge(proj_ready, a + PROJ_CREDIT)
                copy(on_t[:], T1[:, 0:BT]).then_inc(on_copied, 1)

            def kv_copy(a):
                act.wait_ge(kv_ready, a + (1 + KV_CREDIT))
                act.wait_ge(kv_tr_ready, 2 * a + KV_TR_CREDIT)
                copy(kv_t[:], pU[:].rearrange("p b n -> p (b n)")).then_inc(kv_copied, 1)

            def row(a, late, front, xt):
                for u in range(4):
                    k_features(a, u)
                if late:
                    o_copy(a - 1)
                if front:
                    qkv_copy(a + 1)
                for u in range(4):
                    q_features(a, u)
                kv_copy(a)
                if late:
                    on_copy(a - 1)
                if front:
                    norms(a + 1)
                if xt:
                    x_t_copy(a + 2)
                if front:
                    stack_copies(a + 1)

            act.wait_ge(small_loaded, 16 * 3)
            act.wait_ge(const_step, GK_CONSTS)
            copy(gk_hi[:, 0:EXPERTS], gk_raw[:]).then_inc(small_hi_ready, 1)
            copy(sel_r[:], sel_raw[:]).then_inc(small_hi_ready, 1)
            x_hi_part(0, 0, 0)
            weight_hi(0)
            weight_hi(1)
            scores(0)
            weight_hi(2)
            x_hi_part(1, 1, 1)
            scores(1)
            combine_copy(0, 0)
            ffn(0, 0)

            act.wait_ge(rf_loaded, 16 * 13)
            copy(rf_r[:], rf_raw[:]).then_inc(rf_ready, 1)
            nc.scalar.preload_act_table_set("natural_log_exp_and_others")
            x_t_copy(0)
            qkv_copy(0)
            norms(0)
            x_t_copy(1)
            stack_copies(0)
            row(0, False, True, True)
            with act.Fori(1, ROWS - 2) as a:
                row(a, True, True, True)
            row(ROWS - 2, True, True, False)
            row(ROWS - 1, True, False, False)
            o_copy(ROWS - 1)
            on_copy(ROWS - 1)

            x_hi_part(CHUNKS, 0, LN_FFN2)
            scores(CHUNKS)
            x_hi_part(CHUNKS + 1, 1, LN_FFN2 + 1)
            scores(CHUNKS + 1)
            combine_copy(CHUNKS, 0)
            ffn(CHUNKS, LN_FFN2)

        @block.vector
        def _(dve):
            dve.sem_inc(s_used, S_CREDIT)
            dve.sem_inc(gated_done, Q_CREDIT)
            dve.sem_inc(k_lo_done, K_CREDIT)
            dve.sem_inc(n2_ready, N2_CREDIT)
            tt = nc.vector.tensor_tensor

            def ln_stats(p, x0, n):
                if not isinstance(p, int) or p > 0:
                    dve.wait_ge(xn_ready, p)
                for t in range(n):
                    last = nc.vector.bn_stats(stats[:, t, :], X[:, ds(x0 + t * H, H)])
                last.then_inc(bn_step, 1)
                dve.wait_ge(bn_step, p + 1)
                dve.sem_inc(bn_aggr_go, 1)
                for t in range(n):
                    last = nc.vector.bn_aggr(meanvar[:, t, :], stats[:, t, :])
                last.then_inc(mv_ready, 1)

            def ln_apply(p, x0, n):
                dve.wait_ge(rstd_ready, p + 1)
                dve.wait_ge(xt_ready, p + XT_CREDIT)
                for t in range(n):
                    last = nc.vector.tensor_scalar(xn[:, t * H:(t + 1) * H], X[:, ds(x0 + t * H, H)],
                                                   meanvar[:, t, 0:1], rstd[:, t:t + 1], ALU.subtract, ALU.mult)
                last.then_inc(xn_ready, 1)

            def x_lo_part(f, c):
                dve.wait_ge(xhi_ready, f + 1)
                cols = ds(c * CT, CT)
                tt(x_lo[:, cols], T1[:], x_hi[:, cols].bitcast(F32), ALU.subtract).then_inc(xlo_ready, 1)

            def weight_lo(k):
                dve.wait_ge(w_hi_ready, k + 1)
                cols = slice(k * BLOCKS * P, (k + 1) * BLOCKS * P)
                tt(w_lo[:, cols], w_stage[k], w_hi[:, cols].bitcast(F32), ALU.subtract).then_inc(w_lo_ready, 1)

            def per_tile(ap):
                return ap.unsqueeze(2).broadcast_to((P, TILES, EXPERTS))

            def route_scores(f):
                dve.wait_ge(scores_tok_ready, f + 1)
                if not isinstance(f, int) or f > 0:
                    dve.wait_ge(combine_ready, f)
                tt(sfc[:].rearrange("p (t e) -> p t e", t=TILES),
                   T1[:].rearrange("p (t e) -> p t e", t=TILES)[:, :, 0:EXPERTS],
                   gb_rows[:].unsqueeze(1).broadcast_to((P, TILES, EXPERTS)), ALU.add).then_inc(sfc_ready, 1)

            def route_pairs(f, steps):
                dve.wait_ge(sfc_ready, f + 1)
                s4 = sfc[:].rearrange("p (g e) -> p g e", e=EG)
                tt(pair_hi[:], s4[:, :, 0:2], s4[:, :, 2:4], ALU.max)
                steps.mark(tt(pair_lo[:], s4[:, :, 0:2], s4[:, :, 2:4], ALU.min))

            def route_best(f, steps):
                steps.wait()
                tt(g_top[:], pair_hi[:, :, 0], pair_hi[:, :, 1], ALU.max)
                tt(g_mid[:], pair_hi[:, :, 0], pair_hi[:, :, 1], ALU.min)
                steps.mark(tt(g_low[:], pair_lo[:, :, 0], pair_lo[:, :, 1], ALU.max))

            def route_second(f, steps):
                steps.wait()
                steps.mark(tt(g_mid[:], g_mid[:], g_low[:], ALU.max))

            def route_group_sum(f, steps):
                steps.wait()
                steps.mark(tt(g_sum[:].rearrange("p t g -> p (t g)"), g_top[:], g_mid[:], ALU.add))

            def route_compare(f, steps):
                steps.wait()
                other = g_sum[:].unsqueeze(2).broadcast_to((P, TILES, GROUPS, GROUPS))
                own = g_sum[:].unsqueeze(3).broadcast_to((P, TILES, GROUPS, GROUPS))
                tt(g_gt[:], other, own, ALU.is_gt)
                steps.mark(tt(g_eq[:], other, own, ALU.is_equal))

            def route_equal(f, steps):
                steps.wait()
                steps.mark(tt(g_eq[:], g_eq[:], g_before[:].unsqueeze(1).broadcast_to((P, TILES, GROUPS, GROUPS)),
                              ALU.mult))

            def route_before(f, steps):
                steps.wait()
                steps.mark(tt(g_gt[:], g_gt[:], g_eq[:], ALU.add))

            def route_rank(f, steps):
                steps.wait()
                steps.mark(nc.vector.tensor_reduce(g_rank[:], g_gt[:].rearrange("p t g o -> p (t g) o"), AX_X,
                                                   ALU.add))

            def route_masked(f, steps):
                steps.wait()
                steps.mark(nc.vector.scalar_tensor_tensor(
                    masked[:].rearrange("p t (g e) -> p (t g) e", e=EG),
                    g_rank[:].unsqueeze(2).broadcast_to((P, 16, EG)), 2.0,
                    sfc[:].rearrange("p (g e) -> p g e", e=EG), ALU.is_lt, ALU.mult))

            def route_top(f, steps):
                steps.wait()
                dve.sem_inc(max_go, 1)
                for t in range(TILES):
                    last = nc.vector.max(top8[:, t, :], masked[:, t, :])
                steps.mark(last)

            def route_above(f, steps):
                steps.wait()
                fourth = per_tile(top8[:, :, 3])
                tt(above[:], masked[:], fourth, ALU.is_gt)
                steps.mark(tt(tied[:].rearrange("p (t e) -> p t e", t=TILES), masked[:], fourth, ALU.is_equal))

            def route_count(f, steps):
                steps.wait()
                nc.vector.tensor_reduce(n_above[:], above[:], AX_X, ALU.add)
                steps.mark(nc.vector.tensor_tensor_scan(order[:], restart[:], tied[:], 0.0, ALU.mult, ALU.add))

            def route_order(f, steps):
                steps.wait()
                order3 = order[:].rearrange("p (t e) -> p t e", t=TILES)
                steps.mark(tt(order3, order3, per_tile(n_above[:]), ALU.add))

            def route_tied(f, steps):
                steps.wait()
                order3 = order[:].rearrange("p (t e) -> p t e", t=TILES)
                tied3 = tied[:].rearrange("p (t e) -> p t e", t=TILES)
                steps.mark(nc.vector.scalar_tensor_tensor(chosen[:], order3, 4.0, tied3, ALU.is_le, ALU.mult))

            def route_chosen(f, steps):
                steps.wait()
                steps.mark(tt(chosen[:], chosen[:], above[:], ALU.add))

            def route_kept(f, steps):
                steps.wait()
                steps.mark(tt(masked[:], masked[:], chosen[:], ALU.mult))

            def route_sum(f, steps):
                steps.wait()
                steps.mark(nc.vector.tensor_reduce(w_sum[:], masked[:], AX_X, ALU.add))

            def route_guard(f, steps):
                steps.wait()
                steps.mark(nc.vector.tensor_scalar(w_sum[:], w_sum[:], 1e-20, None, ALU.add))

            def route_inverse(f, steps):
                steps.wait()
                steps.mark(nc.vector.reciprocal(w_sum[:], w_sum[:]))

            def route_weights(f, steps):
                steps.wait()
                steps.mark(nc.vector.scalar_tensor_tensor(combine[:], masked[:], SCALE, per_tile(w_sum[:]),
                                                          ALU.mult, ALU.mult))

            def route_split(f, steps):
                assert steps.n == ROUTE_STEPS, steps.n
                steps.wait()
                if not isinstance(f, int) or f > 0:
                    dve.wait_ge(combine_tok_t, f)
                nc.vector.tensor_copy(combine_s[:, :, 0:EXPERTS], combine[:]).then_inc(combine_hi_ready, 1)
                dve.wait_ge(combine_hi_ready, f + 1)
                tt(combine_s[:, :, EXPERTS:2 * EXPERTS], combine[:], combine_s[:, :, 0:EXPERTS].bitcast(F32),
                   ALU.subtract).then_inc(combine_ready, 1)

            def ffn(f0, ln0):
                def add_y(f, c):
                    dve.wait_ge(yt_ready, f + (1 + YT_CREDIT))
                    xs = X[:, ds(c * CT, CT)]
                    nc.vector.scalar_tensor_tensor(xs, T0[:], 0.5, xs, ALU.mult, ALU.add).then_inc(ffn_x_done, 1)

                def chunk(c, prev, nxt, nxt2):
                    f = c + f0
                    n0, m0 = f * BLOCKS, f * PAIRS
                    steps = Steps(dve, route_step, (f + 1) * ROUTE_STEPS)
                    for j in range(BLOCKS):
                        if j < PAIRS:
                            dve.wait_ge(silu_done, n0 + (j + 1 + SILU_CREDIT))
                            dve.wait_ge(c_ready, m0 + (j + 1))
                            dve.wait_ge(gated_done, n0 + (j + 1 - 2 + Q_CREDIT))
                            tt(weighted[:, j % 2], pC[:], silu_g[:, j % 4], ALU.mult).then_inc(s_used, 1)
                        if nxt:
                            if j == 0:
                                route_scores(f + 1)
                            if j == 1:
                                route_best(f + 1, steps)
                            if j == 2:
                                route_group_sum(f + 1, steps)
                            if j == 3:
                                route_equal(f + 1, steps)
                            if j == 4:
                                route_masked(f + 1, steps)
                            if j == 5:
                                route_above(f + 1, steps)
                            if j == 6:
                                route_order(f + 1, steps)
                                route_tied(f + 1, steps)
                            if j == 7:
                                route_sum(f + 1, steps)
                                route_guard(f + 1, steps)
                        if j == 2 and nxt2:
                            if f0 == 0:
                                dve.wait_ge(x_loaded, c * 16 + 48)
                            ln_stats(c + (2 + ln0), (c + 2) * CT, TILES)
                        if j < PAIRS:
                            dve.wait_ge(s_used, m0 + (j + 1 + S_CREDIT))
                            factor = weighted[:, j % 2]
                        else:
                            dve.wait_ge(silu_done, n0 + (j + 1 + SILU_CREDIT))
                            factor = silu_s[:]
                        dve.wait_ge(u_ready, n0 + (j + 1))
                        dve.wait_ge(gated_lo_done, n0 + (j + 1 - 3 + QL_CREDIT))
                        tt(gated[:, j % 3], pU[:, j % 2], factor, ALU.mult).then_inc(gated_done, 1)
                        if nxt:
                            if j == 0:
                                route_pairs(f + 1, steps)
                            if j == 1:
                                route_second(f + 1, steps)
                            if j == 2:
                                route_compare(f + 1, steps)
                            if j == 3:
                                route_before(f + 1, steps)
                                route_rank(f + 1, steps)
                            if j == 4:
                                route_top(f + 1, steps)
                            if j == 5:
                                route_count(f + 1, steps)
                            if j == 6:
                                route_chosen(f + 1, steps)
                                route_kept(f + 1, steps)
                            if j == 7:
                                route_inverse(f + 1, steps)
                                route_weights(f + 1, steps)
                                route_split(f + 1, steps)
                        if j == 4 and nxt2:
                            ln_apply(c + (2 + ln0), (c + 2) * CT, TILES)
                        if j == 5 and prev:
                            add_y(f - 1, c - 1)
                        if j == 6 and nxt2:
                            x_lo_part(f + 2, c + 2)

                chunk(0, False, True, True)
                with dve.Fori(1, CHUNKS - 2) as c:
                    chunk(c, True, True, True)
                chunk(CHUNKS - 2, True, True, False)
                chunk(CHUNKS - 1, True, False, False)
                add_y(f0 + CHUNKS - 1, CHUNKS - 1)

            def route(f):
                steps = Steps(dve, route_step, f * ROUTE_STEPS)
                for stage in (route_pairs, route_best, route_second, route_group_sum, route_compare, route_equal,
                              route_before, route_rank, route_masked, route_top, route_above, route_count, route_order, route_tied,
                              route_chosen, route_kept, route_sum, route_guard, route_inverse,
                              route_weights, route_split):
                    stage(f, steps)

            def att_stats(a):
                ln_stats(a + LN_ATT, a * BT, 2)

            def stack_parts(a):
                dve.wait_ge(qkv_copied, 2 * a + 2)
                dve.wait_ge(stack_t_ready, 4 * a + STACK_CREDIT)
                s4 = stack[:].rearrange("p (t g) s -> p t g s", t=2)
                qk = qkv[:, :, 0:2 * H].rearrange("p t (g d) -> p t g d", g=2 * QG)
                nc.vector.tensor_copy(s4[:, :, :, 0:32], qk).then_inc(stack_ready, 1)
                dve.wait_ge(stack_ready, 2 * a + 1)
                tt(s4[:, :, :, 32:64], qk, s4[:, :, :, 0:32].bitcast(F32), ALU.subtract).then_inc(stack_ready, 1)

            def v_parts(a, steps):
                dve.wait_ge(kv_ready, a + KV_CREDIT)
                for t in range(2):
                    v = qkv[:, t, 2 * H:3 * H].rearrange("p (g k d) -> p g k d", g=QG, k=HG)
                    part = v_r[:, t].rearrange("p g (l k s) -> p l g k s", l=2, s=SLOT)
                    steps.link(nc.vector.tensor_copy(part[:, 0, :, :, 0:HD], v))
                    last = tt(part[:, 1, :, :, 0:HD], v, part[:, 0, :, :, 0:HD].bitcast(F32), ALU.subtract)
                last.then_inc(v_ready, 1)

            def squared_norms(a, steps):
                dve.wait_ge(squares_ready, a + 1)
                if not isinstance(a, int) or a > 0:
                    dve.wait_ge(ln_ready, a)
                steps.link(nc.vector.tensor_reduce(
                    n2[:].rearrange("p (t h) -> p t h", t=2),
                    squares[:].rearrange("p t (h d) -> p t h d", d=HD), AX_X, ALU.add))
                nc.vector.tensor_scalar(n2[:], n2[:], NORM2_LEAST, None, ALU.max).then_inc(n2_ready, 1)

            def norm_parts(a):
                dve.wait_ge(norm_ready, a + 1)
                nrm = norm[:].rearrange("p (t k) -> p t k", k=HG)
                nc.vector.tensor_copy(stack[:, :, 96:100], nrm).then_inc(norm_split, 1)
                dve.wait_ge(norm_split, 2 * a + 1)
                tt(stack[:, :, 100:104], nrm, stack[:, :, 96:100].bitcast(F32), ALU.subtract).then_inc(norm_split, 1)

            def stack_copies(a):
                for s in (1, 3):
                    dve.wait_ge(stack_t_ready, 4 * a + (s + 1 + STACK_CREDIT))
                    nc.vector.tensor_copy(qk_r[:, 2 * s:2 * s + 2].rearrange("p g n -> p (g n)"),
                                          T1[0:STACK, :]).then_inc(qk_odd_ready, 1)

            def k_lo_part(a, u):
                cols = slice(u * CT, (u + 1) * CT)
                dve.wait_ge(k_hi_done, 4 * a + (u + 1))
                tt(k_lo[:, cols], exp_k[:, cols], k_hi[:, cols].bitcast(F32), ALU.subtract).then_inc(k_lo_done, 1)

            def divide(a, steps):
                dve.wait_ge(o_tr_ready, a + 1)
                slots = T0[:].rearrange("p (h s) -> p h s", s=SLOT)
                steps.link(nc.vector.tensor_scalar(den[:], slots[:, :, HD], 1e-6, None, ALU.add))
                steps.link(nc.vector.reciprocal(rden[:], den[:]))
                if not isinstance(a, int) or a > 0:
                    dve.wait_ge(on_tr_ready, a)
                tt(on[:].rearrange("p (h d) -> p h d", d=HD), slots[:, :, 0:HD],
                   rden[:].unsqueeze(2).broadcast_to((P, 2 * HEADS, HD)), ALU.mult).then_inc(on_ready, 1)

            def add_projection(a):
                dve.wait_ge(proj_ready, a + (1 + PROJ_CREDIT))
                xs = X[:, ds(a * BT, BT)]
                tt(xs, T0[:, 0:BT], xs, ALU.add).then_inc(att_x_added, 1)

            def kv_parts(a, steps):
                for jh, bank in enumerate((T0, T1)):
                    dve.wait_ge(kv_tr_ready, 2 * a + (jh + 1 + KV_TR_CREDIT))
                    rows = bank[:].rearrange("p (g r w) -> p g r w", g=2, r=2)
                    for r in range(2):
                        w = 2 * SLOT * r
                        own = slice(r, 4, 2)
                        last = nc.vector.tensor_copy(kv_tmp[:, jh, own, :], rows[:, :, r, M + w:M + w + 2 * SLOT])
                    steps.link(last)
                    for r in range(2):
                        w = 2 * SLOT * r
                        own = slice(r, 4, 2)
                        last = tt(kv_sum[:, jh, own, :], rows[:, :, r, w:w + 2 * SLOT], kv_tmp[:, jh, own, :], ALU.add)
                    last.then_inc(kv_tr_read, 1)
                dve.wait_ge(kv_tr_read, 2 * a + 2)
                flat = "p j k s -> p (j k) s"
                mask = head_mask[:].unsqueeze(1).broadcast_to((P, 8, 2 * SLOT))
                steps.link(tt(kv_own[:].rearrange(flat), kv_sum[:].rearrange(flat), mask, ALU.mult))
                dve.wait_ge(o_ready, a + O_CREDIT)
                hi = kv_hi[:].rearrange("p j (k s) -> p j k s", s=DIAG)[:, :, :, 0:2 * SLOT]
                lo = kv_lo[:].rearrange("p j (k s) -> p j k s", s=DIAG)[:, :, :, 0:2 * SLOT]
                steps.link(nc.vector.tensor_copy(hi, kv_own[:]))
                tt(lo, kv_own[:], hi.bitcast(F32), ALU.subtract).then_inc(kv_split, 1)

            def front_steps(a, steps):
                stack_parts(a)
                v_parts(a, steps)

            def row(a, late, front, ln):
                steps = Steps(dve, att_step, a * ROW_STEPS + (FRONT_STEPS - DIVIDE_STEPS) if late else FRONT_STEPS)
                k_lo_part(a, 0)
                k_lo_part(a, 1)
                if ln:
                    att_stats(a + 2)
                k_lo_part(a, 2)
                k_lo_part(a, 3)
                if ln:
                    ln_apply(a + (2 + LN_ATT), (a + 2) * BT, 2)
                if late:
                    divide(a - 1, steps)
                if front:
                    front_steps(a + 1, steps)
                    squared_norms(a + 1, steps)
                if late:
                    add_projection(a - 1)
                if front:
                    norm_parts(a + 1)
                    stack_copies(a + 1)
                kv_parts(a, steps)
                assert steps.n == (DIVIDE_STEPS if late else 0) + (FRONT_STEPS if front else 0) + KV_STEPS, steps.n

            dve.wait_ge(x_loaded, 16)
            ln_stats(0, 0, TILES)
            ln_apply(0, 0, TILES)
            dve.wait_ge(small_hi_ready, 2)
            tt(gk_lo[:, 0:EXPERTS], gk_raw[:], gk_hi[:, 0:EXPERTS].bitcast(F32), ALU.subtract).then_inc(small_lo_ready, 1)
            x_lo_part(0, 0)
            weight_lo(0)
            weight_lo(1)
            dve.wait_ge(const_step, ROUTE_CONSTS)
            route_scores(0)
            dve.wait_ge(x_loaded, 32)
            ln_stats(1, CT, TILES)
            ln_apply(1, CT, TILES)
            route(0)
            x_lo_part(1, 1)
            weight_lo(2)
            ffn(0, 0)

            dve.wait_ge(const_step, ALL_CONSTS)
            dve.wait_ge(ffn_x_done, CHUNKS)
            att_stats(0)
            ln_apply(LN_ATT, 0, 2)
            dve.wait_ge(rf_ready, 1)
            tt(rf_r[64:96, :], rf_raw[64:96, :], rf_r[64:96, :].bitcast(F32), ALU.subtract).then_inc(rf_ready, 1)
            prologue = Steps(dve, att_step, 0)
            att_stats(1)
            front_steps(0, prologue)
            squared_norms(0, prologue)
            assert prologue.n == FRONT_STEPS, prologue.n
            ln_apply(LN_ATT + 1, BT, 2)
            norm_parts(0)
            stack_copies(0)
            row(0, False, True, True)
            with dve.Fori(1, ROWS - 2) as a:
                row(a, True, True, True)
            row(ROWS - 2, True, True, False)
            row(ROWS - 1, True, False, False)
            divide(ROWS - 1, Steps(dve, att_step, ROWS * ROW_STEPS - DIVIDE_STEPS))
            add_projection(ROWS - 1)

            dve.wait_ge(att_x_done, ROWS)
            ln_stats(LN_FFN2, 0, TILES)
            ln_apply(LN_FFN2, 0, TILES)
            x_lo_part(CHUNKS, 0)
            ln_stats(LN_FFN2 + 1, CT, TILES)
            route_scores(CHUNKS)
            ln_apply(LN_FFN2 + 1, CT, TILES)
            route(CHUNKS)
            x_lo_part(CHUNKS + 1, 1)
            ffn(CHUNKS, LN_FFN2)

        @block.tensor
        def _(pe):
            pe.sem_inc(down_done, D_CREDIT)
            pe.sem_inc(yt_ready, YT_CREDIT)
            pe.sem_inc(xt_ready, XT_CREDIT)
            pe.sem_inc(stack_t_ready, STACK_CREDIT)
            pe.sem_inc(kv_ready, KV_CREDIT)
            pe.sem_inc(kv_tr_ready, KV_TR_CREDIT)
            pe.sem_inc(o_ready, O_CREDIT)
            pe.sem_inc(proj_ready, PROJ_CREDIT)

            def three_passes(o, w_h, w_l, x_h, x_l, start=True, stop=True):
                nc.tensor.matmul(o, w_h, x_h, start=start, stop=False)
                nc.tensor.matmul(o, w_h, x_l, start=False, stop=False)
                return nc.tensor.matmul(o, w_l, x_h, start=False, stop=stop)

            def transpose_x(p, bank, n):
                pe.wait_ge(xn_ready, p + 1)
                for t in range(n):
                    last = nc.tensor.transpose(bank[:, t * P:(t + 1) * P], xn[:, t * H:(t + 1) * H], ident[:])
                last.then_inc(xt_ready, 1)

            def logits(f, c):
                pe.wait_ge(xlo_ready, f + 1)
                cols = ds(c * CT, CT)
                three_passes(T1[:], gk_hi[:], gk_lo[:], x_hi[:, cols], x_lo[:, cols]).then_inc(logits_ready, 1)

            def scores_to_tokens(f):
                pe.wait_ge(scores_ready, f + 1)
                for t in range(TILES):
                    last = nc.tensor.transpose(T1[:, t * P:(t + 1) * P], scores_t[:, t * P:(t + 1) * P], ident[:])
                last.then_inc(scores_tok_ready, 1)

            def transpose_combine(f):
                pe.wait_ge(combine_ready, f + 1)
                for t in range(TILES):
                    last = nc.tensor.transpose(T0[:, t * P:(t + 1) * P], combine_s[:, t, :].bitcast(F32), ident[:])
                last.then_inc(combine_tok_t, 1)

            def ffn(f0, ln0):
                def down(n, j):
                    pe.wait_ge(gated_lo_done, n + (1 + QL_CREDIT))
                    return three_passes(pY[:], w_block(w_hi, 2, j), w_block(w_lo, 2, j), gated_hi[:, j % 3],
                                        gated_lo[:, j % 3], start=(j == 0), stop=(j == BLOCKS - 1)
                                        ).then_inc(down_done, 1)

                def transpose_y(f):
                    pe.wait_ge(y_done, f + (1 + Y_CREDIT))
                    for t in range(TILES):
                        last = nc.tensor.transpose(T0[:, t * P:(t + 1) * P], y_sb[:, t * P:(t + 1) * P], ident[:])
                    last.then_inc(yt_ready, 1)

                def chunk(c, prev, nxt, nxt2):
                    f = c + f0
                    n0, m0 = f * BLOCKS, f * PAIRS
                    cols = ds(c * CT, CT)
                    first = isinstance(f, int) and f == 0
                    for j in range(BLOCKS):
                        if first and j == 0:
                            pe.wait_ge(w_lo_ready, 2)
                        pe.wait_ge(silu_done, n0 + ((j if j == 0 else j - 1) + SILU_CREDIT))
                        three_passes(pG[:, j % 2], w_block(w_hi, 0, j), w_block(w_lo, 0, j), x_hi[:, cols],
                                     x_lo[:, cols]).then_inc(g_ready, 1)
                        pe.wait_ge(gated_done, n0 + ((j if j == 0 else j - 1) + Q_CREDIT))
                        three_passes(pU[:, j % 2], w_block(w_hi, 1, j), w_block(w_lo, 1, j), x_hi[:, cols],
                                     x_lo[:, cols]).then_inc(u_ready, 1)
                        if j < PAIRS:
                            if j == 0:
                                pe.wait_ge(combine_t_ready, f + 1)
                            pe.wait_ge(s_used, m0 + (j + S_CREDIT))
                            nc.tensor.matmul(pC[:], sel_r[:, j * P:(j + 1) * P], combine_t[:, cols], start=True,
                                             stop=True).then_inc(c_ready, 1)
                        if first and j == 3:
                            pe.wait_ge(w_lo_ready, 3)
                        if j == 3:
                            pe.wait_ge(y_done, f + Y_CREDIT)
                        if j >= 3:
                            down(n0 + (j - 3), j - 3)
                        elif prev:
                            down(n0 + (j - 3), j + BLOCKS - 3)
                        if j == 0 and nxt:
                            scores_to_tokens(f + 1)
                        if j == 4 and prev:
                            transpose_y(f - 1)
                        if j == 5 and nxt2:
                            pe.wait_ge(sfc_ready, f + 2)
                            transpose_x(c + (2 + ln0), T1, TILES)
                        if j == 7 and nxt2:
                            logits(f + 2, c + 2)
                        if j == 8 and nxt:
                            if prev:
                                pe.wait_ge(ffn_x_done, f)
                            transpose_combine(f + 1)

                chunk(0, False, True, True)
                with pe.Fori(1, CHUNKS - 2) as c:
                    chunk(c, True, True, True)
                chunk(CHUNKS - 2, True, True, False)
                chunk(CHUNKS - 1, True, False, False)
                for j in range(BLOCKS - 3, BLOCKS):
                    down((f0 + CHUNKS - 1) * BLOCKS + j, j)
                pe.wait_ge(ffn_x_done, f0 + CHUNKS - 1)
                transpose_y(f0 + CHUNKS - 1)

            def qkv_product(a, t):
                bank = (T0, T1)[t]
                if t == 0:
                    pe.wait_ge(xta_ready, a + 1)
                    if not isinstance(a, int) or a > 1:
                        pe.wait_ge(kv_tr_read, 2 * a - 3)
                elif not isinstance(a, int) or a > 1:
                    pe.wait_ge(kv_tr_read, 2 * a - 2)
                nc.tensor.matmul(bank[:, 0:3 * H], x_t[:, t * P:(t + 1) * P], wqkv_sb[:], start=True,
                                 stop=True).then_inc(qkv_ready, 1)

            def transpose_stack(a):
                pe.wait_ge(stack_ready, 2 * a + 2)
                pe.wait_ge(stack_dup_ready, a + 1)
                pe.wait_ge(norm_split, 2 * a + 2)
                for s in range(4):
                    bank = (T0, T1)[s % 2]
                    if s == 2:
                        pe.wait_ge(qk_even_ready, 2 * a + 1)
                    if s == 3:
                        pe.wait_ge(qk_odd_ready, 2 * a + 1)
                    for i in range(2):
                        for t in range(2):
                            last = nc.tensor.transpose(bank[0:STACK, i * BT + t * P:i * BT + (t + 1) * P],
                                                       stack[:, 2 * QG * t + 2 * s + i, :].bitcast(F32), ident[:])
                    last.then_inc(stack_t_ready, 1)

            def k_unit(a, u):
                t, half = u // 2, u % 2
                pe.wait_ge(exp_done, 8 * a + (u + 1 - 2 + EXP_CREDIT))
                for i in range(2):
                    last = nc.tensor.matmul(pG[:, u % 2, i * BT:(i + 1) * BT],
                                            qk_r[:, QG + 2 * half + i, t * P:(t + 1) * P], rf_r[:],
                                            start=True, stop=True)
                last.then_inc(feat_ready, 1)

            def q_unit(a, u):
                pe.wait_ge(exp_done, 8 * a + (4 + u + 1 - 2 + EXP_CREDIT))
                for i in range(2):
                    last = nc.tensor.matmul(pG[:, u % 2, i * BT:(i + 1) * BT], rf_r[:, i * P:(i + 1) * P],
                                            qk_r[:, u, :], start=True, stop=True)
                last.then_inc(feat_ready, 1)

            def kv_product(a):
                pe.wait_ge(v_ready, a + 1)
                pe.wait_ge(k_lo_done, 4 * a + (4 + K_CREDIT))
                pe.wait_ge(kv_copied, a + KV_COPY_CREDIT)
                for g in range(QG):
                    o = pU[:, g // 2, (g % 2) * BT:(g % 2 + 1) * BT]
                    for n, (t, k) in enumerate([(0, k_hi), (0, k_lo), (1, k_hi), (1, k_lo)]):
                        col = t * HEADS * NF + g * BT
                        last = nc.tensor.matmul(o, v_r[:, t, g, :], k[:, col:col + BT], start=(n == 0), stop=(n == 3))
                last.then_inc(kv_ready, 1)

            def transpose_kv(a):
                pe.wait_ge(kv_copied, a + (1 + KV_COPY_CREDIT))
                for jh, bank in enumerate((T0, T1)):
                    for k in range(4):
                        j = 4 * jh + k
                        last = nc.tensor.transpose(bank[:, k * P:(k + 1) * P], kv_t[:, j * P:(j + 1) * P], ident[:])
                    last.then_inc(kv_tr_ready, 1)

            def o_product(a, jh):
                if jh == 0:
                    pe.wait_ge(kv_split, a + 1)
                    pe.wait_ge(o_copied, a + O_COPY_CREDIT)
                    pe.wait_ge(q_lo_done, 4 * a + (2 + QF_CREDIT))
                else:
                    pe.wait_ge(q_lo_done, 4 * a + (4 + QF_CREDIT))
                for k in range(4):
                    q = slice((4 * jh + k) * BT, (4 * jh + k + 1) * BT)
                    w = slice(k * P, (k + 1) * P)
                    last = three_passes(pC[:, jh * BT:(jh + 1) * BT], kv_hi[:, jh, w], kv_lo[:, jh, w], q_hi[:, q],
                                        q_lo[:, q], start=(k == 0), stop=(k == 3))
                if jh == 1:
                    last.then_inc(o_ready, 1)

            def transpose_o(a):
                pe.wait_ge(o_copied, a + (1 + O_COPY_CREDIT))
                for t in range(2):
                    for jh in range(2):
                        c = (2 * t + jh) * P
                        last = nc.tensor.transpose(T0[:, c:c + P], o_sb[:, jh * BT + t * P:jh * BT + (t + 1) * P],
                                                   ident[:])
                last.then_inc(o_tr_ready, 1)

            def transpose_on(a):
                pe.wait_ge(on_ready, a + 1)
                for t in range(2):
                    last = nc.tensor.transpose(T1[:, t * P:(t + 1) * P], on[:, t * P:(t + 1) * P], ident[:])
                last.then_inc(on_tr_ready, 1)

            def projection(a):
                pe.wait_ge(on_copied, a + 1)
                for t in range(2):
                    last = nc.tensor.matmul(T0[:, t * P:(t + 1) * P], on_t[:, t * P:(t + 1) * P], wout_sb[:],
                                            start=True, stop=True)
                last.then_inc(proj_ready, 1)

            def row(a, late, front, xt):
                pe.wait_ge(qk_even_ready, 2 * a + 2)
                pe.wait_ge(qk_odd_ready, 2 * a + 2)
                k_unit(a, 0)
                k_unit(a, 1)
                if late:
                    o_product(a - 1, 0)
                k_unit(a, 2)
                k_unit(a, 3)
                if late:
                    o_product(a - 1, 1)
                if front:
                    qkv_product(a + 1, 0)
                    qkv_product(a + 1, 1)
                q_unit(a, 0)
                q_unit(a, 1)
                if late:
                    if front:
                        pe.wait_ge(qkv_copied, 2 * a + 3)
                    else:
                        pe.wait_ge(kv_tr_read, 2 * a - 1)
                    transpose_o(a - 1)
                q_unit(a, 2)
                kv_product(a)
                q_unit(a, 3)
                if late:
                    if front:
                        pe.wait_ge(qkv_copied, 2 * a + 4)
                    else:
                        pe.wait_ge(kv_tr_read, 2 * a)
                    transpose_on(a - 1)
                    projection(a - 1)
                if xt:
                    if not late:
                        pe.wait_ge(qkv_copied, 2 * a + 4)
                    transpose_x(a + (2 + LN_ATT), T1, 2)
                if front:
                    if late:
                        pe.wait_ge(att_x_added, a)
                        pe.wait_ge(on_copied, a)
                    if xt:
                        pe.wait_ge(xta_ready, a + 3)
                    transpose_stack(a + 1)
                    pe.wait_ge(qk_even_ready, 2 * a + 4)
                    pe.wait_ge(qk_odd_ready, 2 * a + 4)
                else:
                    pe.wait_ge(att_x_added, a)
                    pe.wait_ge(on_copied, a)
                transpose_kv(a)

            pe.wait_ge(const_step, GK_CONSTS)
            transpose_x(0, T1, TILES)
            pe.wait_ge(small_lo_ready, 1)
            logits(0, 0)
            scores_to_tokens(0)
            pe.wait_ge(sfc_ready, 1)
            transpose_x(1, T1, TILES)
            logits(1, 1)
            transpose_combine(0)
            ffn(0, 0)

            pe.wait_ge(small_loaded, 16 * 6)
            pe.wait_ge(silu_done, CHUNKS * BLOCKS + SILU_CREDIT)
            pe.wait_ge(gated_done, CHUNKS * BLOCKS + Q_CREDIT)
            pe.wait_ge(sfc_ready, CHUNKS)
            pe.wait_ge(ffn_x_done, CHUNKS)
            transpose_x(LN_ATT, T1, 2)
            qkv_product(0, 0)
            qkv_product(0, 1)
            pe.wait_ge(qkv_copied, 2)
            transpose_x(LN_ATT + 1, T1, 2)
            pe.wait_ge(xta_ready, 2)
            transpose_stack(0)
            pe.wait_ge(rf_ready, 2)
            row(0, False, True, True)
            with pe.Fori(1, ROWS - 2) as a:
                row(a, True, True, True)
            row(ROWS - 2, True, True, False)
            row(ROWS - 1, True, False, False)
            o_product(ROWS - 1, 0)
            o_product(ROWS - 1, 1)
            pe.wait_ge(kv_tr_read, 2 * ROWS)
            transpose_o(ROWS - 1)
            transpose_on(ROWS - 1)
            projection(ROWS - 1)

            pe.wait_ge(att_x_added, ROWS)
            pe.wait_ge(exp_done, 8 * ROWS + EXP_CREDIT)
            transpose_x(LN_FFN2, T1, TILES)
            logits(CHUNKS, 0)
            scores_to_tokens(CHUNKS)
            pe.wait_ge(sfc_ready, CHUNKS + 1)
            transpose_x(LN_FFN2 + 1, T1, TILES)
            logits(CHUNKS + 1, 1)
            transpose_combine(CHUNKS)
            ffn(CHUNKS, LN_FFN2)


def kernel(**inputs):
    import numpy as np
    import concourse.bacc as bacc
    from concourse.bass_utils import run_bass_kernel_spmd

    i = {name: np.asarray(a) for name, a in inputs.items()}
    shape = i["L0_attn_x"].shape

    def up(name, shared):
        w = i[name].transpose(1, 0, 2).reshape(H, EXPERTS * M)
        return np.concatenate([w, i[shared]], axis=1)

    down = i["L0_ffn_w_down"].reshape(PAIRS, P, H).transpose(1, 0, 2).reshape(P, PAIRS * H)
    down = np.concatenate([down, i["L0_ffn_sw_down"]], axis=1)
    wall = np.concatenate([up("L0_ffn_w_gate", "L0_ffn_sw_gate"), up("L0_ffn_w_up", "L0_ffn_sw_up"), down], axis=1)

    pair_sel = np.zeros((P, PAIRS * P), np.float32)
    for e in range(EXPERTS):
        pair_sel[[e, EXPERTS + e], e * M:(e + 1) * M] = 1.0
    norm_sel = np.zeros((2 * HG, HG * NF), np.float32)
    for h in range(HG):
        norm_sel[[h, HG + h], h * NF:(h + 1) * NF] = -float(NF) ** 0.5

    arrays = {
        "x": i["L0_attn_x"].reshape(TOKENS, H),
        "wall": wall,
        "gate_k": i["L0_ffn_gate_kernel"],
        "gate_b": i["L0_ffn_gate_bias"],
        "wqkv": i["L0_attn_w_qkv"].T,
        "wout": i["L0_attn_w_out"].T,
        "b_out": i["L0_attn_b_out"],
        "rft": i["L0_attn_random_features"].T,
        "pair_sel": pair_sel,
        "norm_sel": norm_sel,
    }
    arrays = {name + "_dram": np.ascontiguousarray(a) for name, a in arrays.items()}
    nc = bacc.Bacc("TRN2", target_bir_lowering=False, num_devices=1)
    args = [nc.dram_tensor(name, a.shape, mybir.dt.from_np(a.dtype), kind="ExternalInput").ap()
            for name, a in arrays.items()]
    args.append(nc.dram_tensor("out_dram", (TOKENS, H), F32, kind="ExternalOutput").ap())
    macaron_kernel(nc, *args)
    r = run_bass_kernel_spmd(nc, [arrays], core_ids=[0])
    return r.results[0]["out_dram"].reshape(shape)
```

```python
from contextlib import ExitStack

import concourse.bass as bass
from concourse import mybir

F32 = mybir.dt.float32
F32R = mybir.dt.float32r
ALU = mybir.AluOpType
ACT = mybir.ActivationFunctionType
AX_X = mybir.AxisListType.X
ds = bass.ds

P = 128
H = 128
TOKENS = 4096
TILES = 4
CT = TILES * P
CHUNKS = TOKENS // CT
EXPERTS = 16
GROUPS = 4
EG = EXPERTS // GROUPS
M = 64
PAIRS = EXPERTS * M // P
BLOCKS = PAIRS + 1
SCALE = 2.5
LN_EPS = 1e-5
HEADS = 16
HD = H // HEADS
NF = 64
HG = 4
QG = HEADS // HG
STACK = 3 * HG * HD + 2 * HG
SLOT = 16
BT = 2 * P
ROWS = TOKENS // BT
DIAG = P + 2 * SLOT
LN_ATT = CHUNKS
LN_FFN2 = CHUNKS + ROWS

SILU_CREDIT = 2
S_CREDIT = 4
Q_CREDIT = 9
QL_CREDIT = 3
D_CREDIT = 3
Y_CREDIT = 1
YT_CREDIT = 1
XT_CREDIT = 1
EXP_CREDIT = 2
K_CREDIT = 4
QF_CREDIT = 4
KV_CREDIT = 1
KV_COPY_CREDIT = 1
KV_TR_CREDIT = 2
O_CREDIT = 2
O_COPY_CREDIT = 1
PROJ_CREDIT = 1
STACK_CREDIT = 4
N2_CREDIT = 1

ROUTE_STEPS = 20
DIVIDE_STEPS = 2
V_STEPS = 2
KV_STEPS = 4
GK_CONSTS = 6
ROUTE_CONSTS = GK_CONSTS + 1 + (GROUPS - 1) + 3
ALL_CONSTS = ROUTE_CONSTS + 7
NORM2_LEAST = 2.0 ** -60


def macaron_kernel(nc, x, wall, gate_k, gate_b, wqkv, wout, b_out, rft, pair_sel, norm_sel, out):
    x_v = x.rearrange("(c b p i) h -> c p b (i h)", c=CHUNKS, b=2, i=2)
    out_v = out.rearrange("(c b p i) h -> c p b (i h)", c=CHUNKS, b=2, i=2)

    with ExitStack() as ctx:
        def sb(name, shape, dt=F32):
            return ctx.enter_context(nc.sbuf_tensor(name, shape, dt))

        def psum(name, shape):
            return ctx.enter_context(nc.psum_tensor(name, shape, F32))

        def sem(name):
            return ctx.enter_context(nc.semaphore(name))

        X = sb("X", [P, CHUNKS * TILES * H])
        ident = sb("ident", [P, P])
        xn = sb("xn", [P, TILES * H])
        stats = sb("stats", [P, TILES, 6])
        meanvar = sb("meanvar", [P, TILES, 2])
        vareps = sb("vareps", [P, TILES])
        rstd = sb("rstd", [P, TILES])
        minus_half = sb("minus_half", [P, TILES])

        w_hi = sb("w_hi", [P, 3 * BLOCKS * P], F32R)
        w_lo = sb("w_lo", [P, 3 * BLOCKS * P], F32R)
        gk_hi = sb("gk_hi", [P, P], F32R)
        gk_lo = sb("gk_lo", [P, P], F32R)
        gk_raw = sb("gk_raw", [P, EXPERTS])
        gb_rows = sb("gb_rows", [P, EXPERTS])
        sel_r = sb("sel_r", [P, PAIRS * P], F32R)
        x_hi = sb("x_hi", [P, CHUNKS * CT], F32R)
        x_lo = sb("x_lo", [P, CHUNKS * CT], F32R)
        combine_t = sb("combine_t", [P, CHUNKS * CT], F32R)
        y_sb = sb("y_sb", [P, CT])
        scores_t = sb("scores_t", [P, CT])
        silu_g = sb("silu_g", [P, 4, CT])
        silu_s = sb("silu_s", [P, CT])
        weighted = sb("weighted", [P, 2, CT])
        gated = sb("gated", [P, 3, CT])
        gated_hi = sb("gated_hi", [P, 3, CT], F32R)
        gated_lo = sb("gated_lo", [P, 3, CT], F32R)

        sfc = sb("sfc", [P, TILES * EXPERTS])
        pair_hi = sb("pair_hi", [P, 16, 2])
        pair_lo = sb("pair_lo", [P, 16, 2])
        g_top = sb("g_top", [P, 16])
        g_mid = sb("g_mid", [P, 16])
        g_low = sb("g_low", [P, 16])
        g_sum = sb("g_sum", [P, TILES, GROUPS])
        g_gt = sb("g_gt", [P, TILES, GROUPS, GROUPS])
        g_eq = sb("g_eq", [P, TILES, GROUPS, GROUPS])
        g_before = sb("g_before", [P, GROUPS, GROUPS])
        g_rank = sb("g_rank", [P, 16])
        masked = sb("masked", [P, TILES, EXPERTS])
        top8 = sb("top8", [P, TILES, 8])
        above = sb("above", [P, TILES, EXPERTS])
        tied = sb("tied", [P, TILES * EXPERTS])
        n_above = sb("n_above", [P, TILES])
        restart = sb("restart", [P, TILES * EXPERTS])
        order = sb("order", [P, TILES * EXPERTS])
        chosen = sb("chosen", [P, TILES, EXPERTS])
        w_sum = sb("w_sum", [P, TILES])
        combine = sb("combine", [P, TILES, EXPERTS])
        combine_s = sb("combine_s", [P, TILES, P], F32R)

        wqkv_sb = sb("wqkv_sb", [P, 3 * H])
        wout_sb = sb("wout_sb", [P, H])
        bout_rows = sb("bout_rows", [P, H])
        rf_raw = sb("rf_raw", [STACK, HG * NF])
        rf_r = sb("rf_r", [STACK, HG * NF], F32R)
        x_t = sb("x_t", [P, BT])
        qkv = sb("qkv", [P, 2, 3 * H])
        squares = sb("squares", [P, 2, 2 * H])
        n2 = sb("n2", [P, 2 * 2 * HEADS])
        norm2_least = sb("norm2_least", [P, 1])
        ln_n2 = sb("ln_n2", [P, 2 * 2 * HEADS])
        norm = sb("norm", [P, 2 * 2 * HEADS])
        stack = sb("stack", [P, 2 * 2 * QG, STACK], F32R)
        qk_r = sb("qk_r", [STACK, 2 * QG, BT], F32R)
        v_r = sb("v_r", [P, 2, QG, P], F32R)
        exp_k = sb("exp_k", [P, 2 * 1024])
        exp_q = silu_g[:].rearrange("p b n -> p (b n)")
        k_lo = x_hi[:, 0:2048]
        q_lo = x_hi[:, 2048:4096]
        k_hi = x_lo[:, 0:2048]
        q_hi = x_lo[:, 2048:4096]
        kv_t = sb("kv_t", [P, 4 * BT])
        kv_tmp = sb("kv_tmp", [P, 2, 4, 2 * SLOT])
        kv_sum = sb("kv_sum", [P, 2, 4, 2 * SLOT])
        kv_own = sb("kv_own", [P, 2, 4, 2 * SLOT])
        head_mask = sb("head_mask", [P, 2 * SLOT])
        kv_hi = sb("kv_hi", [P, 2, 4 * DIAG], F32R)
        kv_lo = sb("kv_lo", [P, 2, 4 * DIAG], F32R)
        o_sb = sb("o_sb", [P, CT])
        den = sb("den", [P, 2 * HEADS])
        rden = sb("rden", [P, 2 * HEADS])
        on = sb("on", [P, BT])
        on_t = sb("on_t", [P, BT])

        pG = psum("pG", [P, 2, 512])
        pU = psum("pU", [P, 2, 512])
        pC = psum("pC", [P, 512])
        pY = psum("pY", [P, 512])
        T0 = psum("T0", [P, 512])
        T1 = psum("T1", [P, 512])
        T2 = pY
        FIRST_BANKS = (pG[:, 0], pG[:, 1])

        qk = qkv[:, :, 0:2 * H].rearrange("p t (g d) -> p t g d", g=2 * QG)
        qk_stack = stack[:].rearrange("p (t g) s -> p t g s", t=2)

        x_loaded = sem("x_loaded")
        w_loaded = [sem(f"w_loaded_{kind}") for kind in ("gate", "up", "down")]
        gate_loaded = sem("gate_loaded")
        small_loaded = sem("small_loaded")
        rf_zeroed = sem("rf_zeroed")
        rf_loaded = sem("rf_loaded")
        rf_ready = sem("rf_ready")
        out_stored = sem("out_stored")
        const_step = sem("const_step")
        w_hi_ready = sem("w_hi_ready")
        w_lo_ready = [sem(f"w_lo_ready_{kind}") for kind in ("gate", "up", "down")]
        small_hi_ready = sem("small_hi_ready")
        small_lo_ready = sem("small_lo_ready")
        route_step = sem("route_step")
        divide_step = sem("divide_step")
        v_step = sem("v_step")
        kv_step = sem("kv_step")
        bn_step = sem("bn_step")
        var_ready = sem("var_ready")
        bn_aggr_go = sem("bn_aggr_go")
        max_go = sem("max_go")
        pool_go = sem("pool_go")
        mv_ready = sem("mv_ready")
        rstd_ready = sem("rstd_ready")
        xn_ready = sem("xn_ready")
        xt_ready = sem("xt_ready")
        xhi_ready = sem("xhi_ready")
        xlo_ready = sem("xlo_ready")
        logits_ready = sem("logits_ready")
        scores_ready = sem("scores_ready")
        scores_tok_ready = sem("scores_tok_ready")
        sfc_ready = sem("sfc_ready")
        combine_hi_ready = sem("combine_hi_ready")
        combine_ready = sem("combine_ready")
        combine_tok_t = sem("combine_tok_t")
        combine_t_ready = sem("combine_t_ready")
        g_ready = sem("g_ready")
        u_ready = sem("u_ready")
        c_ready = sem("c_ready")
        silu_done = sem("silu_done")
        s_used = sem("s_used")
        gated_done = sem("gated_done")
        gated_hi_done = sem("gated_hi_done")
        gated_lo_done = sem("gated_lo_done")
        down_done = sem("down_done")
        y_done = sem("y_done")
        yt_ready = sem("yt_ready")
        ffn_x_done = sem("ffn_x_done")

        xta_ready = sem("xta_ready")
        qkv_ready = sem("qkv_ready")
        qkv_copied = sem("qkv_copied")
        squares_ready = sem("squares_ready")
        n2_ready = sem("n2_ready")
        ln_ready = sem("ln_ready")
        norm_split = sem("norm_split")
        norm_ready = sem("norm_ready")
        stack_ready = sem("stack_ready")
        stack_dup_ready = sem("stack_dup_ready")
        v_ready = sem("v_ready")
        stack_t_ready = sem("stack_t_ready")
        qk_even_ready = sem("qk_even_ready")
        qk_odd_ready = sem("qk_odd_ready")
        feat_ready = sem("feat_ready")
        exp_done = sem("exp_done")
        k_hi_done = sem("k_hi_done")
        k_lo_done = sem("k_lo_done")
        q_hi_done = sem("q_hi_done")
        q_lo_done = sem("q_lo_done")
        kv_ready = sem("kv_ready")
        kv_copied = sem("kv_copied")
        kv_tr_ready = sem("kv_tr_ready")
        kv_tr_read = sem("kv_tr_read")
        kv_split = sem("kv_split")
        o_ready = sem("o_ready")
        o_copied = sem("o_copied")
        o_tr_ready = sem("o_tr_ready")
        on_ready = sem("on_ready")
        on_tr_ready = sem("on_tr_ready")
        on_copied = sem("on_copied")
        proj_ready = sem("proj_ready")
        att_x_added = sem("att_x_added")
        att_x_done = sem("att_x_done")

        def tiles_of(ap, n=TILES):
            return ap.rearrange("p (t h) -> p t h", t=n)

        def w_block(w, kind, j):
            k = (kind * BLOCKS + j) * P
            return w[:, k:k + P]

        wn = BLOCKS * P
        sel_raw = kv_t
        w_stage = [exp_k[:, 0:wn], exp_q[:, 0:wn], gated[:].rearrange("p b n -> p (b n)")[:, 0:wn]]

        def has(a, k):
            return not isinstance(a, int) or 0 <= a + k < ROWS

        def last(a):
            return isinstance(a, int) and a == ROWS - 1

        def before_attention(c, f0):
            return f0 == 0 and isinstance(c, int) and c == CHUNKS - 1

        def attention(eng, row, loop_end=ROWS - 2):
            row(0)
            row(1)
            with eng.Fori(2, loop_end) as a:
                row(a)
            for a in range(loop_end, ROWS - 2):
                row(a)

        class Steps:
            def __init__(self, eng, s, base=0):
                self.eng, self.s, self.base, self.n = eng, s, base, 0

            def mark(self, ins):
                self.n += 1
                ins.then_inc(self.s, 1)

            def wait(self):
                self.eng.wait_ge(self.s, self.base + self.n)

            def link(self, ins):
                self.mark(ins)
                self.wait()

        block = ctx.enter_context(nc.Block())

        @block.sync
        def _(sp):
            def x_chunk(c):
                return X[:, c * CT:(c + 1) * CT].rearrange("p (b w) -> p b w", b=2)

            sp.dma_start(x_chunk(0), x_v[0]).then_inc(x_loaded, 16)
            sp.dma_start(gk_raw[:], gate_k).then_inc(gate_loaded, 16)
            sp.dma_start(gb_rows[:], gate_b.partition_broadcast(P)).then_inc(small_loaded, 16)
            sp.dma_start(sel_raw[:], pair_sel).then_inc(small_loaded, 16)
            for c in range(1, CHUNKS):
                sp.wait_ge(x_loaded, 16 * c)
                sp.dma_start(x_chunk(c), x_v[c]).then_inc(x_loaded, 16)
            sp.dma_start(wqkv_sb[:], wqkv).then_inc(small_loaded, 16)
            sp.dma_start(wout_sb[:], wout).then_inc(small_loaded, 16)
            sp.dma_start(bout_rows[:], b_out.partition_broadcast(P)).then_inc(small_loaded, 16)
            sp.wait_ge(rf_zeroed, 1)
            for part in range(3):
                for hh in range(HG):
                    r = (part * HG + hh) * HD
                    sp.dma_start(rf_raw[r:r + HD, hh * NF:(hh + 1) * NF], rft).then_inc(rf_loaded, 16)
            sp.dma_start(rf_raw[3 * HG * HD:STACK, :], norm_sel).then_inc(rf_loaded, 16)
            for c in range(CHUNKS):
                sp.wait_ge(ffn_x_done, CHUNKS + c + 1)
                sp.dma_start(out_v[c], x_chunk(c)).then_inc(out_stored, 16)
            sp.wait_ge(out_stored, 16 * CHUNKS)

        @block.gpsimd
        def _(pool):
            pool.sem_inc(gated_lo_done, QL_CREDIT)
            pool.sem_inc(q_lo_done, QF_CREDIT)

            def rstd_of(p, n):
                pool.wait_ge(mv_ready, p + 1)
                pool.sem_inc(pool_go, 1)
                nc.gpsimd.tensor_scalar(vareps[:, 0:n], meanvar[:, 0:n, 1], LN_EPS, 0.0, ALU.add,
                                        ALU.add).then_inc(var_ready, 1)
                pool.wait_ge(var_ready, p + 1)
                nc.gpsimd.tensor_tensor(rstd[:, 0:n], vareps[:, 0:n], minus_half[:, 0:n],
                                        ALU.pow).then_inc(rstd_ready, 1)

            def constants():
                steps = Steps(pool, const_step)
                steps.link(nc.gpsimd.memset(minus_half[:], -0.5))
                steps.link(nc.gpsimd.memset(norm2_least[:], NORM2_LEAST))
                steps.link(nc.gpsimd.memset(ident[:], 0.0))
                steps.link(nc.gpsimd.affine_select(out=ident[:], in_=ident[:], compare_op=ALU.not_equal,
                                                   fill=1.0, base=0, pattern=[[-1, P]], channel_multiplier=1))
                steps.link(nc.gpsimd.memset(gk_hi[:].bitcast(F32), 0.0))
                steps.link(nc.gpsimd.memset(gk_lo[:].bitcast(F32), 0.0))
                assert steps.n == GK_CONSTS
                rstd_of(0, TILES)
                steps.link(nc.gpsimd.memset(g_before[:], 0.0))
                for g in range(1, GROUPS):
                    steps.link(nc.gpsimd.memset(g_before[:, g, 0:g], 1.0))
                steps.link(nc.gpsimd.memset(restart[:], 1.0))
                steps.link(nc.gpsimd.memset(restart[:, 0::EXPERTS], 0.0))
                steps.link(nc.gpsimd.memset(combine_s[:].bitcast(F32), 0.0))
                assert steps.n == ROUTE_CONSTS
                rstd_of(1, TILES)
                pool.wait_ge(w_hi_ready, 2)
                cols = slice(BLOCKS * P, 2 * BLOCKS * P)
                nc.gpsimd.tensor_tensor(w_lo[:, cols], w_stage[1], w_hi[:, cols].bitcast(F32),
                                        ALU.subtract).then_inc(w_lo_ready[1], 1)
                nc.gpsimd.memset(rf_raw[:], 0.0).then_inc(rf_zeroed, 1)
                steps.link(nc.gpsimd.memset(head_mask[:], 0.0))
                steps.link(nc.gpsimd.memset(head_mask[0:M, 0:SLOT], 1.0))
                steps.link(nc.gpsimd.memset(head_mask[M:P, SLOT:2 * SLOT], 1.0))
                steps.link(nc.gpsimd.memset(v_r[:].bitcast(F32), 0.0))
                ones_cols = v_r[:, :, :, 0:HG * SLOT].rearrange("p t g (k s) -> p (t g) k s", s=SLOT)[:, :, :, HD]
                steps.link(nc.gpsimd.memset(ones_cols.bitcast(F32), 1.0))
                steps.link(nc.gpsimd.memset(kv_hi[:].bitcast(F32), 0.0))
                steps.link(nc.gpsimd.memset(kv_lo[:].bitcast(F32), 0.0))
                assert steps.n == ALL_CONSTS

            def ffn(f0, ln0):
                def lo_part(n, j):
                    pool.wait_ge(gated_hi_done, n + 1)
                    nc.gpsimd.tensor_tensor(gated_lo[:, j % 3], gated[:, j % 3], gated_hi[:, j % 3].bitcast(F32),
                                            ALU.subtract).then_inc(gated_lo_done, 1)

                def chunk(c, prev, nxt2):
                    n0 = (c + f0) * BLOCKS
                    for j in range(BLOCKS):
                        if j >= 1:
                            lo_part(n0 + (j - 1), j - 1)
                        elif prev:
                            lo_part(n0 - 1, BLOCKS - 1)
                        if j == 2 and nxt2:
                            rstd_of(c + (2 + ln0), TILES)
                        if before_attention(c, f0):
                            if j == 1:
                                rstd_of(LN_ATT, 2)
                            if j == 3:
                                rstd_of(LN_ATT + 1, 2)
                            if j == 6:
                                squares_and_dup(0)

                chunk(0, False, True)
                with pool.Fori(1, CHUNKS - 2) as c:
                    chunk(c, True, True)
                chunk(CHUNKS - 2, True, False)
                chunk(CHUNKS - 1, True, False)
                lo_part((f0 + CHUNKS) * BLOCKS - 1, BLOCKS - 1)

            def squares_and_dup(a):
                pool.wait_ge(qkv_copied, 2 * a + 2)
                pool.wait_ge(n2_ready, a + N2_CREDIT)
                nc.gpsimd.tensor_tensor(squares[:], qkv[:, :, 0:2 * H], qkv[:, :, 0:2 * H],
                                        ALU.mult).then_inc(squares_ready, 1)
                pool.wait_ge(stack_t_ready, 4 * a + STACK_CREDIT)
                pool.sem_inc(pool_go, 1)
                for t in range(2):
                    last = nc.gpsimd.tensor_scalar(
                        stack[:, 8 * t:8 * t + 8, 64:96],
                        qkv[:, t, 0:2 * H].rearrange("p (g d) -> p g d", g=2 * QG),
                        1.0, 0.0, ALU.mult, ALU.add)
                last.then_inc(stack_dup_ready, 1)

            def q_split(a, u):
                cols = slice(u * CT, (u + 1) * CT)
                pool.wait_ge(exp_done, 8 * a + (4 + u + 1 + EXP_CREDIT))
                pool.wait_ge(o_ready, 2 * a + (u // 2 + 1 - 2 + O_CREDIT))
                pool.sem_inc(pool_go, 1)
                nc.gpsimd.tensor_scalar(q_hi[:, cols], exp_q[:, cols], 1.0, 0.0, ALU.mult,
                                        ALU.add).then_inc(q_hi_done, 1)
                pool.wait_ge(q_hi_done, 4 * a + (u + 1))
                nc.gpsimd.tensor_tensor(q_lo[:, cols], exp_q[:, cols], q_hi[:, cols].bitcast(F32),
                                        ALU.subtract).then_inc(q_lo_done, 1)

            def bias(a):
                pool.wait_ge(att_x_added, a + 1)
                xs = tiles_of(X[:, ds(a * BT, BT)], 2)
                nc.gpsimd.tensor_tensor(xs, xs, bout_rows[:].unsqueeze(1).broadcast_to((P, 2, H)),
                                        ALU.add).then_inc(att_x_done, 1)

            def row(a):
                if has(a, 1):
                    squares_and_dup(a + 1)
                if has(a, 2):
                    rstd_of(a + (2 + LN_ATT), 2)
                if has(a, 0):
                    q_split(a, 0)
                if has(a, -2):
                    bias(a - 2)
                if last(a):
                    rstd_of(LN_FFN2 + 1, TILES)
                if has(a, 0):
                    for u in range(1, 4):
                        q_split(a, u)

            constants()
            ffn(0, 0)
            pool.wait_ge(small_loaded, 16 * 5)
            attention(pool, row)
            rstd_of(LN_FFN2, TILES)
            row(ROWS - 2)
            row(ROWS - 1)
            row(ROWS)
            row(ROWS + 1)
            ffn(CHUNKS, LN_FFN2)

        @block.scalar
        def _(act):
            for k, stage in enumerate(w_stage):
                act.dma_start(stage, wall[:, k * BLOCKS * P:(k + 1) * BLOCKS * P]).then_inc(w_loaded[k], 16)
            act.sem_inc(silu_done, SILU_CREDIT)
            act.sem_inc(y_done, Y_CREDIT)
            act.sem_inc(exp_done, EXP_CREDIT)
            act.sem_inc(kv_copied, KV_COPY_CREDIT)
            act.sem_inc(o_copied, O_COPY_CREDIT)

            def copy(o, i):
                return nc.scalar.activation(o, i, ACT.Copy)

            def x_hi_part(f, c, p, bank=T1[:]):
                act.wait_ge(xt_ready, p + (1 + XT_CREDIT))
                copy(x_hi[:, ds(c * CT, CT)], bank).then_inc(xhi_ready, 1)

            def scores(f, bank=T1[:]):
                act.wait_ge(logits_ready, f + 1)
                if not isinstance(f, int) or f > 0:
                    act.wait_ge(scores_tok_ready, f)
                nc.scalar.activation(scores_t[:], bank, ACT.Sigmoid).then_inc(scores_ready, 1)

            def combine_copy(f, c):
                act.wait_ge(combine_tok_t, f + 1)
                copy(combine_t[:, ds(c * CT, CT)], T1[:]).then_inc(combine_t_ready, 1)

            def weight_hi(k):
                act.wait_ge(w_loaded[k], 16)
                copy(w_hi[:, k * BLOCKS * P:(k + 1) * BLOCKS * P], w_stage[k]).then_inc(w_hi_ready, 1)

            def ffn(f0, ln0):
                def hi_part(n, j):
                    act.wait_ge(gated_done, n + (1 + Q_CREDIT))
                    act.wait_ge(down_done, n + (1 - 3 + D_CREDIT))
                    copy(gated_hi[:, j % 3], gated[:, j % 3]).then_inc(gated_hi_done, 1)

                def y_copy(f):
                    act.wait_ge(down_done, f * BLOCKS + (BLOCKS + D_CREDIT))
                    act.wait_ge(yt_ready, f + YT_CREDIT)
                    copy(y_sb[:], pY[:]).then_inc(y_done, 1)

                def chunk(c, prev, nxt, nxt2):
                    f = c + f0
                    n0, m0 = f * BLOCKS, f * PAIRS
                    for j in range(BLOCKS):
                        if j == 3 and prev:
                            y_copy(f - 1)
                        if j == 6 and nxt2:
                            x_hi_part(f + 2, c + 2, c + (ln0 + 2))
                        if j == 8 and nxt2:
                            scores(f + 2)
                        if before_attention(c, f0):
                            if j == 2:
                                act.wait_ge(rf_loaded, 16 * 13)
                                copy(rf_r[:], rf_raw[:]).then_inc(rf_ready, 1)
                            if j == 3:
                                x_t_copy(0, T1)
                            if j == 4:
                                qkv_copy(0)
                            if j == 5:
                                stack_hi(0)
                            if j == 6:
                                x_t_copy(1, T1)
                        act.wait_ge(g_ready, n0 + (j + 1))
                        if j < PAIRS:
                            act.wait_ge(s_used, m0 + (j + 1 - 4 + S_CREDIT))
                            nc.scalar.activation(silu_g[:, j % 4], pG[:, j % 2], ACT.Silu).then_inc(silu_done, 1)
                        else:
                            act.wait_ge(gated_done, n0 + (j + 1 - BLOCKS + Q_CREDIT))
                            nc.scalar.activation(silu_s[:], T0[:], ACT.Silu).then_inc(silu_done, 1)
                        if j == 0 and not prev:
                            if f0 > 0:
                                on_copy(ROWS - 1)
                            combine_copy(f, c)
                        if j == 8 and nxt:
                            combine_copy(f + 1, c + 1)
                        if j >= 1:
                            hi_part(n0 + (j - 1), j - 1)
                        elif prev:
                            hi_part(n0 - 1, BLOCKS - 1)

                chunk(0, False, True, True)
                with act.Fori(1, CHUNKS - 2) as c:
                    chunk(c, True, True, True)
                chunk(CHUNKS - 2, True, True, False)
                chunk(CHUNKS - 1, True, False, False)
                hi_part((f0 + CHUNKS) * BLOCKS - 1, BLOCKS - 1)
                if f0 == 0:
                    nc.scalar.preload_act_table_set("natural_log_exp_and_others")
                    norms(0)
                y_copy(f0 + CHUNKS - 1)

            def x_t_copy(a, bank=T2):
                act.wait_ge(xt_ready, a + (LN_ATT + 1 + XT_CREDIT))
                if not isinstance(a, int) or a > 0:
                    act.wait_ge(qkv_ready, 2 * a)
                copy(x_t[:], bank[:, 0:BT]).then_inc(xta_ready, 1)

            def qkv_copy(a):
                if not isinstance(a, int) or a > 0:
                    act.wait_ge(v_ready, a)
                    act.wait_ge(stack_dup_ready, a)
                for t, bank in enumerate((T0, T1)):
                    act.wait_ge(qkv_ready, 2 * a + (t + 1))
                    copy(qkv[:, t], bank[:, 0:3 * H]).then_inc(qkv_copied, 1)

            def stack_hi(a):
                act.wait_ge(qkv_copied, 2 * a + 2)
                act.wait_ge(stack_t_ready, 4 * a + STACK_CREDIT)
                copy(qk_stack[:, :, :, 0:32], qk).then_inc(stack_ready, 1)

            def norms(a):
                act.wait_ge(n2_ready, a + (1 + N2_CREDIT))
                nc.scalar.activation(ln_n2[:], n2[:], ACT.Ln, bias=norm2_least[:]).then_inc(ln_ready, 1)
                act.wait_ge(ln_ready, a + 1)
                nc.scalar.activation(norm[:], ln_n2[:], ACT.Exp, scale=0.5).then_inc(norm_ready, 1)

            def stack_copy(a, s):
                act.wait_ge(stack_t_ready, 4 * a + ((s + 2) % 4 + 1 + STACK_CREDIT))
                copy(qk_r[:, 2 * s:2 * s + 2].rearrange("p g n -> p (g n)"),
                     T0[0:STACK, :]).then_inc(qk_even_ready, 1)

            def k_features(a, u):
                cols = slice(u * CT, (u + 1) * CT)
                act.wait_ge(feat_ready, 8 * a + (u + 1))
                act.wait_ge(k_lo_done, 4 * a + (u + 1 - 4 + K_CREDIT))
                nc.scalar.activation(exp_k[:, cols], pG[:, u % 2], ACT.Exp, scale=NF ** -0.5).then_inc(exp_done, 1)

            def k_hi_part(a, u):
                cols = slice(u * CT, (u + 1) * CT)
                act.wait_ge(exp_done, 8 * a + (u + 1 + EXP_CREDIT))
                act.wait_ge(kv_ready, a + KV_CREDIT)
                copy(k_hi[:, cols], exp_k[:, cols]).then_inc(k_hi_done, 1)

            def q_features(a, u):
                act.wait_ge(feat_ready, 8 * a + (4 + u + 1))
                act.wait_ge(q_lo_done, 4 * a + (u + 1 - 4 + QF_CREDIT))
                nc.scalar.activation(exp_q[:, u * CT:(u + 1) * CT], pG[:, u % 2], ACT.Exp,
                                     scale=NF ** -0.5).then_inc(exp_done, 1)

            def o_copy(a):
                act.wait_ge(o_ready, 2 * a + (2 + O_CREDIT))
                if not isinstance(a, int) or a > 0:
                    act.wait_ge(o_tr_ready, a)
                copy(o_sb[:], pC[:]).then_inc(o_copied, 1)

            def on_copy(a):
                act.wait_ge(on_tr_ready, a + 1)
                act.wait_ge(proj_ready, a + PROJ_CREDIT)
                copy(on_t[:], T2[:, 0:BT]).then_inc(on_copied, 1)

            def kv_copy(a):
                act.wait_ge(kv_ready, a + (1 + KV_CREDIT))
                act.wait_ge(kv_tr_ready, 2 * a + KV_TR_CREDIT)
                copy(kv_t[:], pU[:].rearrange("p b n -> p (b n)")).then_inc(kv_copied, 1)

            def row(a):
                if has(a, 0):
                    k_features(a, 0)
                    k_features(a, 1)
                    k_hi_part(a, 0)
                    k_features(a, 2)
                    k_features(a, 3)
                if has(a, -2):
                    on_copy(a - 2)
                if has(a, 0):
                    k_hi_part(a, 1)
                    k_hi_part(a, 2)
                    k_hi_part(a, 3)
                    q_features(a, 0)
                    q_features(a, 1)
                if has(a, 1):
                    stack_hi(a + 1)
                    norms(a + 1)
                if has(a, 0):
                    q_features(a, 2)
                if has(a, -1):
                    o_copy(a - 1)
                if has(a, 1):
                    stack_copy(a + 1, 2)
                if has(a, 0):
                    q_features(a, 3)
                if has(a, 2):
                    x_t_copy(a + 2)
                if has(a, 1):
                    stack_copy(a + 1, 0)
                if has(a, 0):
                    kv_copy(a)
                if has(a, 2):
                    qkv_copy(a + 2)

            act.wait_ge(gate_loaded, 16)
            act.wait_ge(const_step, GK_CONSTS)
            copy(gk_hi[:, 0:EXPERTS], gk_raw[:]).then_inc(small_hi_ready, 1)
            x_hi_part(0, 0, 0, FIRST_BANKS[0])
            weight_hi(0)
            weight_hi(1)
            scores(0, FIRST_BANKS[0])
            act.wait_ge(small_loaded, 16 * 2)
            copy(sel_r[:], sel_raw[:]).then_inc(small_hi_ready, 1)
            weight_hi(2)
            x_hi_part(1, 1, 1, FIRST_BANKS[1])
            scores(1, FIRST_BANKS[1])
            ffn(0, 0)

            stack_copy(0, 2)
            stack_copy(0, 0)
            qkv_copy(1)
            attention(act, row)
            row(ROWS - 2)
            row(ROWS - 1)
            act.wait_ge(kv_ready, ROWS + KV_CREDIT)
            x_hi_part(CHUNKS, 0, LN_FFN2, FIRST_BANKS[0])
            on_copy(ROWS - 2)
            scores(CHUNKS, FIRST_BANKS[0])
            x_hi_part(CHUNKS + 1, 1, LN_FFN2 + 1, FIRST_BANKS[1])
            o_copy(ROWS - 1)
            scores(CHUNKS + 1, FIRST_BANKS[1])
            ffn(CHUNKS, LN_FFN2)

        @block.vector
        def _(dve):
            dve.sem_inc(s_used, S_CREDIT)
            dve.sem_inc(gated_done, Q_CREDIT)
            dve.sem_inc(k_lo_done, K_CREDIT)
            dve.sem_inc(n2_ready, N2_CREDIT)
            tt = nc.vector.tensor_tensor

            def ln_stats(p, x0, n):
                if not isinstance(p, int) or p > 0:
                    dve.wait_ge(xn_ready, p)
                for t in range(n):
                    last = nc.vector.bn_stats(stats[:, t, :], X[:, ds(x0 + t * H, H)])
                last.then_inc(bn_step, 1)
                dve.wait_ge(bn_step, p + 1)
                dve.sem_inc(bn_aggr_go, 1)
                for t in range(n):
                    last = nc.vector.bn_aggr(meanvar[:, t, :], stats[:, t, :])
                last.then_inc(mv_ready, 1)

            def ln_apply(p, x0, n):
                dve.wait_ge(rstd_ready, p + 1)
                dve.wait_ge(xt_ready, p + XT_CREDIT)
                for t in range(n):
                    last = nc.vector.tensor_scalar(xn[:, t * H:(t + 1) * H], X[:, ds(x0 + t * H, H)],
                                                   meanvar[:, t, 0:1], rstd[:, t:t + 1], ALU.subtract, ALU.mult)
                last.then_inc(xn_ready, 1)

            def x_lo_part(f, c, bank=T1[:]):
                dve.wait_ge(xhi_ready, f + 1)
                cols = ds(c * CT, CT)
                tt(x_lo[:, cols], bank, x_hi[:, cols].bitcast(F32), ALU.subtract).then_inc(xlo_ready, 1)

            def weight_lo(k):
                dve.wait_ge(w_hi_ready, k + 1)
                cols = slice(k * BLOCKS * P, (k + 1) * BLOCKS * P)
                tt(w_lo[:, cols], w_stage[k], w_hi[:, cols].bitcast(F32), ALU.subtract).then_inc(w_lo_ready[k], 1)

            def per_tile(ap):
                return ap.unsqueeze(2).broadcast_to((P, TILES, EXPERTS))

            def route_scores(f, bank=T1[:]):
                dve.wait_ge(scores_tok_ready, f + 1)
                if not isinstance(f, int) or f > 0:
                    dve.wait_ge(combine_ready, f)
                tt(sfc[:].rearrange("p (t e) -> p t e", t=TILES),
                   bank.rearrange("p (t e) -> p t e", t=TILES)[:, :, 0:EXPERTS],
                   gb_rows[:].unsqueeze(1).broadcast_to((P, TILES, EXPERTS)), ALU.add).then_inc(sfc_ready, 1)

            def route_pairs(f, steps):
                dve.wait_ge(sfc_ready, f + 1)
                s4 = sfc[:].rearrange("p (g e) -> p g e", e=EG)
                tt(pair_hi[:], s4[:, :, 0:2], s4[:, :, 2:4], ALU.max)
                steps.mark(tt(pair_lo[:], s4[:, :, 0:2], s4[:, :, 2:4], ALU.min))

            def route_best(f, steps):
                steps.wait()
                tt(g_top[:], pair_hi[:, :, 0], pair_hi[:, :, 1], ALU.max)
                tt(g_mid[:], pair_hi[:, :, 0], pair_hi[:, :, 1], ALU.min)
                steps.mark(tt(g_low[:], pair_lo[:, :, 0], pair_lo[:, :, 1], ALU.max))

            def route_second(f, steps):
                steps.wait()
                steps.mark(tt(g_mid[:], g_mid[:], g_low[:], ALU.max))

            def route_group_sum(f, steps):
                steps.wait()
                steps.mark(tt(g_sum[:].rearrange("p t g -> p (t g)"), g_top[:], g_mid[:], ALU.add))

            def route_compare(f, steps):
                steps.wait()
                other = g_sum[:].unsqueeze(2).broadcast_to((P, TILES, GROUPS, GROUPS))
                own = g_sum[:].unsqueeze(3).broadcast_to((P, TILES, GROUPS, GROUPS))
                tt(g_gt[:], other, own, ALU.is_gt)
                steps.mark(tt(g_eq[:], other, own, ALU.is_equal))

            def route_equal(f, steps):
                steps.wait()
                steps.mark(tt(g_eq[:], g_eq[:], g_before[:].unsqueeze(1).broadcast_to((P, TILES, GROUPS, GROUPS)),
                              ALU.mult))

            def route_before(f, steps):
                steps.wait()
                steps.mark(tt(g_gt[:], g_gt[:], g_eq[:], ALU.add))

            def route_rank(f, steps):
                steps.wait()
                steps.mark(nc.vector.tensor_reduce(g_rank[:], g_gt[:].rearrange("p t g o -> p (t g) o"), AX_X,
                                                   ALU.add))

            def route_masked(f, steps):
                steps.wait()
                steps.mark(nc.vector.scalar_tensor_tensor(
                    masked[:].rearrange("p t (g e) -> p (t g) e", e=EG),
                    g_rank[:].unsqueeze(2).broadcast_to((P, 16, EG)), 2.0,
                    sfc[:].rearrange("p (g e) -> p g e", e=EG), ALU.is_lt, ALU.mult))

            def route_top(f, steps):
                steps.wait()
                dve.sem_inc(max_go, 1)
                for t in range(TILES):
                    last = nc.vector.max(top8[:, t, :], masked[:, t, :])
                steps.mark(last)

            def route_above(f, steps):
                steps.wait()
                fourth = per_tile(top8[:, :, 3])
                tt(above[:], masked[:], fourth, ALU.is_gt)
                steps.mark(tt(tied[:].rearrange("p (t e) -> p t e", t=TILES), masked[:], fourth, ALU.is_equal))

            def route_count(f, steps):
                steps.wait()
                nc.vector.tensor_reduce(n_above[:], above[:], AX_X, ALU.add)
                steps.mark(nc.vector.tensor_tensor_scan(order[:], restart[:], tied[:], 0.0, ALU.mult, ALU.add))

            def route_order(f, steps):
                steps.wait()
                order3 = order[:].rearrange("p (t e) -> p t e", t=TILES)
                steps.mark(tt(order3, order3, per_tile(n_above[:]), ALU.add))

            def route_tied(f, steps):
                steps.wait()
                order3 = order[:].rearrange("p (t e) -> p t e", t=TILES)
                tied3 = tied[:].rearrange("p (t e) -> p t e", t=TILES)
                steps.mark(nc.vector.scalar_tensor_tensor(chosen[:], order3, 4.0, tied3, ALU.is_le, ALU.mult))

            def route_chosen(f, steps):
                steps.wait()
                steps.mark(tt(chosen[:], chosen[:], above[:], ALU.add))

            def route_kept(f, steps):
                steps.wait()
                steps.mark(tt(masked[:], masked[:], chosen[:], ALU.mult))

            def route_sum(f, steps):
                steps.wait()
                steps.mark(nc.vector.tensor_reduce(w_sum[:], masked[:], AX_X, ALU.add))

            def route_guard(f, steps):
                steps.wait()
                steps.mark(nc.vector.tensor_scalar(w_sum[:], w_sum[:], 1e-20, None, ALU.add))

            def route_inverse(f, steps):
                steps.wait()
                steps.mark(nc.vector.reciprocal(w_sum[:], w_sum[:]))

            def route_weights(f, steps):
                steps.wait()
                steps.mark(nc.vector.scalar_tensor_tensor(combine[:], masked[:], SCALE, per_tile(w_sum[:]),
                                                          ALU.mult, ALU.mult))

            def route_split(f, steps):
                assert steps.n == ROUTE_STEPS, steps.n
                steps.wait()
                if not isinstance(f, int) or f > 0:
                    dve.wait_ge(combine_tok_t, f)
                nc.vector.tensor_copy(combine_s[:, :, 0:EXPERTS], combine[:]).then_inc(combine_hi_ready, 1)
                dve.wait_ge(combine_hi_ready, f + 1)
                tt(combine_s[:, :, EXPERTS:2 * EXPERTS], combine[:], combine_s[:, :, 0:EXPERTS].bitcast(F32),
                   ALU.subtract).then_inc(combine_ready, 1)

            def ffn(f0, ln0):
                def add_y(f, c, bank=T0):
                    dve.wait_ge(yt_ready, f + (1 + YT_CREDIT))
                    xs = X[:, ds(c * CT, CT)]
                    nc.vector.scalar_tensor_tensor(xs, bank[:], 0.5, xs, ALU.mult, ALU.add).then_inc(ffn_x_done, 1)

                def chunk(c, prev, nxt, nxt2):
                    f = c + f0
                    n0, m0 = f * BLOCKS, f * PAIRS
                    steps = Steps(dve, route_step, (f + 1) * ROUTE_STEPS)
                    for j in range(BLOCKS):
                        if j < PAIRS:
                            dve.wait_ge(silu_done, n0 + (j + 1 + SILU_CREDIT))
                            dve.wait_ge(c_ready, m0 + (j + 1))
                            dve.wait_ge(gated_done, n0 + (j + 1 - 2 + Q_CREDIT))
                            tt(weighted[:, j % 2], pC[:], silu_g[:, j % 4], ALU.mult).then_inc(s_used, 1)
                        if nxt:
                            if j == 0:
                                route_scores(f + 1)
                            if j == 1:
                                route_best(f + 1, steps)
                            if j == 2:
                                route_group_sum(f + 1, steps)
                            if j == 3:
                                route_equal(f + 1, steps)
                            if j == 4:
                                route_masked(f + 1, steps)
                            if j == 5:
                                route_above(f + 1, steps)
                            if j == 6:
                                route_order(f + 1, steps)
                                route_tied(f + 1, steps)
                            if j == 7:
                                route_sum(f + 1, steps)
                                route_guard(f + 1, steps)
                        if j == 2 and nxt2:
                            if f0 == 0:
                                dve.wait_ge(x_loaded, c * 16 + 48)
                            elif not prev:
                                dve.wait_ge(att_x_done, ROWS)
                            ln_stats(c + (2 + ln0), (c + 2) * CT, TILES)
                        if j < PAIRS:
                            dve.wait_ge(s_used, m0 + (j + 1 + S_CREDIT))
                            up, factor = pU[:, j % 2], weighted[:, j % 2]
                        else:
                            dve.wait_ge(silu_done, n0 + (j + 1 + SILU_CREDIT))
                            up, factor = pC[:], silu_s[:]
                        dve.wait_ge(u_ready, n0 + (j + 1))
                        dve.wait_ge(gated_lo_done, n0 + (j + 1 - 3 + QL_CREDIT))
                        tt(gated[:, j % 3], up, factor, ALU.mult).then_inc(gated_done, 1)
                        if nxt:
                            if j == 0:
                                route_pairs(f + 1, steps)
                            if j == 1:
                                route_second(f + 1, steps)
                            if j == 2:
                                route_compare(f + 1, steps)
                            if j == 3:
                                route_before(f + 1, steps)
                                route_rank(f + 1, steps)
                            if j == 4:
                                route_top(f + 1, steps)
                            if j == 5:
                                route_count(f + 1, steps)
                            if j == 6:
                                route_chosen(f + 1, steps)
                                route_kept(f + 1, steps)
                            if j == 7:
                                route_inverse(f + 1, steps)
                                route_weights(f + 1, steps)
                                route_split(f + 1, steps)
                        if j == 3 and nxt2:
                            ln_apply(c + (2 + ln0), (c + 2) * CT, TILES)
                        if j == 5 and nxt2:
                            x_lo_part(f + 2, c + 2)
                        if j == 5 and prev:
                            add_y(f - 1, c - 1)
                        if before_attention(c, f0):
                            if j == 0:
                                att_stats(0)
                            if j == 1:
                                ln_apply(LN_ATT, 0, 2)
                            if j == 2:
                                att_stats(1)
                            if j == 3:
                                dve.wait_ge(const_step, ALL_CONSTS)
                                dve.wait_ge(rf_ready, 1)
                                tt(rf_r[64:96, :], rf_raw[64:96, :], rf_r[64:96, :].bitcast(F32),
                                   ALU.subtract).then_inc(rf_ready, 1)
                            if j == 4:
                                ln_apply(LN_ATT + 1, BT, 2)
                            if j == 6:
                                stack_lo(0)
                            if j == 7:
                                squared_norms(0)
                                att_stats(2)
                            if j == 8:
                                norm_parts(0)

                chunk(0, False, True, True)
                with dve.Fori(1, CHUNKS - 2) as c:
                    chunk(c, True, True, True)
                chunk(CHUNKS - 2, True, True, False)
                chunk(CHUNKS - 1, True, False, False)
                add_y(f0 + CHUNKS - 1, CHUNKS - 1, T2 if f0 == 0 else T0)

            def route(f, first, last):
                steps = Steps(dve, route_step, f * ROUTE_STEPS)
                steps.n = first
                stages = (route_pairs, route_best, route_second, route_group_sum, route_compare, route_equal,
                          route_before, route_rank, route_masked, route_top, route_above, route_count, route_order,
                          route_tied, route_chosen, route_kept, route_sum, route_guard, route_inverse, route_weights,
                          route_split)
                for stage in stages[first:last]:
                    stage(f, steps)

            def att_stats(a):
                ln_stats(a + LN_ATT, a * BT, 2)

            def stack_lo(a):
                dve.wait_ge(stack_ready, 2 * a + 1)
                tt(qk_stack[:, :, :, 32:64], qk, qk_stack[:, :, :, 0:32].bitcast(F32), ALU.subtract).then_inc(stack_ready, 1)

            def v_parts(a):
                steps = Steps(dve, v_step, a * V_STEPS)
                dve.wait_ge(kv_ready, a + KV_CREDIT)
                for t in range(2):
                    v = qkv[:, t, 2 * H:3 * H].rearrange("p (g k d) -> p g k d", g=QG, k=HG)
                    part = v_r[:, t].rearrange("p g (l k s) -> p l g k s", l=2, s=SLOT)
                    steps.link(nc.vector.tensor_copy(part[:, 0, :, :, 0:HD], v))
                    last = tt(part[:, 1, :, :, 0:HD], v, part[:, 0, :, :, 0:HD].bitcast(F32), ALU.subtract)
                last.then_inc(v_ready, 1)

            def squared_norms(a):
                dve.wait_ge(squares_ready, a + 1)
                if not isinstance(a, int) or a > 0:
                    dve.wait_ge(ln_ready, a)
                nc.vector.tensor_reduce(
                    n2[:].rearrange("p (t h) -> p t h", t=2),
                    squares[:].rearrange("p t (h d) -> p t h d", d=HD), AX_X, ALU.add).then_inc(n2_ready, 1)

            def norm_parts(a):
                dve.wait_ge(norm_ready, a + 1)
                nrm = norm[:].rearrange("p (t k) -> p t k", k=HG)
                nc.vector.tensor_copy(stack[:, :, 96:100], nrm).then_inc(norm_split, 1)
                dve.wait_ge(norm_split, 2 * a + 1)
                tt(stack[:, :, 100:104], nrm, stack[:, :, 96:100].bitcast(F32), ALU.subtract).then_inc(norm_split, 1)

            def stack_copy(a, s):
                dve.wait_ge(stack_t_ready, 4 * a + ((s + 2) % 4 + 1 + STACK_CREDIT))
                nc.vector.tensor_copy(qk_r[:, 2 * s:2 * s + 2].rearrange("p g n -> p (g n)"),
                                      T1[0:STACK, :]).then_inc(qk_odd_ready, 1)

            def k_lo_part(a, u):
                cols = slice(u * CT, (u + 1) * CT)
                dve.wait_ge(k_hi_done, 4 * a + (u + 1))
                tt(k_lo[:, cols], exp_k[:, cols], k_hi[:, cols].bitcast(F32), ALU.subtract).then_inc(k_lo_done, 1)

            def divide(a):
                steps = Steps(dve, divide_step, a * DIVIDE_STEPS)
                dve.wait_ge(o_tr_ready, a + 1)
                slots = T2[:].rearrange("p (h s) -> p h s", s=SLOT)
                steps.link(nc.vector.tensor_scalar(den[:], slots[:, :, HD], 1e-6, None, ALU.add))
                steps.link(nc.vector.reciprocal(rden[:], den[:]))
                if not isinstance(a, int) or a > 0:
                    dve.wait_ge(on_tr_ready, a)
                tt(on[:].rearrange("p (h d) -> p h d", d=HD), slots[:, :, 0:HD],
                   rden[:].unsqueeze(2).broadcast_to((P, 2 * HEADS, HD)), ALU.mult).then_inc(on_ready, 1)

            def add_projection(a):
                dve.wait_ge(proj_ready, a + (1 + PROJ_CREDIT))
                xs = X[:, ds(a * BT, BT)]
                tt(xs, T2[:, 0:BT], xs, ALU.add).then_inc(att_x_added, 1)

            def kv_sums(a):
                steps = Steps(dve, kv_step, a * KV_STEPS)
                rows = [bank[:].rearrange("p (g r w) -> p g r w", g=2, r=2) for bank in (T0, T1)]
                for jh in range(2):
                    dve.wait_ge(kv_tr_ready, 2 * a + (jh + 1 + KV_TR_CREDIT))
                    for r in range(2):
                        w = M + 2 * SLOT * r
                        last = nc.vector.tensor_copy(kv_tmp[:, jh, r:4:2, :], rows[jh][:, :, r, w:w + 2 * SLOT])
                    steps.mark(last)
                steps.wait()
                for jh in range(2):
                    for r in range(2):
                        w = 2 * SLOT * r
                        last = tt(kv_sum[:, jh, r:4:2, :], rows[jh][:, :, r, w:w + 2 * SLOT],
                                  kv_tmp[:, jh, r:4:2, :], ALU.add)
                    last.then_inc(kv_tr_read, 1)

            def kv_parts(a):
                steps = Steps(dve, kv_step, a * KV_STEPS + 2)
                dve.wait_ge(kv_tr_read, 2 * a + 2)
                flat = "p j k s -> p (j k) s"
                mask = head_mask[:].unsqueeze(1).broadcast_to((P, 8, 2 * SLOT))
                steps.link(tt(kv_own[:].rearrange(flat), kv_sum[:].rearrange(flat), mask, ALU.mult))
                dve.wait_ge(o_ready, 2 * a + O_CREDIT)
                hi = kv_hi[:].rearrange("p j (k s) -> p j k s", s=DIAG)[:, :, :, 0:2 * SLOT]
                lo = kv_lo[:].rearrange("p j (k s) -> p j k s", s=DIAG)[:, :, :, 0:2 * SLOT]
                steps.link(nc.vector.tensor_copy(hi, kv_own[:]))
                tt(lo, kv_own[:], hi.bitcast(F32), ALU.subtract).then_inc(kv_split, 1)

            def row(a):
                if has(a, 0):
                    v_parts(a)
                    stack_copy(a, 1)
                if has(a, -2):
                    divide(a - 2)
                if has(a, -1):
                    kv_sums(a - 1)
                    kv_parts(a - 1)
                if has(a, 0):
                    k_lo_part(a, 0)
                    k_lo_part(a, 1)
                if has(a, 1):
                    squared_norms(a + 1)
                if has(a, 0):
                    k_lo_part(a, 2)
                    k_lo_part(a, 3)
                if last(a):
                    ln_apply(LN_FFN2, 0, TILES)
                    dve.wait_ge(att_x_done, 4)
                    ln_stats(LN_FFN2 + 1, CT, TILES)
                if has(a, 1):
                    stack_lo(a + 1)
                    norm_parts(a + 1)
                if has(a, -2):
                    add_projection(a - 2)
                if has(a, 2):
                    ln_apply(a + (2 + LN_ATT), (a + 2) * BT, 2)
                if has(a, 3):
                    att_stats(a + 3)
                elif a == ROWS - 3:
                    dve.wait_ge(att_x_done, 2)
                    ln_stats(LN_FFN2, 0, TILES)
                if has(a, 1):
                    stack_copy(a + 1, 3)

            dve.wait_ge(x_loaded, 16)
            ln_stats(0, 0, TILES)
            ln_apply(0, 0, TILES)
            dve.wait_ge(small_hi_ready, 1)
            tt(gk_lo[:, 0:EXPERTS], gk_raw[:], gk_hi[:, 0:EXPERTS].bitcast(F32), ALU.subtract).then_inc(small_lo_ready, 1)
            x_lo_part(0, 0, FIRST_BANKS[0])
            weight_lo(0)
            dve.wait_ge(x_loaded, 32)
            ln_stats(1, CT, TILES)
            dve.wait_ge(const_step, ROUTE_CONSTS)
            dve.wait_ge(small_loaded, 16 * 2)
            route_scores(0, FIRST_BANKS[0])
            ln_apply(1, CT, TILES)
            route(0, 0, ROUTE_STEPS // 2)
            x_lo_part(1, 1, FIRST_BANKS[1])
            route(0, ROUTE_STEPS // 2, ROUTE_STEPS + 1)
            weight_lo(2)
            ffn(0, 0)

            stack_copy(0, 3)
            dve.wait_ge(ffn_x_done, CHUNKS)
            attention(dve, row, ROWS - 3)
            row(ROWS - 2)
            row(ROWS - 1)
            x_lo_part(CHUNKS, 0, FIRST_BANKS[0])
            divide(ROWS - 2)
            kv_sums(ROWS - 1)
            kv_parts(ROWS - 1)
            add_projection(ROWS - 2)
            ln_apply(LN_FFN2 + 1, CT, TILES)
            route_scores(CHUNKS, FIRST_BANKS[0])
            route(CHUNKS, 0, ROUTE_STEPS // 3)
            x_lo_part(CHUNKS + 1, 1, FIRST_BANKS[1])
            route(CHUNKS, ROUTE_STEPS // 3, 2 * ROUTE_STEPS // 3)
            divide(ROWS - 1)
            route(CHUNKS, 2 * ROUTE_STEPS // 3, ROUTE_STEPS + 1)
            add_projection(ROWS - 1)
            ffn(CHUNKS, LN_FFN2)

        @block.tensor
        def _(pe):
            pe.sem_inc(down_done, D_CREDIT)
            pe.sem_inc(yt_ready, YT_CREDIT)
            pe.sem_inc(xt_ready, XT_CREDIT)
            pe.sem_inc(stack_t_ready, STACK_CREDIT)
            pe.sem_inc(kv_ready, KV_CREDIT)
            pe.sem_inc(kv_tr_ready, KV_TR_CREDIT)
            pe.sem_inc(o_ready, O_CREDIT)
            pe.sem_inc(proj_ready, PROJ_CREDIT)

            def three_passes(o, w_h, w_l, x_h, x_l, start=True, stop=True):
                nc.tensor.matmul(o, w_h, x_h, start=start, stop=False)
                nc.tensor.matmul(o, w_h, x_l, start=False, stop=False)
                return nc.tensor.matmul(o, w_l, x_h, start=False, stop=stop)

            def transpose_x(p, bank, n):
                pe.wait_ge(xn_ready, p + 1)
                for t in range(n):
                    last = nc.tensor.transpose(bank[:, t * P:(t + 1) * P], xn[:, t * H:(t + 1) * H], ident[:])
                last.then_inc(xt_ready, 1)

            def logits(f, c, bank=T1[:]):
                pe.wait_ge(xlo_ready, f + 1)
                cols = ds(c * CT, CT)
                three_passes(bank, gk_hi[:], gk_lo[:], x_hi[:, cols], x_lo[:, cols]).then_inc(logits_ready, 1)

            def scores_to_tokens(f, bank=T1[:]):
                pe.wait_ge(scores_ready, f + 1)
                for t in range(TILES):
                    last = nc.tensor.transpose(bank[:, t * P:(t + 1) * P], scores_t[:, t * P:(t + 1) * P], ident[:])
                last.then_inc(scores_tok_ready, 1)

            def transpose_combine(f):
                pe.wait_ge(combine_ready, f + 1)
                for t in range(TILES):
                    last = nc.tensor.transpose(T1[:, t * P:(t + 1) * P], combine_s[:, t, :].bitcast(F32), ident[:])
                last.then_inc(combine_tok_t, 1)

            def ffn(f0, ln0):
                def down(n, j):
                    pe.wait_ge(gated_lo_done, n + (1 + QL_CREDIT))
                    return three_passes(pY[:], w_block(w_hi, 2, j), w_block(w_lo, 2, j), gated_hi[:, j % 3],
                                        gated_lo[:, j % 3], start=(j == 0), stop=(j == BLOCKS - 1)
                                        ).then_inc(down_done, 1)

                def transpose_y(f, bank=T0):
                    pe.wait_ge(y_done, f + (1 + Y_CREDIT))
                    for t in range(TILES):
                        last = nc.tensor.transpose(bank[:, t * P:(t + 1) * P], y_sb[:, t * P:(t + 1) * P], ident[:])
                    last.then_inc(yt_ready, 1)

                def chunk(c, prev, nxt, nxt2):
                    f = c + f0
                    n0, m0 = f * BLOCKS, f * PAIRS
                    cols = ds(c * CT, CT)
                    first = isinstance(f, int) and f == 0
                    for j in range(BLOCKS):
                        if first and j == 0:
                            pe.wait_ge(w_lo_ready[0], 1)
                            pe.wait_ge(w_lo_ready[1], 1)
                        if not prev and j == 0:
                            pe.wait_ge(sfc_ready, f + 1)
                        if not prev and j == 1:
                            pe.wait_ge(scores_ready, f + 2)
                        if j < PAIRS:
                            gate, up = pG[:, j % 2], pU[:, j % 2]
                            if prev or j >= 2:
                                before = j - 2 if j >= 2 else j - 2 - (BLOCKS - PAIRS)
                                pe.wait_ge(silu_done, n0 + (before + 1 + SILU_CREDIT))
                        else:
                            gate, up = T0[:], pC[:]
                            if prev:
                                pe.wait_ge(ffn_x_done, f)
                        three_passes(gate, w_block(w_hi, 0, j), w_block(w_lo, 0, j), x_hi[:, cols],
                                     x_lo[:, cols]).then_inc(g_ready, 1)
                        if prev and j == 0:
                            if nxt:
                                pe.wait_ge(scores_ready, f + 2)
                            transpose_combine(f)
                        if j == PAIRS:
                            pe.wait_ge(s_used, m0 + (j + S_CREDIT))
                        elif prev or j >= 2:
                            pe.wait_ge(gated_done, n0 + (before + 1 + Q_CREDIT))
                        three_passes(up, w_block(w_hi, 1, j), w_block(w_lo, 1, j), x_hi[:, cols],
                                     x_lo[:, cols]).then_inc(u_ready, 1)
                        if j == 0 and not prev:
                            if f0 > 0:
                                transpose_on(ROWS - 1)
                                projection(ROWS - 1)
                            transpose_combine(f)
                        if prev and j == 0:
                            down(n0 - 3, BLOCKS - 3)
                        if j < PAIRS:
                            if j == 0:
                                pe.wait_ge(combine_t_ready, f + 1)
                                if prev:
                                    pe.wait_ge(gated_done, n0 + Q_CREDIT)
                            pe.wait_ge(s_used, m0 + (j + S_CREDIT))
                            nc.tensor.matmul(pC[:], sel_r[:, j * P:(j + 1) * P], combine_t[:, cols], start=True,
                                             stop=True).then_inc(c_ready, 1)
                        if first and j == 3:
                            pe.wait_ge(w_lo_ready[2], 1)
                        if j == 3:
                            if not prev and f0 > 0:
                                pe.wait_ge(att_x_added, ROWS)
                            pe.wait_ge(y_done, f + Y_CREDIT)
                        if j >= 3:
                            down(n0 + (j - 3), j - 3)
                        elif prev and j > 0:
                            down(n0 + (j - 3), j + BLOCKS - 3)
                        if j == 0 and nxt:
                            scores_to_tokens(f + 1)
                        if before_attention(c, f0):
                            if j == 2:
                                pe.wait_ge(sfc_ready, CHUNKS)
                                transpose_x(LN_ATT, T1, 2)
                            if j == 3:
                                pe.wait_ge(small_loaded, 16 * 5)
                                qkv_product(0)
                            if j == 4:
                                pe.wait_ge(qkv_copied, 1)
                            if j == 5:
                                pe.wait_ge(qkv_copied, 2)
                                transpose_x(LN_ATT + 1, T1, 2)
                        if j == 4 and prev:
                            transpose_y(f - 1)
                        if j == 5 and nxt2:
                            pe.wait_ge(sfc_ready, f + 2)
                            transpose_x(c + (2 + ln0), T1, TILES)
                        if j == 6 and nxt2:
                            logits(f + 2, c + 2)

                chunk(0, False, True, True)
                with pe.Fori(1, CHUNKS - 2) as c:
                    chunk(c, True, True, True)
                chunk(CHUNKS - 2, True, True, False)
                chunk(CHUNKS - 1, True, False, False)
                for j in range(BLOCKS - 3, BLOCKS):
                    down((f0 + CHUNKS - 1) * BLOCKS + j, j)
                pe.wait_ge(silu_done, (f0 + CHUNKS) * BLOCKS + SILU_CREDIT)
                if f0 == 0:
                    pe.wait_ge(xta_ready, 2)
                    transpose_k_stack(0)
                    transpose_y(CHUNKS - 1, T2)
                    transpose_q_stack(0)
                    qkv_product(1)
                else:
                    transpose_y(f0 + CHUNKS - 1)

            def qkv_product(a):
                pe.wait_ge(xta_ready, a + 1)
                for t, bank in enumerate((T0, T1)):
                    if not isinstance(a, int) or a > 0:
                        pe.wait_ge((qk_even_ready, qk_odd_ready)[t], 2 * a)
                    nc.tensor.matmul(bank[:, 0:3 * H], x_t[:, t * P:(t + 1) * P], wqkv_sb[:], start=True,
                                     stop=True).then_inc(qkv_ready, 1)

            def transpose_stack(a, s, bank):
                for i in range(2):
                    for t in range(2):
                        last = nc.tensor.transpose(bank[0:STACK, i * BT + t * P:i * BT + (t + 1) * P],
                                                   stack[:, 2 * QG * t + 2 * s + i, :].bitcast(F32), ident[:])
                last.then_inc(stack_t_ready, 1)

            def transpose_k_stack(a):
                pe.wait_ge(stack_ready, 2 * a + 2)
                pe.wait_ge(stack_dup_ready, a + 1)
                pe.wait_ge(norm_split, 2 * a + 2)
                transpose_stack(a, 2, T0)
                transpose_stack(a, 3, T1)

            def transpose_q_stack(a):
                pe.wait_ge(qk_even_ready, 2 * a + 1)
                transpose_stack(a, 0, T0)
                pe.wait_ge(qk_odd_ready, 2 * a + 1)
                transpose_stack(a, 1, T1)

            def k_unit(a, u):
                t, half = u // 2, u % 2
                pe.wait_ge(exp_done, 8 * a + (u + 1 - 2 + EXP_CREDIT))
                for i in range(2):
                    last = nc.tensor.matmul(pG[:, u % 2, i * BT:(i + 1) * BT],
                                            qk_r[:, QG + 2 * half + i, t * P:(t + 1) * P], rf_r[:],
                                            start=True, stop=True)
                last.then_inc(feat_ready, 1)

            def q_unit(a, u):
                pe.wait_ge(exp_done, 8 * a + (4 + u + 1 - 2 + EXP_CREDIT))
                for i in range(2):
                    last = nc.tensor.matmul(pG[:, u % 2, i * BT:(i + 1) * BT], rf_r[:, i * P:(i + 1) * P],
                                            qk_r[:, u, :], start=True, stop=True)
                last.then_inc(feat_ready, 1)

            def kv_product(a, half):
                if half == 0:
                    pe.wait_ge(v_ready, a + 1)
                    pe.wait_ge(k_lo_done, 4 * a + (4 + K_CREDIT))
                    pe.wait_ge(kv_copied, a + KV_COPY_CREDIT)
                for g in (2 * half, 2 * half + 1):
                    o = pU[:, g // 2, (g % 2) * BT:(g % 2 + 1) * BT]
                    for n, (t, k) in enumerate([(0, k_hi), (0, k_lo), (1, k_hi), (1, k_lo)]):
                        col = t * HEADS * NF + g * BT
                        last = nc.tensor.matmul(o, v_r[:, t, g, :], k[:, col:col + BT], start=(n == 0), stop=(n == 3))
                if half == 1:
                    last.then_inc(kv_ready, 1)

            def transpose_kv(a, now):
                pe.wait_ge(kv_copied, a + (1 + KV_COPY_CREDIT))
                for jh, bank in enumerate((T0, T1)):
                    if has(now, 1):
                        pe.wait_ge(qkv_copied, 2 * now + (3 + jh))
                    elif has(now, 0):
                        pe.wait_ge((qk_even_ready, qk_odd_ready)[jh], 2 * now + 2)
                    else:
                        pe.wait_ge(kv_tr_read, 2 * now - 2)
                    for k in range(4):
                        j = 4 * jh + k
                        last = nc.tensor.transpose(bank[:, k * P:(k + 1) * P], kv_t[:, j * P:(j + 1) * P], ident[:])
                    last.then_inc(kv_tr_ready, 1)

            def o_product(a, jh):
                if jh == 0:
                    pe.wait_ge(kv_split, a + 1)
                    pe.wait_ge(o_copied, a + O_COPY_CREDIT)
                    pe.wait_ge(q_lo_done, 4 * a + (2 + QF_CREDIT))
                else:
                    pe.wait_ge(q_lo_done, 4 * a + (4 + QF_CREDIT))
                for k in range(4):
                    q = slice((4 * jh + k) * BT, (4 * jh + k + 1) * BT)
                    w = slice(k * P, (k + 1) * P)
                    last = three_passes(pC[:, jh * BT:(jh + 1) * BT], kv_hi[:, jh, w], kv_lo[:, jh, w], q_hi[:, q],
                                        q_lo[:, q], start=(k == 0), stop=(k == 3))
                last.then_inc(o_ready, 1)

            def transpose_o(a):
                pe.wait_ge(o_copied, a + (1 + O_COPY_CREDIT))
                for t in range(2):
                    for jh in range(2):
                        c = (2 * t + jh) * P
                        last = nc.tensor.transpose(T2[:, c:c + P], o_sb[:, jh * BT + t * P:jh * BT + (t + 1) * P],
                                                   ident[:])
                last.then_inc(o_tr_ready, 1)

            def transpose_on(a):
                pe.wait_ge(on_ready, a + 1)
                for t in range(2):
                    last = nc.tensor.transpose(T2[:, t * P:(t + 1) * P], on[:, t * P:(t + 1) * P], ident[:])
                last.then_inc(on_tr_ready, 1)

            def projection(a):
                pe.wait_ge(on_copied, a + 1)
                for t in range(2):
                    last = nc.tensor.matmul(T2[:, t * P:(t + 1) * P], on_t[:, t * P:(t + 1) * P], wout_sb[:],
                                            start=True, stop=True)
                last.then_inc(proj_ready, 1)

            def row(a):
                if has(a, 0):
                    pe.wait_ge(qk_even_ready, 2 * a + 1)
                    pe.wait_ge(qk_odd_ready, 2 * a + 1)
                    k_unit(a, 0)
                    k_unit(a, 1)
                if has(a, -1):
                    transpose_kv(a - 1, a)
                if has(a, 0):
                    k_unit(a, 2)
                if has(a, -2):
                    transpose_on(a - 2)
                if has(a, 0):
                    k_unit(a, 3)
                    pe.wait_ge(qk_even_ready, 2 * a + 2)
                    pe.wait_ge(qk_odd_ready, 2 * a + 2)
                    q_unit(a, 0)
                    q_unit(a, 1)
                if has(a, -1):
                    o_product(a - 1, 0)
                if has(a, -2):
                    projection(a - 2)
                if has(a, -1):
                    o_product(a - 1, 1)
                if has(a, 0):
                    q_unit(a, 2)
                    kv_product(a, 0)
                if has(a, 1):
                    if has(a, -1):
                        pe.wait_ge(kv_tr_read, 2 * a)
                    else:
                        pe.wait_ge(qkv_copied, 2 * a + 4)
                    transpose_k_stack(a + 1)
                if has(a, 0):
                    q_unit(a, 3)
                if has(a, 2):
                    if has(a, -2):
                        pe.wait_ge(att_x_added, a - 1)
                    elif has(a, 1):
                        pe.wait_ge(xta_ready, a + 2)
                    transpose_x(a + (2 + LN_ATT), T2, 2)
                if has(a, 0):
                    kv_product(a, 1)
                if has(a, 1):
                    transpose_q_stack(a + 1)
                if has(a, -1):
                    if has(a, 2):
                        pe.wait_ge(xta_ready, a + 3)
                    elif has(a, -2):
                        pe.wait_ge(att_x_added, a - 1)
                    transpose_o(a - 1)
                if has(a, 2):
                    qkv_product(a + 2)

            pe.wait_ge(const_step, GK_CONSTS)
            transpose_x(0, FIRST_BANKS[0], TILES)
            pe.wait_ge(small_lo_ready, 1)
            logits(0, 0, FIRST_BANKS[0])
            scores_to_tokens(0, FIRST_BANKS[0])
            transpose_x(1, FIRST_BANKS[1], TILES)
            logits(1, 1, FIRST_BANKS[1])
            ffn(0, 0)

            pe.wait_ge(silu_done, CHUNKS * BLOCKS + SILU_CREDIT)
            pe.wait_ge(gated_done, CHUNKS * BLOCKS + Q_CREDIT)
            pe.wait_ge(sfc_ready, CHUNKS)
            pe.wait_ge(ffn_x_done, CHUNKS)
            pe.wait_ge(y_done, CHUNKS + Y_CREDIT)
            pe.wait_ge(rf_ready, 2)
            attention(pe, row)

            row(ROWS - 2)
            row(ROWS - 1)
            pe.wait_ge(exp_done, 8 * ROWS + EXP_CREDIT)
            transpose_x(LN_FFN2, FIRST_BANKS[0], TILES)
            transpose_kv(ROWS - 1, ROWS)
            transpose_on(ROWS - 2)
            logits(CHUNKS, 0, FIRST_BANKS[0])
            projection(ROWS - 2)
            scores_to_tokens(CHUNKS, FIRST_BANKS[0])
            o_product(ROWS - 1, 0)
            transpose_x(LN_FFN2 + 1, FIRST_BANKS[1], TILES)
            o_product(ROWS - 1, 1)
            pe.wait_ge(att_x_added, ROWS - 1)
            transpose_o(ROWS - 1)
            logits(CHUNKS + 1, 1, FIRST_BANKS[1])
            ffn(CHUNKS, LN_FFN2)


def kernel(**inputs):
    import numpy as np
    import concourse.bacc as bacc
    from concourse.bass_utils import run_bass_kernel_spmd

    i = {name: np.asarray(a) for name, a in inputs.items()}
    shape = i["L0_attn_x"].shape

    def up(name, shared):
        w = i[name].transpose(1, 0, 2).reshape(H, EXPERTS * M)
        return np.concatenate([w, i[shared]], axis=1)

    down = i["L0_ffn_w_down"].reshape(PAIRS, P, H).transpose(1, 0, 2).reshape(P, PAIRS * H)
    down = np.concatenate([down, i["L0_ffn_sw_down"]], axis=1)
    wall = np.concatenate([up("L0_ffn_w_gate", "L0_ffn_sw_gate"), up("L0_ffn_w_up", "L0_ffn_sw_up"), down], axis=1)

    pair_sel = np.zeros((P, PAIRS * P), np.float32)
    for e in range(EXPERTS):
        pair_sel[[e, EXPERTS + e], e * M:(e + 1) * M] = 1.0
    norm_sel = np.zeros((2 * HG, HG * NF), np.float32)
    for h in range(HG):
        norm_sel[[h, HG + h], h * NF:(h + 1) * NF] = -float(NF) ** 0.5

    arrays = {
        "x": i["L0_attn_x"].reshape(TOKENS, H),
        "wall": wall,
        "gate_k": i["L0_ffn_gate_kernel"],
        "gate_b": i["L0_ffn_gate_bias"],
        "wqkv": i["L0_attn_w_qkv"].T,
        "wout": i["L0_attn_w_out"].T,
        "b_out": i["L0_attn_b_out"],
        "rft": i["L0_attn_random_features"].T,
        "pair_sel": pair_sel,
        "norm_sel": norm_sel,
    }
    arrays = {name + "_dram": np.ascontiguousarray(a) for name, a in arrays.items()}
    nc = bacc.Bacc("TRN2", target_bir_lowering=False, num_devices=1)
    args = [nc.dram_tensor(name, a.shape, mybir.dt.from_np(a.dtype), kind="ExternalInput").ap()
            for name, a in arrays.items()]
    args.append(nc.dram_tensor("out_dram", (TOKENS, H), F32, kind="ExternalOutput").ap())
    macaron_kernel(nc, *args)
    r = run_bass_kernel_spmd(nc, [arrays], core_ids=[0])
    return r.results[0]["out_dram"].reshape(shape)
```
